# Optimizing a Trainium2 kernel written in Bass

```python
import numpy as np
import jax
import jax.numpy as jnp

def _softmax(x, axis=-1):
    return jax.nn.softmax(x, axis=axis)

def _gelu(x):
    return jax.nn.gelu(x, approximate=True)

def _silu(x):
    return jax.nn.silu(x)

def _sigmoid(x):
    return jax.nn.sigmoid(x)

def _layernorm(x, axis=-1, eps=1e-05):
    m = jnp.mean(x, axis=axis, keepdims=True)
    v = jnp.var(x, axis=axis, keepdims=True)
    return (x - m) / jnp.sqrt(v + eps)

def _scatter_add(tgt, idx, src, axis=0):
    return tgt.at[idx].add(src)

def _segment_sum(src, seg, n):
    return jax.ops.segment_sum(src, seg, n)
kernel_name = 'mk_seq_postln_d1_jaxref_r8_97627a'

def setup_inputs(seed: int=0):
    np.random.seed(seed)
    _w = jnp.asarray

    def _L0_attn_setup():
        import jax, jax.numpy as jnp
        import numpy as np
        import math
        D = 256
        H = 16
        KV = 4
        DH = D // H
        REP = H // KV
        LAMBDA_INIT = 0.8 - 0.6 * math.exp(-0.3 * 0)
        ROPE_BASE = 10000.0
        EPS = 1e-05

        def _rope(x, cos, sin):
            x1, x2 = (x[..., ::2], x[..., 1::2])
            c = cos[None, None]
            s = sin[None, None]
            o1 = x1 * c - x2 * s
            o2 = x1 * s + x2 * c
            return jnp.stack([o1, o2], axis=-1).reshape(x.shape)

        def _forward(x, Wq, Wk, Wv, Wo, lambda_q1, lambda_k1, lambda_q2, lambda_k2, gn_w, gn_b):
            B, T, _ = x.shape
            q = (x @ Wq).reshape(B, T, H, 2 * DH).transpose(0, 2, 1, 3)
            k = (x @ Wk).reshape(B, T, KV, 2 * DH).transpose(0, 2, 1, 3)
            v = (x @ Wv).reshape(B, T, KV, 2 * DH).transpose(0, 2, 1, 3)
            q1, q2 = (q[..., :DH], q[..., DH:])
            k1, k2 = (k[..., :DH], k[..., DH:])
            inv = 1.0 / ROPE_BASE ** (jnp.arange(0, DH, 2, dtype=jnp.float32) / DH)
            freqs = jnp.arange(T, dtype=jnp.float32)[:, None] * inv[None, :]
            cos, sin = (jnp.cos(freqs), jnp.sin(freqs))
            q1, q2 = (_rope(q1, cos, sin), _rope(q2, cos, sin))
            k1, k2 = (_rope(k1, cos, sin), _rope(k2, cos, sin))
            k1 = jnp.repeat(k1, REP, axis=1)
            k2 = jnp.repeat(k2, REP, axis=1)
            v = jnp.repeat(v, REP, axis=1)
            mask = jnp.triu(jnp.full((T, T), -jnp.inf, dtype=x.dtype), k=1)[None, None]
            scale = 1.0 / math.sqrt(DH)
            s1 = jnp.einsum('bhtd,bhsd->bhts', q1, k1) * scale + mask
            s2 = jnp.einsum('bhtd,bhsd->bhts', q2, k2) * scale + mask
            a1 = jax.nn.softmax(s1, axis=-1)
            a2 = jax.nn.softmax(s2, axis=-1)
            lam = jnp.exp(jnp.sum(lambda_q1 * lambda_k1)) - jnp.exp(jnp.sum(lambda_q2 * lambda_k2)) + LAMBDA_INIT
            diff = a1 - lam * a2
            out = jnp.einsum('bhts,bhsd->bhtd', diff, v)
            out = out.transpose(0, 2, 1, 3)
            mean = jnp.mean(out, axis=(1, 3), keepdims=True)
            var = jnp.var(out, axis=(1, 3), keepdims=True)
            out = (out - mean) * jax.lax.rsqrt(var + EPS)
            out = out * gn_w.reshape(1, 1, H, 2 * DH) + gn_b.reshape(1, 1, H, 2 * DH)
            out = out.reshape(B, T, 2 * H * DH) * (1.0 - LAMBDA_INIT)
            return out @ Wo
        key = jax.random.key(seed)
        ks = jax.random.split(key, 12)
        B, T = (1, 256)
        s = 0.02
        return {'x': jax.random.normal(ks[0], (B, T, D), jnp.float32), 'Wq': jax.random.normal(ks[1], (D, 2 * H * DH), jnp.float32) * s, 'Wk': jax.random.normal(ks[2], (D, 2 * KV * DH), jnp.float32) * s, 'Wv': jax.random.normal(ks[3], (D, 2 * KV * DH), jnp.float32) * s, 'Wo': jax.random.normal(ks[4], (2 * H * DH, D), jnp.float32) * s, 'lambda_q1': jax.random.normal(ks[5], (DH,), jnp.float32) * 0.1, 'lambda_k1': jax.random.normal(ks[6], (DH,), jnp.float32) * 0.1, 'lambda_q2': jax.random.normal(ks[7], (DH,), jnp.float32) * 0.1, 'lambda_k2': jax.random.normal(ks[8], (DH,), jnp.float32) * 0.1, 'gn_w': jnp.ones((2 * H * DH,), jnp.float32), 'gn_b': jnp.zeros((2 * H * DH,), jnp.float32)}
    _L0_attn_in = _L0_attn_setup()

    def _L0_ffn_setup():
        import jax, jax.numpy as jnp
        import numpy as np
        B, S, D, F, E, K = (2, 256, 256, 512, 8, 1)

        def _silu_mul(gu):
            g, u = jnp.split(gu, 2, axis=-1)
            return jax.nn.silu(g) * u

        def _moe_forward(hidden_states, router_w, w_gate_up, w_down, shared_gate_up, shared_down, top_k=K):
            b, s, d = hidden_states.shape
            x = hidden_states.reshape(-1, d)
            router_logits = x @ router_w.T
            topk_vals, topk_ids = jax.lax.top_k(router_logits, top_k)
            gate = jax.nn.sigmoid(topk_vals.astype(jnp.float32)).astype(x.dtype)
            xs = (x[:, None, :] * gate[:, :, None]).reshape(-1, d)
            ids_flat = topk_ids.reshape(-1)
            n_experts = w_gate_up.shape[0]

            def body(acc, inp):
                wg, wd, e = inp
                h = _silu_mul(xs @ wg)
                o = h @ wd
                mask = (ids_flat == e)[:, None]
                return (acc + jnp.where(mask, o, jnp.zeros((), o.dtype)), None)
            acc0 = jnp.zeros_like(xs)
            routed, _ = jax.lax.scan(body, acc0, (w_gate_up, w_down, jnp.arange(n_experts)))
            routed = routed.reshape(-1, top_k, d).sum(1)
            shared = _silu_mul(x @ shared_gate_up) @ shared_down
            return (routed + shared).reshape(b, s, d)
        key = jax.random.key(seed)
        ks = jax.random.split(key, 6)
        scale = 0.02
        return {'hidden_states': jax.random.normal(ks[0], (B, S, D), jnp.float32), 'router_w': jax.random.normal(ks[1], (E, D), jnp.float32) * scale, 'w_gate_up': jax.random.normal(ks[2], (E, D, 2 * F), jnp.float32) * scale, 'w_down': jax.random.normal(ks[3], (E, F, D), jnp.float32) * scale, 'shared_gate_up': jax.random.normal(ks[4], (D, 2 * F), jnp.float32) * scale, 'shared_down': jax.random.normal(ks[5], (F, D), jnp.float32) * scale}
    _L0_ffn_in = _L0_ffn_setup()
    _d = {'L0_attn_x': _L0_attn_in['x'], 'L0_attn_Wq': _L0_attn_in['Wq'], 'L0_attn_Wk': _L0_attn_in['Wk'], 'L0_attn_Wv': _L0_attn_in['Wv'], 'L0_attn_Wo': _L0_attn_in['Wo'], 'L0_attn_lambda_q1': _L0_attn_in['lambda_q1'], 'L0_attn_lambda_k1': _L0_attn_in['lambda_k1'], 'L0_attn_lambda_q2': _L0_attn_in['lambda_q2'], 'L0_attn_lambda_k2': _L0_attn_in['lambda_k2'], 'L0_attn_gn_w': _L0_attn_in['gn_w'], 'L0_attn_gn_b': _L0_attn_in['gn_b'], 'L0_ffn_router_w': _L0_ffn_in['router_w'], 'L0_ffn_w_gate_up': _L0_ffn_in['w_gate_up'], 'L0_ffn_w_down': _L0_ffn_in['w_down'], 'L0_ffn_shared_gate_up': _L0_ffn_in['shared_gate_up'], 'L0_ffn_shared_down': _L0_ffn_in['shared_down']}
    _x0 = _d['L0_attn_x']
    _d['L0_attn_x'] = jax.random.normal(jax.random.fold_in(jax.random.key(seed), 1), (4, 512, 256), dtype=_x0.dtype)
    del _x0
    return _d

def reference(L0_attn_x, L0_attn_Wq, L0_attn_Wk, L0_attn_Wv, L0_attn_Wo, L0_attn_lambda_q1, L0_attn_lambda_k1, L0_attn_lambda_q2, L0_attn_lambda_k2, L0_attn_gn_w, L0_attn_gn_b, L0_ffn_router_w, L0_ffn_w_gate_up, L0_ffn_w_down, L0_ffn_shared_gate_up, L0_ffn_shared_down):

    def _L0_attn_ref(x, Wq, Wk, Wv, Wo, lambda_q1, lambda_k1, lambda_q2, lambda_k2, gn_w, gn_b):
        import jax, jax.numpy as jnp
        import numpy as np
        import math
        D = 256
        H = 16
        KV = 4
        DH = D // H
        REP = H // KV
        LAMBDA_INIT = 0.8 - 0.6 * math.exp(-0.3 * 0)
        ROPE_BASE = 10000.0
        EPS = 1e-05

        def _rope(x, cos, sin):
            x1, x2 = (x[..., ::2], x[..., 1::2])
            c = cos[None, None]
            s = sin[None, None]
            o1 = x1 * c - x2 * s
            o2 = x1 * s + x2 * c
            return jnp.stack([o1, o2], axis=-1).reshape(x.shape)

        def _forward(x, Wq, Wk, Wv, Wo, lambda_q1, lambda_k1, lambda_q2, lambda_k2, gn_w, gn_b):
            B, T, _ = x.shape
            q = (x @ Wq).reshape(B, T, H, 2 * DH).transpose(0, 2, 1, 3)
            k = (x @ Wk).reshape(B, T, KV, 2 * DH).transpose(0, 2, 1, 3)
            v = (x @ Wv).reshape(B, T, KV, 2 * DH).transpose(0, 2, 1, 3)
            q1, q2 = (q[..., :DH], q[..., DH:])
            k1, k2 = (k[..., :DH], k[..., DH:])
            inv = 1.0 / ROPE_BASE ** (jnp.arange(0, DH, 2, dtype=jnp.float32) / DH)
            freqs = jnp.arange(T, dtype=jnp.float32)[:, None] * inv[None, :]
            cos, sin = (jnp.cos(freqs), jnp.sin(freqs))
            q1, q2 = (_rope(q1, cos, sin), _rope(q2, cos, sin))
            k1, k2 = (_rope(k1, cos, sin), _rope(k2, cos, sin))
            k1 = jnp.repeat(k1, REP, axis=1)
            k2 = jnp.repeat(k2, REP, axis=1)
            v = jnp.repeat(v, REP, axis=1)
            mask = jnp.triu(jnp.full((T, T), -jnp.inf, dtype=x.dtype), k=1)[None, None]
            scale = 1.0 / math.sqrt(DH)
            s1 = jnp.einsum('bhtd,bhsd->bhts', q1, k1) * scale + mask
            s2 = jnp.einsum('bhtd,bhsd->bhts', q2, k2) * scale + mask
            a1 = jax.nn.softmax(s1, axis=-1)
            a2 = jax.nn.softmax(s2, axis=-1)
            lam = jnp.exp(jnp.sum(lambda_q1 * lambda_k1)) - jnp.exp(jnp.sum(lambda_q2 * lambda_k2)) + LAMBDA_INIT
            diff = a1 - lam * a2
            out = jnp.einsum('bhts,bhsd->bhtd', diff, v)
            out = out.transpose(0, 2, 1, 3)
            mean = jnp.mean(out, axis=(1, 3), keepdims=True)
            var = jnp.var(out, axis=(1, 3), keepdims=True)
            out = (out - mean) * jax.lax.rsqrt(var + EPS)
            out = out * gn_w.reshape(1, 1, H, 2 * DH) + gn_b.reshape(1, 1, H, 2 * DH)
            out = out.reshape(B, T, 2 * H * DH) * (1.0 - LAMBDA_INIT)
            return out @ Wo
        return _forward(x, Wq, Wk, Wv, Wo, lambda_q1, lambda_k1, lambda_q2, lambda_k2, gn_w, gn_b)

    def _L0_ffn_ref(hidden_states, router_w, w_gate_up, w_down, shared_gate_up, shared_down):
        import jax, jax.numpy as jnp
        import numpy as np
        B, S, D, F, E, K = (2, 256, 256, 512, 8, 1)

        def _silu_mul(gu):
            g, u = jnp.split(gu, 2, axis=-1)
            return jax.nn.silu(g) * u

        def _moe_forward(hidden_states, router_w, w_gate_up, w_down, shared_gate_up, shared_down, top_k=K):
            b, s, d = hidden_states.shape
            x = hidden_states.reshape(-1, d)
            router_logits = x @ router_w.T
            topk_vals, topk_ids = jax.lax.top_k(router_logits, top_k)
            gate = jax.nn.sigmoid(topk_vals.astype(jnp.float32)).astype(x.dtype)
            xs = (x[:, None, :] * gate[:, :, None]).reshape(-1, d)
            ids_flat = topk_ids.reshape(-1)
            n_experts = w_gate_up.shape[0]

            def body(acc, inp):
                wg, wd, e = inp
                h = _silu_mul(xs @ wg)
                o = h @ wd
                mask = (ids_flat == e)[:, None]
                return (acc + jnp.where(mask, o, jnp.zeros((), o.dtype)), None)
            acc0 = jnp.zeros_like(xs)
            routed, _ = jax.lax.scan(body, acc0, (w_gate_up, w_down, jnp.arange(n_experts)))
            routed = routed.reshape(-1, top_k, d).sum(1)
            shared = _silu_mul(x @ shared_gate_up) @ shared_down
            return (routed + shared).reshape(b, s, d)
        return _moe_forward(hidden_states, router_w, w_gate_up, w_down, shared_gate_up, shared_down)
    x = L0_attn_x
    x = _layernorm(x + _L0_attn_ref(x, L0_attn_Wq, L0_attn_Wk, L0_attn_Wv, L0_attn_Wo, L0_attn_lambda_q1, L0_attn_lambda_k1, L0_attn_lambda_q2, L0_attn_lambda_k2, L0_attn_gn_w, L0_attn_gn_b), axis=-1)
    x = _layernorm(x + _L0_ffn_ref(x, L0_ffn_router_w, L0_ffn_w_gate_up, L0_ffn_w_down, L0_ffn_shared_gate_up, L0_ffn_shared_down), axis=-1)
    return x

_drawn_inputs = setup_inputs


def setup_inputs(seed=0):
    import zlib

    import numpy as np

    out = dict(_drawn_inputs(seed))
    spreads = {'L0_attn_gn_w': (1.0, 0.2), 'L0_attn_gn_b': (0.0, 0.1)}
    factors = {'L0_attn_lambda_q1': 8.0,
     'L0_attn_lambda_k1': 7.319,
     'L0_attn_lambda_q2': 8.0,
     'L0_attn_lambda_k2': 8.0,
     'L0_ffn_router_w': 6.667,
     'L0_ffn_w_gate_up': 6.181,
     'L0_ffn_w_down': 6.171,
     'L0_ffn_shared_gate_up': 8.0,
     'L0_ffn_shared_down': 8.0}
    for name, (base, spread) in spreads.items():
        noise = np.random.default_rng([zlib.crc32(name.encode()), seed]).standard_normal(out[name].shape)
        drawn = base * np.exp(spread * noise) if base else spread * noise
        out[name] = jnp.asarray(drawn.astype(out[name].dtype))
    for name, factor in factors.items():
        out[name] = (out[name] * factor).astype(out[name].dtype)
    return out
```

```python
from contextlib import ExitStack

import numpy as np

import concourse.bass as bass
from concourse import mybir

F32 = mybir.dt.float32
BF16 = mybir.dt.bfloat16
I32 = mybir.dt.int32
ALU = mybir.AluOpType
ACT = mybir.ActivationFunctionType
AX = mybir.AxisListType

P = 128
B, T, D = 4, 512, 256
H, KV, DH = 16, 4, 16
HS = 2 * H
DV = 2 * DH
QT = T // P
DC = D // P
SLOTS = 6
QPART = (0, 0, 0, 1, 1, 2)
KPART = (0, 1, 2, 0, 1, 0)
KROWS = SLOTS * DH
MROWS = KROWS + 2
LAMBDA_INIT = 0.2
EPS = 1e-5
NEG = -1e30
NP = 4
E, F = 8, 512
NTOK = B * QT
NROUTE = NTOK + E - 1
NTILE = NTOK + NROUTE
WUP = DC * 2 * F
WEXP = WUP + F // P * D


class Chain:

    def __init__(self, eng, sem):
        self.eng, self.sem, self.n, self.turns = eng, sem, 0, 0

    def link(self, ins):
        self.n += 1
        ins.then_inc(self.sem, 1)
        self.eng.wait_ge(self.sem, self.turns + self.n)

    def turn(self, head, per, done):
        assert self.n in (head, head + per), (self.n, head, per)
        self.n, self.turns = head, done * per


STEPS = [(qt, g, kt) for qt in range(QT) for g in range(KV) for kt in range(qt + 1)]
NSTEP = len(STEPS)
NUNIT = QT * KV
DIAG = [n for n, (qt, g, kt) in enumerate(STEPS) if kt == qt]


def banks(qt):
    per = max(1, QT // (qt + 1))
    return [list(range(i, i + per)) for i in range(0, HS, per)]


NBANK = [len(banks(qt)) for qt in range(QT)]
FIRST_ST = [min(n for n, s in enumerate(STEPS) if s[0] == qt) for qt in range(QT)]
LAST_ST = [max(n for n, s in enumerate(STEPS) if s[0] == qt) for qt in range(QT)]


def spread(count, lo, hi):
    at = {}
    for i in range(count):
        at.setdefault(lo + i * (hi - lo) // count, []).append(i)
    return at


BANKS_AT = {}
for _qt, (_lo, _hi) in {2: (0, 7), 3: (7, 19)}.items():
    for _n, _idx in spread(NBANK[_qt], _lo, _hi).items():
        BANKS_AT.setdefault(_n, []).extend((_qt, i) for i in _idx)

TASKS_AT = {n: [] for n in range(NSTEP)}
TASKS_AT[7].append(("mt", 2))
TASKS_AT[19].append(("mt", 3))
for _u in range(NUNIT - 1):
    _qt, _g = divmod(_u, KV)
    TASKS_AT[FIRST_ST[_qt] + (_g + 1) * (_qt + 1)].append(("norm", _u))
POST_AT = {0: [("square", 0)], 3: [("var", 0)]}
for _qt in range(QT):
    for _name, _n in (("affine", 19), ("turn", 21), ("project", 22), ("x2", 23), ("retake", 24), ("logits", 25)):
        POST_AT.setdefault(_n + 3 * _qt, []).append((_name, _qt))
BOUNDARY = [("norm", 15), ("v", 0), ("banks", (0, 0, 8)), ("mean", 0), ("mt", 0), ("banks", (1, 0, 16)), ("mt", 1)]
POST = [("square", 0), ("var", 0)] + [(name, qt) for qt in range(QT) for name in ("affine", "turn", "project", "x2", "retake", "logits")]
TAIL = [("norm", 15), ("mean", 0)] + POST
HEAD = [("v", 0), ("banks", (0, 0, 8)), ("mt", 0), ("banks", (1, 0, 16)), ("mt", 1)]
OLD = ("norm", "mean") + ("square", "var", "affine", "turn", "project", "x2", "retake", "logits")
MISC_TASKS = ("v", "mt", "norm", "mean", "var", "turn", "project", "retake", "logits")


def tasks_at(n, post):
    return [(t, 0) for t in TASKS_AT[n]] + [(t, 1) for t in (POST_AT.get(n, []) if post else [])]


BODY = [t for n in range(NSTEP) for t, _ in tasks_at(n, False)]
BODY_POST = [t for n in range(NSTEP) for t, _ in tasks_at(n, True)]


def misc_count(tasks):
    return sum(t[0] in MISC_TASKS for t in tasks)


MISC_HEAD, MISC_TURN = misc_count(HEAD + BODY), misc_count(BOUNDARY + BODY_POST)
BANK_HEAD, BANK_TURN = sum(NBANK), sum(NBANK)
ST_HEAD, ST_PREP = 4, 4
ST_TURN = ST_PREP + NSTEP
LINKS = {"norm": 4, "mean": 1}
POOL_TURN = 2 + QT
DVE_TURN = sum(LINKS.get(t[0], 0) for t in BOUNDARY + BODY_POST) + QT + QT * 2


def fill_of(tasks, task):
    return misc_count(tasks[:tasks.index(task) + 1])


def turned_maxima(b, qt):
    if isinstance(b, int) and b == 0:
        return fill_of(HEAD + BODY, ("mt", qt))
    return MISC_HEAD + (b - 1) * MISC_TURN + fill_of(BOUNDARY + BODY_POST, ("mt", qt))


PREP = [("cos", 0), ("sin", 0), ("even", 0), ("odd", 0), ("cos", 1), ("sin", 1), ("rest", 0), ("even", 1), ("odd", 1),
        ("cos", 2), ("low", 0), ("sin", 2), ("rest", 1), ("even", 2), ("odd", 2), ("low", 1), ("rest", 2), ("low", 2)]
PREP_AT = {k: i for i, k in enumerate(PREP)}
PREP_DONE = {k: i + 1 for i, k in enumerate(PREP)}
NPREP = len(PREP)


def build(nc, x, wqk, wv, wo, lams, gnw, gnb, cos_d, sin_d, ident_d, mask_d,
          router, w_up, w_down, s_up, s_down, counts_d, out):
    scratch = nc.dram_tensor("qk_parts", (B, 3, 3, QT, 2, P, P), BF16, kind="Internal").ap()
    mrows = nc.dram_tensor("max_rows", (B, QT, 2 * HS, P), BF16, kind="Internal").ap()

    x2_rows = nc.dram_tensor("x2_rows", (NTOK * P, D), F32, kind="Internal").ap()
    sorted_rows = nc.dram_tensor("sorted_rows", (NROUTE * P, D), F32, kind="Internal").ap()
    routed_rows = nc.dram_tensor("routed_rows", (NROUTE * P, D), F32, kind="Internal").ap()

    ctx = ExitStack()
    with ctx:
        def sb(name, shape, dt=F32):
            return ctx.enter_context(nc.sbuf_tensor(name, shape, dt))

        def sem(name):
            return ctx.enter_context(nc.semaphore(name))

        w_exp = sb("w_exp", [P, E * WEXP])
        work = sb("work", [P, 11264])

        class Place:

            def __init__(self, tensor):
                self.tensor, self.at = tensor, 0

            def take(self, columns, dt=F32):
                a = self.tensor[:, self.at:self.at + columns]
                self.at += columns
                return a if dt == F32 else a.bitcast(dt)

        early = Place(w_exp)
        raw = early.take(3 * 2 * T).rearrange("p (a h t) -> p a h t", a=3, h=2)
        rot = early.take(2 * 2 * T).rearrange("p (a h t) -> p a h t", a=2, h=2)
        parts = early.take(3 * 3 * T, BF16).rearrange("p (a s q h t) -> p a s q h t", a=3, s=3, q=QT, h=2)
        q_stack = early.take(QT * HS * P // 2, BF16).rearrange("p (q r t) -> p q r t", q=QT, r=HS)
        k_stack = early.take(QT * KV * P, BF16).rearrange("p (q r t) -> p q r t", q=QT, r=2 * KV)
        probs = early.take(NP * 2 * T).rearrange("p (n s t) -> p n s t", n=NP, s=2)
        assert early.at <= E * WEXP

        mine = Place(work)
        att = mine.take(QT * H * DV).rearrange("p (q h d) -> p q h d", q=QT, h=H)
        dev = mine.take(QT * H * DV).rearrange("p (q h d) -> p q h d", q=QT, h=H)
        sq = mine.take(QT * H * DV).rearrange("p (q h d) -> p q h d", q=QT, h=H)
        vo = mine.take(QT * KV * 2 * DV).rearrange("p (t g d) -> p t g d", t=QT, g=KV)
        xin = mine.take(QT * D).rearrange("p (n d) -> p n d", n=QT)
        xT = mine.take(DC * T).rearrange("p (c t) -> p c t", c=DC)
        ol = mine.take(2 * T).rearrange("p (u t) -> p u t", u=2)
        z = mine.take(2 * T).rearrange("p (u t) -> p u t", u=2)

        tables = sb("tables", [P, 3584])
        mine = Place(tables)
        cos = mine.take(T)
        sin = mine.take(T)
        wqk_sb = mine.take(DC * 3 * 2 * P).rearrange("p (c a h m) -> p c a h m", c=DC, a=3, h=2)
        wo_sb = mine.take(4 * D).rearrange("p (c n) -> p c n", c=4)

        theirs = Place(tables)
        xe = theirs.take(2 * D).rearrange("p (u d) -> p u d", u=2)
        xeT = theirs.take(2 * D).rearrange("p (u c t) -> p u c t", u=2, c=DC)
        yo = theirs.take(2 * D).rearrange("p (u d) -> p u d", u=2)
        is_top = theirs.take(NTOK * E).rearrange("p (n e) -> p n e", e=E)
        choice = theirs.take(NTOK * E).rearrange("p (n e) -> p n e", e=E)
        chosen = theirs.take(NTOK * E).rearrange("p (n e) -> p n e", e=E)
        scan = theirs.take(2 * NTOK * E).rearrange("p (u n e) -> p u n e", u=2, e=E)
        tiles_cmp = theirs.take(E * NTOK).rearrange("p (e n) -> p e n", e=E)
        place_f = theirs.take(NTOK * E).rearrange("p (n e) -> p n e", e=E)
        owner_cmp = theirs.take(NROUTE * E).rearrange("p (n e) -> p n e", e=E)

        theirs = Place(work)
        gated = theirs.take(NTOK * D).rearrange("p (n d) -> p n d", n=NTOK)
        total = theirs.take(NTOK * D).rearrange("p (n d) -> p n d", n=NTOK)
        silu = theirs.take(2 * F).rearrange("p (u f) -> p u f", u=2)
        hid = theirs.take(2 * F).rearrange("p (u f) -> p u f", u=2)
        hidT = theirs.take(2 * F).rearrange("p (u c t) -> p u c t", u=2, c=F // P)

        wv_sb = sb("wv_sb", [P, DC, P])
        w_sh = sb("w_sh", [P, WEXP])
        router_sb = sb("router_sb", [P, DC, E])
        gw = sb("gw", [P, 2 * H * DH])
        gb = sb("gb", [P, 2 * H * DH])
        ident = sb("ident", [P, P])
        identb = sb("identb", [P, P], BF16)
        mask_f = sb("mask_f", [P, P])
        mask = sb("mask", [P, P], BF16)
        before = sb("before", [P, P], BF16)
        onesb = sb("onesb", [P, P], BF16)
        zero_row = sb("zero_row", [P, D])
        lamv = sb("lamv", [P, 4, DH])
        lamp = sb("lamp", [P, 2, DH])
        lams2 = sb("lams2", [P, 2])
        lame = sb("lame", [P, 2])
        neglam = sb("neglam", [P, 1])
        mneg = sb("mneg", [P, QT, HS])
        msplit = sb("msplit", [P, 2, P], BF16)
        mT = sb("mT", [2 * HS, 2, P], BF16)
        rl = sb("rl", [P, 4, 2])
        o1 = sb("o1", [P, 4, DV])
        o2 = sb("o2", [P, 4, DV])
        head_sum = sb("head_sum", [P, QT, H])
        head_tot = sb("head_tot", [P, H])
        head_sq = sb("head_sq", [P, H])
        head_var = sb("head_var", [P, H])
        head_rstd = sb("head_rstd", [P, H])
        scale_row = sb("scale_row", [P, H, DV])
        averager = sb("averager", [P, P])
        st6 = sb("st6", [P, 6])
        mv = sb("mv", [P, 2, 2])
        rstd = sb("rstd", [P, 2])
        halfneg = sb("halfneg", [P, 1])
        zT = sb("zT", [P, 4, P])
        xres = sb("xres", [P, 2, D])
        y = sb("y", [P, 2, D])
        x2s = sb("x2s", [P, 2, D])
        x2T = sb("x2T", [P, DC, P])
        x2 = sb("x2", [P, NTOK, D])
        logits = sb("logits", [P, NTOK, E])
        counts = sb("counts", [P, E + NTOK + NROUTE])
        top = sb("top", [P, NTOK])
        gate = sb("gate", [P, 2, NTOK])
        first = sb("first", [P, NTOK])
        chosenb = sb("chosenb", [P, NTOK, E], BF16)
        tiles_n = sb("tiles_n", [P, E])
        tiles_cum = sb("tiles_cum", [P, 2, E])
        first_slot = sb("first_slot", [P, E])
        slot_f = sb("slot_f", [P, NTOK])
        slot = sb("slot", [P, NTOK], I32)
        owner_f = sb("owner_f", [P, NROUTE])
        owner = sb("owner", [P, NROUTE], I32)
        st6f = sb("st6f", [P, NTOK, 6])
        mvf = sb("mvf", [P, NTOK, 2])
        rstdf = sb("rstdf", [P, NTOK])

        s_ps = ctx.enter_context(nc.psum_tensor("s_ps", [P, 2, T], F32))
        st_ps = ctx.enter_context(nc.psum_tensor("st_ps", [P, 2, 2, T], F32))
        pv_ps = ctx.enter_context(nc.psum_tensor("pv_ps", [P, T], F32))
        misc = ctx.enter_context(nc.psum_tensor("misc", [P, T], F32))

        consts_loaded = sem("consts_loaded")
        consts_ready = sem("consts_ready")
        x_loaded = sem("x_loaded")
        xres_loaded = [sem(f"xres_loaded{i}") for i in range(2)]
        parts_written = sem("parts_written")
        q_loaded = [sem(f"q_loaded{i}") for i in range(QT)]
        k_loaded = sem("k_loaded")
        max_stored = sem("max_stored")
        max_loaded = [sem(f"max_loaded{i}") for i in range(QT)]
        st_full = sem("st_full")
        st_done = sem("st_done")
        bank_full = sem("bank_full")
        bank_done = sem("bank_done")
        misc_full = sem("misc_full")
        misc_done = sem("misc_done")
        pv_done = sem("pv_done")
        pv_step = sem("pv_step")
        diag_done = sem("diag_done")
        prep_done = sem("prep_done")
        high_done = sem("high_done")
        mid_done = sem("mid_done")
        split_done = sem("split_done")
        dve_chain = sem("dve_chain")
        pool_chain = sem("pool_chain")
        lam_summed = sem("lam_summed")
        lam_exp = sem("lam_exp")
        summed = sem("summed")
        centred = sem("centred")
        squared = sem("squared")
        stats_taken = sem("stats_taken")
        exps_taken = sem("exps_taken")
        squares_summed = sem("squares_summed")
        att_var = sem("att_var")
        scaled = sem("scaled")
        y_var = sem("y_var")
        y_rstd = sem("y_rstd")
        x2_done = sem("x2_done")
        x2_stored = [sem(f"x2_stored{i}") for i in range(2)]
        x2_kept = sem("x2_kept")
        stored = sem("stored")
        zeroed = sem("zeroed")
        zero_ready = sem("zero_ready")
        shared_loaded = sem("shared_loaded")
        experts_loaded = sem("experts_loaded")
        gate_exp = sem("gate_exp")
        top_found = sem("top_found")
        gated_done = sem("gated_done")
        chosen_done = sem("chosen_done")
        ranked = sem("ranked")
        slots_done = sem("slots_done")
        owners_done = sem("owners_done")
        scattered = sem("scattered")
        tile_loaded = [sem(f"tile_loaded{i}") for i in range(2)]
        turned = sem("turned")
        turned_done = sem("turned_done")
        up_full = sem("up_full")
        silu_done = sem("silu_done")
        hid_done = sem("hid_done")
        hid_turned = sem("hid_turned")
        hidT_done = sem("hidT_done")
        down_full = sem("down_full")
        down_done = sem("down_done")
        routed_stored = [sem(f"routed_stored{i}") for i in range(2)]
        gathered = [sem(f"gathered{i}") for i in range(4)]
        final_var = sem("final_var")
        final_rstd = sem("final_rstd")
        final_done = sem("final_done")

        block = ctx.enter_context(nc.Block())

        NCONST = 15

        def by_half(part):
            return part.rearrange("p q h t -> p h q t")

        def raw_q(pair):
            return raw[:, pair].rearrange("p h (q t) -> p h q t", q=QT)

        def st_at(b, k, prep):
            return ST_HEAD + b * ST_TURN + (ST_PREP if prep else 0) + k + 1

        def prep_slot(b, k):
            return k + 1 if b is None else ST_HEAD + b * ST_TURN + k + 1

        class Misc:

            def __init__(self):
                self.n, self.turns = 0, 0

            def next(self):
                self.n += 1
                return self.turns + self.n

            def turn(self, head, per, done):
                assert self.n in (head, head + per), (self.n, head, per)
                self.n, self.turns = head, done * per

        @block.sync
        def _(sp):
            def load_x(b):
                sp.dma_start(xin[:], x[b].rearrange("(n p) d -> p n d", p=P)).then_inc(x_loaded, 16)

            sp.dma_start(ident[:], ident_d).then_inc(consts_loaded, 16)
            load_x(0)
            sp.dma_start(wqk_sb[:], wqk.rearrange("(c p) a h m -> p c a h m", p=P)).then_inc(consts_loaded, 16)
            sp.dma_start(cos[:], cos_d).then_inc(consts_loaded, 16)
            sp.dma_start(sin[:], sin_d).then_inc(consts_loaded, 16)
            sp.dma_start(mask_f[:], mask_d).then_inc(consts_loaded, 16)
            sp.dma_start(wv_sb[:], wv.rearrange("(c p) m -> p c m", p=P)).then_inc(consts_loaded, 16)
            sp.dma_start(wo_sb[:], wo.rearrange("(c p) m -> p c m", p=P)).then_inc(consts_loaded, 16)
            for i, v in enumerate(lams):
                sp.dma_start(lamv[:, i, :], v.unsqueeze(0).to_broadcast([P, DH])).then_inc(consts_loaded, 16)
            sp.dma_start(gw[:], gnw.unsqueeze(0).to_broadcast([P, T])).then_inc(consts_loaded, 16)
            sp.dma_start(gb[:], gnb.unsqueeze(0).to_broadcast([P, T])).then_inc(consts_loaded, 16)

            sp.dma_start(router_sb[:], router.rearrange("(c p) e -> p c e", p=P)).then_inc(consts_loaded, 16)
            sp.dma_start(counts[:], counts_d.unsqueeze(0).to_broadcast([P, E + NTOK + NROUTE])).then_inc(consts_loaded, 16)
            sp.dma_start(w_sh[:, 0:WUP].rearrange("p (c n) -> p c n", c=DC), s_up.rearrange("(c p) n -> p c n", p=P)).then_inc(shared_loaded, 16)
            sp.dma_start(w_sh[:, WUP:WEXP].rearrange("p (c n) -> p c n", c=F // P), s_down.rearrange("(c p) n -> p c n", p=P)).then_inc(shared_loaded, 16)
            sp.wait_ge(zero_ready, 1)
            sp.dma_start(sorted_rows.rearrange("(n p) d -> p n d", p=P), zero_row[:].unsqueeze(1).to_broadcast([P, NROUTE, D])).then_inc(zeroed, 16)

            def load_q(b, qt, used):
                if used is not None:
                    sp.wait_ge(st_full, used)
                sp.wait_ge(parts_written, (b + 1) * 3 * 16)
                for s in range(SLOTS):
                    sp.dma_start(q_stack[s * DH:(s + 1) * DH, qt].rearrange("p (a r) t -> p a r t", a=2),
                                 scratch[b, 0:2, QPART[s], qt].rearrange("a h (j r) t -> (h j) a r t", j=8)
                                 ).then_inc(q_loaded[qt], 16)

            def load_k(b):
                sp.wait_ge(parts_written, (b + 1) * 3 * 16)
                for s in range(SLOTS):
                    sp.dma_start(k_stack[s * DH:(s + 1) * DH],
                                 scratch[b, 2, KPART[s]].rearrange("q h (j r) t -> (h j) q r t", j=8)[:, :, 0:2 * KV, :]
                                 ).then_inc(k_loaded, 16)

            def max_rows(b, qt):
                sp.wait_ge(misc_done, turned_maxima(b, qt))
                sp.dma_start(mrows[b, qt], mT[:, qt % 2, :]).then_inc(max_stored, 16)
                sp.wait_ge(max_stored, (b * QT + qt + 1) * 16)
                sp.dma_start(q_stack[KROWS:MROWS, qt, :, :],
                             mrows[b, qt].rearrange("(m r) t -> m r t", m=2)).then_inc(max_loaded[qt], 16)

            def load_residual(b, qt):
                sp.wait_ge(x2_done, b * QT + (qt - 1 if qt >= 2 else 0))
                sp.dma_start(xres[:, qt % 2, :], x[b, qt * P:(qt + 1) * P, :]).then_inc(xres_loaded[qt % 2], 16)

            def keep(b, qt):
                sp.wait_ge(x2_done, b * QT + qt + 1)
                sp.dma_start(x2_rows[bass.ds((b * QT + qt) * P, P), :], x2s[:, qt % 2]).then_inc(x2_stored[qt % 2], 16)

            def body(b, prep, post):
                if prep:
                    sp.wait_ge(st_full, b * ST_TURN + 1)
                    load_x(b + 1)
                max_rows(b, 2)
                if post:
                    load_residual(b - 1, 0)
                    load_residual(b - 1, 1)
                max_rows(b, 3)
                if prep:
                    load_q(b + 1, 0, st_at(b, LAST_ST[0], prep))
                    load_q(b + 1, 1, st_at(b, LAST_ST[1], prep))
                if post:
                    keep(b - 1, 0)
                    load_residual(b - 1, 2)
                if prep:
                    load_q(b + 1, 2, st_at(b, LAST_ST[2], prep))
                if post:
                    keep(b - 1, 1)
                    load_residual(b - 1, 3)
                    keep(b - 1, 2)
                    keep(b - 1, 3)

            def boundary(b):
                sp.wait_ge(st_full, st_at(b - 1, NSTEP - 1, True))
                load_k(b)
                load_q(b, 3, None)
                max_rows(b, 0)
                max_rows(b, 1)

            load_k(0)
            for qt in range(QT):
                load_q(0, qt, None)
            max_rows(0, 0)
            max_rows(0, 1)
            body(0, True, False)
            with sp.Fori(1, B - 1) as b:
                boundary(b)
                body(b, True, True)
            boundary(B - 1)
            body(B - 1, False, True)
            load_residual(B - 1, 0)
            load_residual(B - 1, 1)
            keep(B - 1, 0)
            load_residual(B - 1, 2)
            keep(B - 1, 1)
            load_residual(B - 1, 3)
            keep(B - 1, 2)
            keep(B - 1, 3)

            sp.wait_ge(pv_step, B * NSTEP)
            for e in range(E):
                w = w_exp[:, e * WEXP:(e + 1) * WEXP]
                sp.dma_start(w[:, 0:WUP].rearrange("p (c n) -> p c n", c=DC), w_up[e].rearrange("(c p) n -> p c n", p=P)).then_inc(experts_loaded, 16)
                sp.dma_start(w[:, WUP:WEXP].rearrange("p (c n) -> p c n", c=F // P), w_down[e].rearrange("(c p) n -> p c n", p=P)).then_inc(experts_loaded, 16)

            def load_tile(rows, i, pair, r):
                if not (isinstance(pair, int) and pair == 0):
                    sp.wait_ge(turned, 2 * pair + r - 1)
                sp.dma_start(xe[:, r], rows[bass.ds(i * P, P), :]).then_inc(tile_loaded[r], 16)

            for r in range(2):
                sp.wait_ge(x2_stored[r], B * 2 * 16)
            for r in range(2):
                load_tile(x2_rows, r, 0, r)
            with sp.Fori(1, NTOK // 2) as k:
                for r in range(2):
                    load_tile(x2_rows, k * 2 + r, k, r)
            sp.wait_ge(scattered, NTOK * 16)
            with sp.Fori(NTOK // 2, NTILE // 2) as k:
                for r in range(2):
                    load_tile(sorted_rows, k * 2 + r - NTOK, k, r)
            load_tile(sorted_rows, NROUTE - 1, NTILE // 2, 0)

            for g in range(4):
                sp.wait_ge(final_done, g + 1)
                sp.dma_start(out[g].rearrange("(n p) d -> p n d", p=P), total[:, g * 4:(g + 1) * 4]).then_inc(stored, 16)
            sp.wait_ge(stored, 4 * 16)

        @block.tensor
        def _(pe):
            m = Misc()
            bank = Misc()

            def prep(b):
                nb = 0 if b is None else b + 1
                pe.wait_ge(x_loaded, (nb + 1) * 16)
                for k in range(4):
                    v = prep_slot(b, k)
                    if not (b is None and k < 2):
                        pe.wait_ge(st_done, v - 2)
                    slot = st_ps[:, k % 2]
                    if k == 0:
                        for c in range(DC):
                            for t in range(QT):
                                last = nc.tensor.transpose(slot[:, c, t * P:(t + 1) * P], xin[:, t, c * P:(c + 1) * P], ident[:])
                    else:
                        if k == 1:
                            pe.wait_ge(st_done, prep_slot(b, 0))
                        for half in range(2):
                            for c in range(DC):
                                last = nc.tensor.matmul(slot[:, half, :], wqk_sb[:, c, k - 1, half, :], xT[:, c, :],
                                                        start=(c == 0), stop=(c == DC - 1))
                    last.then_inc(st_full, 1)

            def score_bank(b, qt, i):
                v = bank.next()
                if not (isinstance(v, int) and v <= 2):
                    pe.wait_ge(bank_done, v - 2)
                rows = banks(qt)[i]
                w = (qt + 1) * P
                for n, hs in enumerate(rows):
                    gs = hs // 4
                    o = s_ps[:, (i % 2), n * w:(n + 1) * w]
                    nc.tensor.matmul(o, q_stack[0:KROWS, qt, hs, :], k_stack[0:KROWS, 0:qt + 1, gs, :], start=True, stop=False)
                    last = nc.tensor.matmul(o[:, w - P:w], identb[:], mask[:], start=False, stop=True)
                last.then_inc(bank_full, 1)

            def task(name, arg, b):
                if name == "banks":
                    qt, lo, hi = arg
                    if lo == 0:
                        pe.wait_ge(q_loaded[qt], (b + 1) * SLOTS * 16)
                        pe.wait_ge(k_loaded, (b + 1) * SLOTS * 16)
                    for i in range(lo, hi):
                        score_bank(b, qt, i)
                if name not in MISC_TASKS:
                    return
                v = m.next()
                if not (isinstance(v, int) and v == 1):
                    pe.wait_ge(misc_done, v - 1)
                if name == "v":
                    for t in range(QT):
                        for c in range(DC):
                            last = nc.tensor.matmul(misc[:, t * P:(t + 1) * P], xT[:, c, t * P:(t + 1) * P], wv_sb[:, c, :],
                                                    start=(c == 0), stop=(c == DC - 1))
                elif name == "mt":
                    pe.wait_ge(split_done, b * QT + arg + 1)
                    last = nc.tensor.transpose(misc[:, 0:P // 2].bitcast(BF16), msplit[:, arg % 2, :], identb[:])
                elif name == "norm":
                    pe.wait_ge(pv_done, b * NUNIT + arg + 1)
                    for r in range(4):
                        last = nc.tensor.transpose(misc[:, r * P:(r + 1) * P], ol[:, arg % 2, r * P:(r + 1) * P], ident[:])
                elif name == "mean":
                    pe.wait_ge(summed, b + 1)
                    last = nc.tensor.matmul(misc[:, 0:H], averager[:], head_tot[:], start=True, stop=True)
                elif name == "var":
                    pe.wait_ge(squares_summed, b + 1)
                    last = nc.tensor.matmul(misc[:, 0:H], averager[:], head_sq[:], start=True, stop=True)
                elif name == "turn":
                    pe.wait_ge(scaled, b * QT + arg + 1)
                    for r in range(4):
                        last = nc.tensor.transpose(misc[:, r * P:(r + 1) * P], z[:, arg % 2, r * P:(r + 1) * P], ident[:])
                elif name == "project":
                    for r in range(4):
                        last = nc.tensor.matmul(misc[:, 0:D], zT[:, r, :], wo_sb[:, r, :], start=(r == 0), stop=(r == 3))
                elif name == "retake":
                    pe.wait_ge(x2_done, b * QT + arg + 1)
                    for ch in range(DC):
                        last = nc.tensor.transpose(misc[:, ch * P:(ch + 1) * P], x2s[:, arg % 2, ch * P:(ch + 1) * P], ident[:])
                elif name == "logits":
                    for ch in range(DC):
                        last = nc.tensor.matmul(misc[:, 0:E], x2T[:, ch, :], router_sb[:, ch, :], start=(ch == 0), stop=(ch == DC - 1))
                last.then_inc(misc_full, 1)

            def scores(b, n, prep):
                qt, g, kt = STEPS[n]
                v = st_at(b, n, prep)
                if n == FIRST_ST[qt]:
                    pe.wait_ge(max_loaded[qt], (b + 1) * 16)
                pe.wait_ge(st_done, v - 2)
                for s in range(2):
                    gs = 2 * g + s
                    last = nc.tensor.matmul(st_ps[:, n % 2, s, :], k_stack[0:MROWS, kt, gs, :],
                                            q_stack[0:MROWS, qt, gs * 4:gs * 4 + 4, :], start=True, stop=True)
                last.then_inc(st_full, 1)

            def weigh(b, n, prep):
                qt, g, kt = STEPS[n]
                u = qt * KV + g
                if kt == qt:
                    pe.wait_ge(diag_done, b * NUNIT + DIAG.index(n) + 1)
                else:
                    pe.wait_ge(st_done, st_at(b, n, prep))
                if kt == 0:
                    if u > 0:
                        pe.wait_ge(pv_done, b * NUNIT + u)
                for s in range(2):
                    last = nc.tensor.matmul(pv_ps[s * 64:(s + 1) * 64, :], vo[:, kt, g, :], probs[:, n % NP, s, :],
                                            start=(kt == 0), stop=(kt == qt))
                last.then_inc(pv_step, 1)

            def body(b, prep_next, post):
                if prep_next:
                    prep(b)
                scores(b, 0, prep_next)
                scores(b, 1, prep_next)
                for n in range(NSTEP):
                    for qt, i in BANKS_AT.get(n, []):
                        if i == 0:
                            pe.wait_ge(q_loaded[qt], (b + 1) * SLOTS * 16)
                        score_bank(b, qt, i)
                    if n + 2 < NSTEP:
                        scores(b, n + 2, prep_next)
                    weigh(b, n, prep_next)
                    for (name, arg), back in tasks_at(n, post):
                        task(name, arg, b - back)

            def boundary(b):
                for name, arg in BOUNDARY:
                    task(name, arg, b - 1 if name in OLD else b)

            pe.wait_ge(consts_loaded, NCONST * 16)
            pe.wait_ge(consts_ready, 2)
            prep(None)
            for name, arg in HEAD:
                task(name, arg, 0)
            body(0, True, False)
            with pe.Fori(1, B - 1) as b:
                m.turn(MISC_HEAD, MISC_TURN, b - 1)
                bank.turn(BANK_HEAD, BANK_TURN, b - 1)
                boundary(b)
                body(b, True, True)
            m.turn(MISC_HEAD, MISC_TURN, B - 2)
            bank.turn(BANK_HEAD, BANK_TURN, B - 2)
            boundary(B - 1)
            body(B - 1, False, True)
            for name, arg in TAIL:
                task(name, arg, B - 1)

            def turn_tile(pair, r):
                i = 2 * pair + r
                pe.wait_ge(tile_loaded[r], (pair + 1) * 16)
                if not (isinstance(i, int) and i == 0):
                    pe.wait_ge(turned_done, i)
                for ch in range(DC):
                    last = nc.tensor.transpose(s_ps[:, 0, ch * P:(ch + 1) * P], xe[:, r, ch * P:(ch + 1) * P], ident[:])
                last.then_inc(turned, 1)

            def up(pair, r, weights):
                i = 2 * pair + r
                pe.wait_ge(turned_done, i + 1)
                if not (isinstance(i, int) and i < 2):
                    pe.wait_ge(hid_done, i - 1)
                for half in range(2):
                    for ch in range(DC):
                        last = nc.tensor.matmul(st_ps[:, r, half, :], xeT[:, r, ch, :], weights(ch * 2 * F + half * F, F),
                                                start=(ch == 0), stop=(ch == DC - 1))
                last.then_inc(up_full, 1)

            def turn_hidden(pair, r):
                i = 2 * pair + r
                pe.wait_ge(hid_done, i + 1)
                if not (isinstance(i, int) and i == 0):
                    pe.wait_ge(hidT_done, i)
                for ch in range(F // P):
                    last = nc.tensor.transpose(s_ps[:, 1, ch * P:(ch + 1) * P], hid[:, r, ch * P:(ch + 1) * P], ident[:])
                last.then_inc(hid_turned, 1)

            def down(pair, r, weights):
                i = 2 * pair + r
                pe.wait_ge(hidT_done, i + 1)
                if not (isinstance(i, int) and i < 1):
                    pe.wait_ge(down_done, i)
                for ch in range(F // P):
                    last = nc.tensor.matmul(pv_ps[:, 0:D], hidT[:, r, ch, :], weights(WUP + ch * D, D),
                                            start=(ch == 0), stop=(ch == F // P - 1))
                last.then_inc(down_full, 1)

            def of_shared(at, n):
                return w_sh[:, at:at + n]

            def of_expert(i):
                e = pe.value_load(owner[0:1, bass.ds(i - NTOK, 1)], min_val=0, max_val=E - 1)
                return lambda at, n: w_exp[:, bass.ds(e * WEXP + at, n)]

            pe.wait_ge(shared_loaded, 32)
            turn_tile(0, 0)
            up(0, 0, of_shared)
            pe.wait_ge(chosen_done, 1)
            nc.tensor.matmul(misc[:, 0:NTOK * E], before[:], chosenb[:], start=True, stop=True)
            nc.tensor.matmul(misc[:, NTOK * E:2 * NTOK * E], onesb[:], chosenb[:], start=True, stop=True).then_inc(ranked, 1)
            with pe.Fori(0, NTOK // 2 - 1) as k:
                for r in range(2):
                    turn_tile(k + r, 1 - r)
                    up(k + r, 1 - r, of_shared)
                    turn_hidden(k, r)
                    down(k, r, of_shared)
            k = NTOK // 2 - 1
            turn_tile(k, 1)
            up(k, 1, of_shared)
            turn_hidden(k, 0)
            down(k, 0, of_shared)
            pe.wait_ge(owners_done, 1)
            pe.wait_ge(experts_loaded, 2 * E * 16)
            turn_tile(k + 1, 0)
            up(k + 1, 0, of_expert(NTOK))
            turn_hidden(k, 1)
            down(k, 1, of_shared)
            with pe.Fori(NTOK // 2, NTILE // 2) as k:
                for r in range(2):
                    turn_tile(k + r, 1 - r)
                    up(k + r, 1 - r, of_expert(k * 2 + r + 1))
                    turn_hidden(k, r)
                    down(k, r, of_expert(k * 2 + r))
            k = NTILE // 2
            turn_hidden(k, 0)
            down(k, 0, of_expert(NTILE - 1))

        @block.scalar
        def _(act):
            m = Misc()

            def evacuate(b, k):
                act.wait_ge(st_full, prep_slot(b, k))
                if k == 0:
                    nc.scalar.copy(xT[:], st_ps[:, 0]).then_inc(st_done, 1)
                else:
                    nc.scalar.copy(raw[:, k - 1], st_ps[:, k % 2]).then_inc(st_done, 1)

            def cast(nb, part, pair):
                if part == 0:
                    if not (isinstance(nb, int) and nb == 0):
                        act.wait_ge(parts_written, nb * 3 * 16)
                    act.wait_ge(prep_done, nb * NPREP + PREP_DONE[("odd", pair)])
                    nc.scalar.copy(by_half(parts[:, pair, 0]), raw_q(pair)).then_inc(high_done, 1)
                else:
                    act.wait_ge(prep_done, nb * NPREP + PREP_DONE[("rest", pair)])
                    nc.scalar.copy(by_half(parts[:, pair, 1]), raw_q(pair)).then_inc(mid_done, 1)

            def write_parts(nb, pair):
                act.wait_ge(prep_done, nb * NPREP + PREP_DONE[("low", pair)])
                act.dma_start(scratch[nb, pair].rearrange("s q h r t -> r (s q h) t"),
                              parts[:, pair].rearrange("p s q h t -> p (s q h) t")).then_inc(parts_written, 16)

            casts_at = {}
            for pair in range(3):
                casts_at.setdefault(PREP_AT[("odd", pair)] + 2, []).append(("cast", 0, pair))
                casts_at.setdefault(PREP_AT[("rest", pair)] + 2, []).append(("cast", 1, pair))
                casts_at.setdefault(PREP_AT[("low", pair)] + 3, []).append(("write", 0, pair))

            def task(name, arg, b):
                if name == "square":
                    act.wait_ge(centred, b + 1)
                    nc.scalar.activation(sq[:], dev[:], ACT.Square).then_inc(squared, 1)
                if name not in MISC_TASKS:
                    return
                v = m.next()
                if name == "v":
                    act.wait_ge(misc_full, v)
                    nc.scalar.copy(vo[:, :, :, 0:DV], misc[:].rearrange("p (t g d) -> p t g d", t=QT, g=KV)).then_inc(misc_done, 1)
                elif name == "turn":
                    act.wait_ge(misc_full, v)
                    nc.scalar.copy(zT[:], misc[:].rearrange("p (r t) -> p r t", r=4)).then_inc(misc_done, 1)
                elif name == "retake":
                    act.wait_ge(misc_full, v)
                    nc.scalar.copy(x2T[:], misc[:, 0:D].rearrange("p (c t) -> p c t", c=DC)).then_inc(misc_done, 1)

            def body(b, prep, post):
                if prep:
                    for k in range(4):
                        evacuate(b, k)
                for n in range(NSTEP):
                    qt, g, kt = STEPS[n]
                    v = st_at(b, n, prep)
                    act.wait_ge(st_full, v)
                    if n >= NP or (isinstance(b, int) and b > 0):
                        act.wait_ge(pv_step, b * NSTEP + n + 1 - NP)
                    nc.scalar.activation(probs[:, n % NP], st_ps[:, n % 2], ACT.Exp, scale=float(DH) ** -0.5).then_inc(st_done, 1)
                    if n >= 1:
                        finish_unit(b, n - 1)
                    for (name, arg), back in tasks_at(n - 1, post) if n else []:
                        task(name, arg, b - back)
                    for what, part, pair in casts_at.get(n, []) if prep else []:
                        if what == "cast":
                            cast(b + 1, part, pair)
                        else:
                            write_parts(b + 1, pair)
                finish_unit(b, NSTEP - 1)
                for (name, arg), back in tasks_at(NSTEP - 1, post):
                    task(name, arg, b - back)

            def finish_unit(b, n):
                qt, g, kt = STEPS[n]
                if kt != qt:
                    return
                u = qt * KV + g
                act.wait_ge(pv_step, b * NSTEP + n + 1)
                nc.scalar.copy(ol[:, u % 2], pv_ps[:]).then_inc(pv_done, 1)

            act.wait_ge(lam_summed, 1)
            nc.scalar.activation(lame[:], lams2[:], ACT.Exp).then_inc(lam_exp, 1)
            for k in range(4):
                evacuate(None, k)
            for op in PREP:
                if op[0] == "odd":
                    cast(0, 0, op[1])
                elif op[0] == "rest":
                    cast(0, 1, op[1])
                elif op[0] == "low":
                    write_parts(0, op[1])
            for name, arg in HEAD:
                task(name, arg, 0)
            def boundary(b):
                for name, arg in BOUNDARY:
                    task(name, arg, b - 1 if name in OLD else b)

            body(0, True, False)
            with act.Fori(1, B - 1) as b:
                m.turn(MISC_HEAD, MISC_TURN, b - 1)
                boundary(b)
                body(b, True, True)
            m.turn(MISC_HEAD, MISC_TURN, B - 2)
            boundary(B - 1)
            body(B - 1, False, True)
            for name, arg in TAIL:
                task(name, arg, B - 1)

            act.wait_ge(top_found, 1)
            nc.scalar.activation(gate[:, 0], top[:], ACT.Exp, scale=-1.0).then_inc(gate_exp, 1)

            def take_tile(pair, r):
                act.wait_ge(turned, 2 * pair + r + 1)
                nc.scalar.copy(xeT[:, r], s_ps[:, 0, 0:D].rearrange("p (c t) -> p c t", c=DC)).then_inc(turned_done, 1)

            def make_silu(pair, r):
                act.wait_ge(up_full, 2 * pair + r + 1)
                nc.scalar.activation(silu[:, r], st_ps[:, r, 0, :], ACT.Silu).then_inc(silu_done, 1)

            def take_hidden(pair, r):
                act.wait_ge(hid_turned, 2 * pair + r + 1)
                nc.scalar.copy(hidT[:, r], s_ps[:, 1].rearrange("p (c t) -> p c t", c=F // P)).then_inc(hidT_done, 1)

            def store_routed(pair, r):
                act.wait_ge(down_done, 2 * pair + r + 1)
                act.dma_start(routed_rows[bass.ds((pair * 2 + r - NTOK) * P, P), :], yo[:, r]).then_inc(routed_stored[r], 16)

            take_tile(0, 0)
            make_silu(0, 0)
            with act.Fori(0, NTOK // 2) as k:
                for r in range(2):
                    take_tile(k + r, 1 - r)
                    make_silu(k + r, 1 - r)
                    take_hidden(k, r)
            with act.Fori(NTOK // 2, NTILE // 2) as k:
                for r in range(2):
                    take_tile(k + r, 1 - r)
                    make_silu(k + r, 1 - r)
                    take_hidden(k, r)
                    store_routed(k, r)
            k = NTILE // 2
            take_hidden(k, 0)
            store_routed(k, 0)

        @block.gpsimd
        def _(pool):
            c = Chain(pool, pool_chain)

            def prep(b, op):
                what, pair = op
                i = PREP_AT[op]
                X = raw[:, pair]
                base = b * NPREP
                both = [P, 2, T]
                if what == "cos":
                    pool.wait_ge(st_done, (pair + 2) if isinstance(b, int) else ST_HEAD + (b - 1) * ST_TURN + pair + 2)
                    if pair > 0:
                        pool.wait_ge(prep_done, base + PREP_DONE[("odd", pair - 1)])
                    elif not isinstance(b, int):
                        pool.wait_ge(prep_done, base)
                    ins = nc.gpsimd.tensor_tensor(rot[:, 0], X, cos[:].unsqueeze(1).to_broadcast(both), ALU.mult)
                elif what == "sin":
                    ins = nc.gpsimd.tensor_tensor(rot[:, 1], X, sin[:].unsqueeze(1).to_broadcast(both), ALU.mult)
                elif what == "even":
                    pool.wait_ge(prep_done, base + PREP_DONE[("sin", pair)])
                    ins = nc.gpsimd.tensor_tensor(X[:, 0], rot[:, 0, 0], rot[:, 1, 1], ALU.subtract)
                elif what == "odd":
                    ins = nc.gpsimd.tensor_tensor(X[:, 1], rot[:, 1, 0], rot[:, 0, 1], ALU.add)
                elif what == "rest":
                    pool.wait_ge(high_done, b * 3 + pair + 1)
                    ins = nc.gpsimd.tensor_tensor(raw_q(pair), raw_q(pair), by_half(parts[:, pair, 0]), ALU.subtract)
                elif what == "low":
                    pool.wait_ge(mid_done, b * 3 + pair + 1)
                    ins = nc.gpsimd.tensor_tensor(by_half(parts[:, pair, 2]), raw_q(pair), by_half(parts[:, pair, 1]), ALU.subtract)
                ins.then_inc(prep_done, 1)

            def task(name, arg, b):
                if name == "var":
                    pool.wait_ge(att_var, b + 1)
                    c.link(nc.gpsimd.tensor_tensor(head_rstd[:], head_var[:], halfneg[:].to_broadcast([P, H]), ALU.pow))
                    c.link(nc.gpsimd.tensor_tensor(scale_row[:], gw[:].rearrange("p (h d) -> p h d", h=H),
                                                   head_rstd[:].unsqueeze(2).to_broadcast([P, H, DV]), ALU.mult))
                elif name == "affine":
                    c.link(nc.gpsimd.tensor_tensor(z[:, arg % 2], dev[:, arg].rearrange("p h d -> p (h d)"),
                                                   scale_row[:].rearrange("p h d -> p (h d)"), ALU.mult))
                    nc.gpsimd.tensor_tensor(z[:, arg % 2], z[:, arg % 2], gb[:], ALU.add).then_inc(scaled, 1)
                elif name == "project":
                    pool.wait_ge(y_var, b * QT + arg + 1)
                    nc.gpsimd.tensor_tensor(rstd[:, arg % 2:arg % 2 + 1], mv[:, arg % 2, 1:2], halfneg[:], ALU.pow).then_inc(y_rstd, 1)

            def body(b, prep_next, post):
                for n in range(NSTEP):
                    qt, g, kt = STEPS[n]
                    if kt == qt:
                        pool.wait_ge(st_done, st_at(b, n, prep_next))
                        pool.sem_inc(exps_taken, 1)
                        e = probs[:, n % NP].rearrange("p s (r q) -> p (s r) q", r=4)
                        nc.gpsimd.affine_select(out=e, in_=e, compare_op=ALU.is_ge, fill=0.0, base=0,
                                                pattern=[[0, 8], [1, P]], channel_multiplier=-1).then_inc(diag_done, 1)
                    if n >= 1:
                        for (name, arg), back in tasks_at(n - 1, post):
                            task(name, arg, b - back)
                    if prep_next and n < NPREP:
                        prep(b + 1, PREP[n])
                for (name, arg), back in tasks_at(NSTEP - 1, post):
                    task(name, arg, b - back)

            c.link(nc.gpsimd.memset(halfneg[:], -0.5))
            pool.wait_ge(consts_loaded, NCONST * 16)
            c.link(nc.gpsimd.tensor_scalar(gw[:], gw[:], 1.0 - LAMBDA_INIT, None, ALU.mult))
            c.link(nc.gpsimd.tensor_scalar(gb[:], gb[:], 1.0 - LAMBDA_INIT, None, ALU.mult))
            for op in PREP:
                prep(0, op)
            body(0, True, False)
            head = c.n
            with pool.Fori(1, B - 1) as b:
                c.turn(head, POOL_TURN, b - 1)
                body(b, True, True)
            c.turn(head, POOL_TURN, B - 2)
            body(B - 1, False, True)
            for name, arg in TAIL:
                task(name, arg, B - 1)

            pool.wait_ge(zeroed, 16)
            pool.wait_ge(slots_done, 1)
            pool.wait_ge(gated_done, 1)
            for t in range(NTOK):
                nc.gpsimd.indirect_dma_start(out=sorted_rows, out_offset=bass.IndirectOffsetOnAxis(ap=slot[:, t:t + 1], axis=0),
                                             in_=gated[:, t], in_offset=None).then_inc(scattered, 16)
            for r in range(2):
                pool.wait_ge(routed_stored[r], (NROUTE + 1 - r) // 2 * 16)
            for t in range(NTOK):
                nc.gpsimd.indirect_dma_start(out=gated[:, t], out_offset=None, in_=routed_rows,
                                             in_offset=bass.IndirectOffsetOnAxis(ap=slot[:, t:t + 1], axis=0)).then_inc(gathered[t // 4], 16)
            for g in range(4):
                pool.wait_ge(final_var, g + 1)
                nc.gpsimd.tensor_tensor(rstdf[:, g * 4:(g + 1) * 4], mvf[:, g * 4:(g + 1) * 4, 1], halfneg[:].to_broadcast([P, 4]),
                                        ALU.pow).then_inc(final_rstd, 1)

        @block.vector
        def _(dve):
            c = Chain(dve, dve_chain)
            m = Misc()
            bank = Misc()

            def maximum(qt, i):
                v = bank.next()
                rows = banks(qt)[i]
                dve.wait_ge(bank_full, v)
                w = (qt + 1) * P
                nc.vector.tensor_reduce(out=mneg[:, qt, rows[0]:rows[-1] + 1],
                                        in_=s_ps[:, i % 2, 0:len(rows) * w].rearrange("p (r k) -> p r k", r=len(rows)),
                                        axis=AX.X, op=ALU.max, negate=True).then_inc(bank_done, 1)
                if i == NBANK[qt] - 1:
                    dve.wait_ge(bank_done, v)
                    c.link(nc.vector.tensor_copy(msplit[:, qt % 2, 0:HS], mneg[:, qt]))
                    nc.vector.tensor_tensor(msplit[:, qt % 2, HS:2 * HS], mneg[:, qt], msplit[:, qt % 2, 0:HS],
                                            ALU.subtract).then_inc(split_done, 1)

            def task(name, arg, b):
                if name == "banks":
                    for i in range(arg[1], arg[2]):
                        maximum(arg[0], i)
                if name in MISC_TASKS:
                    v = m.next()
                if name == "mt":
                    dve.wait_ge(misc_full, v)
                    if not (isinstance(b, int) and b == 0 and arg < 2):
                        dve.wait_ge(max_stored, (b * QT + arg - 1) * 16)
                    nc.vector.tensor_copy(mT[:, arg % 2, :], misc[0:2 * HS, 0:P // 2].bitcast(BF16)).then_inc(misc_done, 1)
                elif name == "norm":
                    qt, g = divmod(arg, KV)
                    dve.wait_ge(misc_full, v)
                    t = misc[:].rearrange("p (r s d) -> p r s d", r=4, s=2)
                    c.link(nc.vector.reciprocal(rl[:], t[:, :, :, DV]))
                    c.link(nc.vector.tensor_scalar(rl[:, :, 1], rl[:, :, 1], neglam[:], None, ALU.mult))
                    nc.vector.tensor_tensor(o1[:], t[:, :, 0, 0:DV], rl[:, :, 0:1].to_broadcast([P, 4, DV]), ALU.mult)
                    ins = nc.vector.tensor_tensor(o2[:], t[:, :, 1, 0:DV], rl[:, :, 1:2].to_broadcast([P, 4, DV]), ALU.mult)
                    ins.then_inc(misc_done, 1)
                    dve.wait_ge(misc_done, v)
                    c.link(nc.vector.tensor_tensor(att[:, qt, g * 4:g * 4 + 4, :], o1[:], o2[:], ALU.add))
                    c.link(nc.vector.tensor_reduce(out=head_sum[:, qt, g * 4:g * 4 + 4], in_=att[:, qt, g * 4:g * 4 + 4, :],
                                                   axis=AX.X, op=ALU.add))
                elif name == "mean":
                    nc.vector.tensor_reduce(out=head_tot[:], in_=head_sum[:].rearrange("p q h -> p h q"), axis=AX.X,
                                            op=ALU.add).then_inc(summed, 1)
                    dve.wait_ge(misc_full, v)
                    mean = misc[:, 0:H].unsqueeze(2).to_broadcast([P, H, DV])
                    for qt in range(QT):
                        ins = nc.vector.tensor_tensor(dev[:, qt], att[:, qt], mean, ALU.subtract)
                        if qt == QT - 2:
                            c.link(ins)
                        if qt == QT - 1:
                            ins.then_inc(misc_done, 1)
                    dve.wait_ge(misc_done, v)
                    dve.sem_inc(centred, 1)
                elif name == "var":
                    dve.wait_ge(squared, b + 1)
                    nc.vector.tensor_reduce(out=head_sq[:], in_=sq[:].rearrange("p q h d -> p h q d"), axis=AX.XY,
                                            op=ALU.add).then_inc(squares_summed, 1)
                    dve.wait_ge(misc_full, v)
                    nc.vector.tensor_scalar(head_var[:], misc[:, 0:H], EPS, None, ALU.add).then_inc(misc_done, 1)
                    dve.wait_ge(misc_done, v)
                    dve.sem_inc(att_var, 1)
                elif name == "project":
                    dve.wait_ge(misc_full, v)
                    dve.wait_ge(xres_loaded[arg % 2], (b * 2 + arg // 2 + 1) * 16)
                    nc.vector.tensor_tensor(y[:, arg % 2], misc[:, 0:D], xres[:, arg % 2], ALU.add).then_inc(misc_done, 1)
                    dve.wait_ge(misc_done, v)
                    c.link(nc.vector.bn_stats(st6[:], y[:, arg % 2]))
                    dve.sem_inc(stats_taken, 1)
                    c.link(nc.vector.bn_aggr(mv[:, arg % 2], st6[:]))
                    nc.vector.tensor_scalar(mv[:, arg % 2, 1:2], mv[:, arg % 2, 1:2], EPS, None, ALU.add).then_inc(y_var, 1)
                elif name == "x2":
                    dve.wait_ge(y_rstd, b * QT + arg + 1)
                    if not (isinstance(b, int) and b == 0 and arg < 2):
                        dve.wait_ge(x2_stored[arg % 2], (b * 2 + arg // 2) * 16)
                    nc.vector.tensor_scalar(x2s[:, arg % 2], y[:, arg % 2], mv[:, arg % 2, 0:1],
                                            rstd[:, arg % 2:arg % 2 + 1], ALU.subtract, ALU.mult).then_inc(x2_done, 1)
                    nc.vector.tensor_scalar(x2[:, bass.ds(b * QT + arg, 1), :], y[:, arg % 2:arg % 2 + 1], mv[:, arg % 2, 0:1],
                                            rstd[:, arg % 2:arg % 2 + 1], ALU.subtract, ALU.mult).then_inc(x2_kept, 1)
                elif name == "logits":
                    dve.wait_ge(misc_full, v)
                    nc.vector.tensor_copy(logits[:, bass.ds(b * QT + arg, 1), :], misc[:, 0:E].unsqueeze(1)).then_inc(misc_done, 1)

            def body(b, post):
                for n in range(NSTEP):
                    for qt, i in BANKS_AT.get(n, []):
                        maximum(qt, i)
                    for (name, arg), back in tasks_at(n, post):
                        task(name, arg, b - back)

            def boundary(b):
                for name, arg in BOUNDARY:
                    task(name, arg, b - 1 if name in OLD else b)

            nc.vector.memset(zero_row[:], 0.0).then_inc(zero_ready, 1)
            c.link(nc.vector.memset(onesb[:], 1.0))
            c.link(nc.vector.memset(msplit[:, :, 2 * HS:P], 0.0))
            c.link(nc.vector.memset(averager[:], 1.0 / (T * DV)))
            c.link(nc.vector.memset(vo[:, :, :, DV:2 * DV], 1.0))
            c.link(nc.vector.memset(k_stack[KROWS:P], 1.0))
            dve.wait_ge(consts_loaded, NCONST * 16)
            nc.vector.tensor_copy(identb[:], ident[:]).then_inc(consts_ready, 1)
            nc.vector.tensor_copy(mask[:], mask_f[:]).then_inc(consts_ready, 1)
            c.link(nc.vector.tensor_scalar(before[:], mask_f[:], 0.0, None, ALU.is_lt))
            c.link(nc.vector.tensor_tensor(lamp[:], lamv[:, 0:4:2, :], lamv[:, 1:4:2, :], ALU.mult))
            nc.vector.tensor_reduce(out=lams2[:], in_=lamp[:], axis=AX.X, op=ALU.add).then_inc(lam_summed, 1)
            dve.wait_ge(lam_exp, 1)
            c.link(nc.vector.tensor_tensor(neglam[:], lame[:, 1:2], lame[:, 0:1], ALU.subtract))
            c.link(nc.vector.tensor_scalar(neglam[:], neglam[:], -LAMBDA_INIT, None, ALU.add))
            for name, arg in HEAD:
                task(name, arg, 0)
            body(0, False)
            head = c.n
            with dve.Fori(1, B - 1) as b:
                m.turn(MISC_HEAD, MISC_TURN, b - 1)
                bank.turn(BANK_HEAD, BANK_TURN, b - 1)
                c.turn(head, DVE_TURN, b - 1)
                boundary(b)
                body(b, True)
            m.turn(MISC_HEAD, MISC_TURN, B - 2)
            bank.turn(BANK_HEAD, BANK_TURN, B - 2)
            c.turn(head, DVE_TURN, B - 2)
            boundary(B - 1)
            body(B - 1, True)
            for name, arg in TAIL:
                task(name, arg, B - 1)

            dve.wait_ge(misc_done, m.turns + m.n)
            dve.wait_ge(x2_kept, NTOK)
            tok = [P, NTOK, E]
            expert = counts[:, 0:E].unsqueeze(1).to_broadcast(tok)
            nc.vector.tensor_reduce(out=top[:], in_=logits[:], axis=AX.X, op=ALU.max).then_inc(top_found, 1)
            dve.wait_ge(top_found, 1)
            c.link(nc.vector.tensor_tensor(is_top[:], logits[:], top[:].unsqueeze(2).to_broadcast(tok), ALU.is_equal))
            c.link(nc.vector.tensor_scalar(is_top[:], is_top[:], -float(E), float(E), ALU.mult, ALU.add))
            c.link(nc.vector.tensor_tensor(choice[:], is_top[:], expert, ALU.add))
            c.link(nc.vector.tensor_reduce(out=first[:], in_=choice[:], axis=AX.X, op=ALU.min))
            picked = first[:].unsqueeze(2).to_broadcast(tok)
            nc.vector.tensor_tensor(chosenb[:], expert, picked, ALU.is_equal).then_inc(chosen_done, 1)
            c.link(nc.vector.tensor_tensor(chosen[:], expert, picked, ALU.is_equal))
            dve.wait_ge(gate_exp, 1)
            c.link(nc.vector.tensor_scalar(gate[:, 0], gate[:, 0], 1.0, None, ALU.add))
            c.link(nc.vector.reciprocal(gate[:, 1], gate[:, 0]))
            nc.vector.tensor_tensor(gated[:], x2[:], gate[:, 1].unsqueeze(2).to_broadcast([P, NTOK, D]), ALU.mult).then_inc(gated_done, 1)
            dve.wait_ge(ranked, 1)
            rank = misc[:, 0:NTOK * E].rearrange("p (n e) -> p n e", e=E)
            c.link(nc.vector.tensor_copy(scan[:, 0], misc[:, NTOK * E:2 * NTOK * E].rearrange("p (n e) -> p n e", e=E)))
            a = 0
            for d in (1, 2, 4, 8):
                nc.vector.tensor_copy(scan[:, 1 - a, 0:d], scan[:, a, 0:d])
                c.link(nc.vector.tensor_tensor(scan[:, 1 - a, d:], scan[:, a, d:], scan[:, a, 0:NTOK - d], ALU.add))
                a = 1 - a
            cmp = [P, E, NTOK]
            c.link(nc.vector.tensor_tensor(tiles_cmp[:], scan[:, a, NTOK - 1].unsqueeze(2).to_broadcast(cmp),
                                           counts[:, E:E + NTOK].unsqueeze(1).to_broadcast(cmp), ALU.is_gt))
            c.link(nc.vector.tensor_reduce(out=tiles_n[:], in_=tiles_cmp[:], axis=AX.X, op=ALU.add))
            c.link(nc.vector.tensor_copy(tiles_cum[:, 0], tiles_n[:]))
            t = 0
            for d in (1, 2, 4):
                nc.vector.tensor_copy(tiles_cum[:, 1 - t, 0:d], tiles_cum[:, t, 0:d])
                c.link(nc.vector.tensor_tensor(tiles_cum[:, 1 - t, d:], tiles_cum[:, t, d:], tiles_cum[:, t, 0:E - d], ALU.add))
                t = 1 - t
            c.link(nc.vector.tensor_tensor(first_slot[:], tiles_cum[:, t], tiles_n[:], ALU.subtract))
            c.link(nc.vector.tensor_scalar(first_slot[:], first_slot[:], float(P), None, ALU.mult))
            c.link(nc.vector.tensor_tensor(place_f[:], rank, scan[:, a], ALU.add))
            c.link(nc.vector.tensor_tensor(scan[:, 1 - a], misc[:, NTOK * E:2 * NTOK * E].rearrange("p (n e) -> p n e", e=E),
                                           first_slot[:].unsqueeze(1).to_broadcast(tok), ALU.subtract))
            c.link(nc.vector.tensor_tensor(place_f[:], place_f[:], scan[:, 1 - a], ALU.subtract))
            c.link(nc.vector.tensor_tensor(place_f[:], place_f[:], chosen[:], ALU.mult))
            c.link(nc.vector.tensor_reduce(out=slot_f[:], in_=place_f[:], axis=AX.X, op=ALU.add))
            nc.vector.tensor_copy(slot[:], slot_f[:]).then_inc(slots_done, 1)
            own = [P, NROUTE, E]
            c.link(nc.vector.tensor_tensor(owner_cmp[:], tiles_cum[:, t].unsqueeze(1).to_broadcast(own),
                                           counts[:, E + NTOK:].unsqueeze(2).to_broadcast(own), ALU.is_le))
            c.link(nc.vector.tensor_reduce(out=owner_f[:], in_=owner_cmp[:], axis=AX.X, op=ALU.add))
            nc.vector.tensor_scalar(owner[:], owner_f[:], float(E - 1), None, ALU.min).then_inc(owners_done, 1)

            def make_hidden(pair, r):
                i = 2 * pair + r
                dve.wait_ge(silu_done, i + 1)
                nc.vector.tensor_tensor(hid[:, r], silu[:, r], st_ps[:, r, 1, :], ALU.mult).then_inc(hid_done, 1)

            def add_shared(pair, r):
                i = 2 * pair + r
                dve.wait_ge(down_full, i + 1)
                nc.vector.tensor_tensor(total[:, bass.ds(i, 1), :], x2[:, bass.ds(i, 1), :], pv_ps[:, 0:D].unsqueeze(1), ALU.add).then_inc(down_done, 1)

            def take_routed(pair, r):
                i = 2 * pair + r
                dve.wait_ge(down_full, i + 1)
                if not (isinstance(pair, int) and pair == NTOK // 2):
                    dve.wait_ge(routed_stored[r], (pair - NTOK // 2) * 16)
                nc.vector.tensor_copy(yo[:, r], pv_ps[:, 0:D]).then_inc(down_done, 1)

            make_hidden(0, 0)
            with dve.Fori(0, NTOK // 2) as k:
                for r in range(2):
                    make_hidden(k + r, 1 - r)
                    add_shared(k, r)
            with dve.Fori(NTOK // 2, NTILE // 2) as k:
                for r in range(2):
                    make_hidden(k + r, 1 - r)
                    take_routed(k, r)
            take_routed(NTILE // 2, 0)

            for g in range(4):
                dve.wait_ge(gathered[g], 4 * 16)
                if g == 0:
                    dve.wait_ge(down_done, NTILE)
                rows = slice(g * 4, (g + 1) * 4)
                c.link(nc.vector.tensor_tensor(total[:, rows], total[:, rows], gated[:, rows], ALU.add))
                for t in range(g * 4, g * 4 + 4):
                    ins = nc.vector.bn_stats(st6f[:, t], total[:, t])
                c.link(ins)
                for t in range(g * 4, g * 4 + 4):
                    ins = nc.vector.bn_aggr(mvf[:, t], st6f[:, t])
                c.link(ins)
                nc.vector.tensor_scalar(mvf[:, rows, 1], mvf[:, rows, 1], EPS, None, ALU.add).then_inc(final_var, 1)
            for g in range(4):
                dve.wait_ge(final_rstd, g + 1)
                for t in range(g * 4, g * 4 + 4):
                    ins = nc.vector.tensor_scalar(total[:, t], total[:, t], mvf[:, t, 0:1], rstdf[:, t:t + 1], ALU.subtract, ALU.mult)
                ins.then_inc(final_done, 1)


def kernel(**inputs):
    import concourse.bacc as bacc
    from concourse.bass_utils import run_bass_kernel_spmd as run

    a = {k.replace("L0_", ""): np.ascontiguousarray(v) for k, v in inputs.items()}
    wq = a["attn_Wq"].reshape(D, 2, 2, 4, 2, 8, 2).transpose(0, 1, 6, 5, 2, 4, 3).reshape(D, 2, 2, P)
    wk = a["attn_Wk"].reshape(D, KV, 2, 8, 2).transpose(0, 4, 3, 1, 2).reshape(D, 2, 8, 2 * KV)
    wk = np.concatenate([wk, wk], axis=3).reshape(D, 1, 2, P)
    inv = (1.0 / np.float32(10000.0) ** (np.arange(0, DH, 2, dtype=np.float32) / np.float32(DH))).astype(np.float32)
    angle = (np.arange(T, dtype=np.float32)[:, None] * inv[None, :]).astype(np.float32)
    cos = np.repeat(np.cos(angle.astype(np.float64)).T.astype(np.float32), 16, axis=0)
    sin = np.repeat(np.sin(angle.astype(np.float64)).T.astype(np.float32), 16, axis=0)
    i = np.arange(P)
    arrays = {
        "x": a["attn_x"], "wqk": np.ascontiguousarray(np.concatenate([wq, wk], axis=1)), "wv": a["attn_Wv"], "wo": a["attn_Wo"],
        "lq1": a["attn_lambda_q1"], "lk1": a["attn_lambda_k1"], "lq2": a["attn_lambda_q2"], "lk2": a["attn_lambda_k2"],
        "gnw": a["attn_gn_w"], "gnb": a["attn_gn_b"], "cos_d": np.ascontiguousarray(cos), "sin_d": np.ascontiguousarray(sin),
        "ident_d": np.eye(P, dtype=np.float32), "mask_d": np.where(i[None, :] > i[:, None], NEG, 0.0).astype(np.float32),
        "router": np.ascontiguousarray(a["ffn_router_w"].T), "w_up": a["ffn_w_gate_up"], "w_down": a["ffn_w_down"],
        "s_up": a["ffn_shared_gate_up"], "s_down": a["ffn_shared_down"],
        "counts_d": np.concatenate([np.arange(E), np.arange(NTOK) * P, np.arange(NROUTE)]).astype(np.float32),
    }
    nc = bacc.Bacc("TRN2", target_bir_lowering=False, num_devices=1)
    t = {n: nc.dram_tensor(n + "_in", v.shape, mybir.dt.from_np(v.dtype), kind="ExternalInput").ap() for n, v in arrays.items()}
    out = nc.dram_tensor("out", (B, T, D), F32, kind="ExternalOutput").ap()
    build(nc, t["x"], t["wqk"], t["wv"], t["wo"], [t["lq1"], t["lk1"], t["lq2"], t["lk2"]], t["gnw"], t["gnb"],
          t["cos_d"], t["sin_d"], t["ident_d"], t["mask_d"],
          t["router"], t["w_up"], t["w_down"], t["s_up"], t["s_down"], t["counts_d"], out)
    r = run(nc, [{n + "_in": v for n, v in arrays.items()}], core_ids=[0])
    return r.results[0]["out"]
```

```python
from contextlib import ExitStack

import numpy as np

import concourse.bass as bass
from concourse import mybir

F32 = mybir.dt.float32
BF16 = mybir.dt.bfloat16
I32 = mybir.dt.int32
ALU = mybir.AluOpType
ACT = mybir.ActivationFunctionType
AX = mybir.AxisListType

P = 128
B, T, D = 4, 512, 256
H, KV, DH = 16, 4, 16
HS = 2 * H
DV = 2 * DH
QT = T // P
DC = D // P
SLOTS = 6
QPART = (0, 0, 0, 1, 1, 2)
KPART = (0, 1, 2, 0, 1, 0)
KROWS = SLOTS * DH
MROWS = KROWS + 2
LAMBDA_INIT = 0.2
EPS = 1e-5
NEG = -1e30
BEGUN = 1
NP = 4
E, F = 8, 512
NTOK = B * QT
NROUTE = NTOK + E - 1
LOOPED = (NROUTE - 2) // 2
WUP = DC * 2 * F
WEXP = WUP + F // P * D


class Chain:

    def __init__(self, eng, sem):
        self.eng, self.sem, self.n, self.turns = eng, sem, 0, 0

    def link(self, ins):
        self.n += 1
        ins.then_inc(self.sem, 1)
        self.eng.wait_ge(self.sem, self.turns + self.n)

    def turn(self, head, per, done):
        assert self.n in (head, head + per), (self.n, head, per)
        self.n, self.turns = head, done * per


STEPS = [(qt, g, kt) for qt in range(QT) for g in range(KV) for kt in range(qt + 1)]
NSTEP = len(STEPS)
NUNIT = QT * KV
DIAG = [n for n, (qt, g, kt) in enumerate(STEPS) if kt == qt]


def banks(qt):
    per = max(1, QT // (qt + 1))
    return [list(range(i, i + per)) for i in range(0, HS, per)]


NBANK = [len(banks(qt)) for qt in range(QT)]
FIRST_ST = [min(n for n, s in enumerate(STEPS) if s[0] == qt) for qt in range(QT)]
LAST_ST = [max(n for n, s in enumerate(STEPS) if s[0] == qt) for qt in range(QT)]


def spread(count, lo, hi):
    at = {}
    for i in range(count):
        at.setdefault(lo + i * (hi - lo) // count, []).append(i)
    return at


BANKS_AT = {}
for _qt, _lo, _hi, _back in ((2, 0, 7, 0), (3, 7, 18, 0), (0, 33, 35, -1), (1, 35, 39, -1)):
    for _n, _idx in spread(NBANK[_qt], _lo, _hi).items():
        BANKS_AT.setdefault(_n, []).extend((_qt, i, _back) for i in _idx)

TASKS = {n: [] for n in range(NSTEP)}
for _u in range(NUNIT - 1):
    _qt, _g = divmod(_u, KV)
    TASKS[FIRST_ST[_qt] + (_g + 1) * (_qt + 1) + 1].append(("norm", _u, 0))
TASKS[7].append(("mt", 2, 0))
TASKS[18].append(("mt", 3, 0))
TASKS[35].append(("mt", 0, -1))
TASKS[39].append(("mt", 1, -1))
PER_TILE = ("affine", "turn", "project", "x2", "retake", "logits")
SHARED = [(name, fc) for fc in range(F // P) for name in ("shared_gate", "shared_up")] + [("shared_down", t) for t in range(QT)]
for _n, _name in ((0, "mean"), (2, "square"), (4, "var")):
    TASKS[_n].append((_name, 0, 1))
for _qt in range(QT):
    for _i, _name in enumerate(PER_TILE):
        TASKS[6 + 4 * _qt + _i].append((_name, _qt, 1))
TASKS[24].append(("top", 0, 1))
TASKS[25].append(("gate", 0, 1))
for _i, (_name, _arg) in enumerate(SHARED):
    TASKS[28 + _i].append((_name, _arg, 1))

HEAD = [("v", 0, 0), ("banks", (0, 0, 8), 0), ("mt", 0, 0), ("banks", (1, 0, 16), 0), ("mt", 1, 0)]
BOUNDARY = [("v", 0, 0), ("norm", NUNIT - 1, 1)]
TAIL = [("norm", NUNIT - 1, 0), ("mean", 0, 0), ("square", 0, 0), ("var", 0, 0)] + [(_name, _qt, 0) for _name, _qt in (
    ("affine", 0), ("turn", 0), ("affine", 1), ("project", 0), ("turn", 1), ("affine", 2), ("project", 1), ("x2", 0), ("retake", 0),
    ("turn", 2), ("affine", 3), ("logits", 0), ("project", 2), ("x2", 1), ("retake", 1), ("turn", 3), ("logits", 1),
    ("project", 3), ("x2", 2), ("retake", 2), ("logits", 2), ("x2", 3), ("retake", 3), ("logits", 3), ("top", 0), ("gate", 0))]
MISC_TASKS = ("v", "mt", "norm", "mean", "var", "turn", "project", "retake", "logits",
              "shared_gate", "shared_up", "shared_down")


def tasks_at(n, ahead, post):
    return [t for t in TASKS[n] if t[2] == 0 or (t[2] < 0 and ahead) or (t[2] > 0 and post)]


def body_tasks(ahead, post):
    return [t for n in range(NSTEP) for t in tasks_at(n, ahead, post)]


def misc_count(tasks):
    return sum(t[0] in MISC_TASKS for t in tasks)


FIRST, TURN = HEAD + body_tasks(True, False), BOUNDARY + body_tasks(True, True)
MISC_HEAD, MISC_TURN = misc_count(FIRST), misc_count(TURN)
BANK_HEAD, BANK_TURN = sum(NBANK) + NBANK[0] + NBANK[1], sum(NBANK)
ST_HEAD, ST_PREP = 4, 4
ST_TURN = ST_PREP + NSTEP
LINKS = {"norm": 2, "mean": 1, "project": 2, "gate": 2}
POOL_TURN = 2 + QT
DVE_TURN = sum(LINKS.get(t[0], 0) for t in TURN) + QT


def turned_maxima(b, qt, back):
    tasks, before = (FIRST, 0) if isinstance(b, int) and b == 0 else (TURN, MISC_HEAD + (b - 1) * MISC_TURN)
    return before + misc_count(tasks[:tasks.index(("mt", qt, back)) + 1])


PREP = [("cos", 0), ("sin", 0), ("even", 0), ("odd", 0), ("cos", 1), ("sin", 1), ("rest", 0), ("even", 1), ("odd", 1),
        ("cos", 2), ("low", 0), ("sin", 2), ("rest", 1), ("even", 2), ("odd", 2), ("low", 1), ("rest", 2), ("low", 2)]
PREP_AT = {k: i for i, k in enumerate(PREP)}
PREP_DONE = {k: i + 1 for i, k in enumerate(PREP)}
NPREP = len(PREP)
PREP_FROM = 5


def build(nc, x, wqk, wv, wo, lams, gnw, gnb, cos_d, sin_d, ident_d, mask_d,
          router, w_up, w_down, s_up, s_down, counts_d, out):
    scratch = nc.dram_tensor("qk_parts", (B, 3, 3, QT, 2, P, P), BF16, kind="Internal").ap()
    mrows = nc.dram_tensor("max_rows", (B, QT, 2 * HS, P), BF16, kind="Internal").ap()

    gated_rows = nc.dram_tensor("gated_rows", (B, T, D), F32, kind="Internal").ap()
    sorted_rows = nc.dram_tensor("sorted_rows", (NROUTE * P, D), F32, kind="Internal").ap()
    routed_rows = nc.dram_tensor("routed_rows", (NROUTE * P, D), F32, kind="Internal").ap()

    ctx = ExitStack()
    with ctx:
        def sb(name, shape, dt=F32):
            return ctx.enter_context(nc.sbuf_tensor(name, shape, dt))

        def sem(name):
            return ctx.enter_context(nc.semaphore(name))

        w_exp = sb("w_exp", [P, E * WEXP])
        work = sb("work", [P, 11264])

        class Place:

            def __init__(self, tensor):
                self.tensor, self.at = tensor, 0

            def take(self, columns, dt=F32):
                a = self.tensor[:, self.at:self.at + columns]
                self.at += columns
                return a if dt == F32 else a.bitcast(dt)

        early = Place(w_exp)
        raw = early.take(3 * 2 * T).rearrange("p (a h t) -> p a h t", a=3, h=2)
        parts = early.take(3 * 3 * T, BF16).rearrange("p (a s q h t) -> p a s q h t", a=3, s=3, q=QT, h=2)
        k_near = early.take(2 * KV * P, BF16).rearrange("p (q r t) -> p q r t", q=2, r=2 * KV)
        q_stack = early.take(QT * HS * P // 2, BF16).rearrange("p (q r t) -> p q r t", q=QT, r=HS)
        k_stack = early.take(QT * KV * P, BF16).rearrange("p (q r t) -> p q r t", q=QT, r=2 * KV)
        vo_lam = early.take(QT * KV * 2 * DV).rearrange("p (t g d) -> p t g d", t=QT, g=KV)
        probs = early.take(NP * 2 * T).rearrange("p (n s t) -> p n s t", n=NP, s=2)
        assert early.at <= E * WEXP and 2 * WEXP <= 3 * 2 * T + 3 * 3 * T
        assert 4 * WEXP <= 3 * 2 * T + 3 * 3 * T + 2 * KV * P + 2 * HS * P // 2

        mine = Place(work)
        att = mine.take(QT * H * DV).rearrange("p (q h d) -> p q h d", q=QT, h=H)
        dev = mine.take(QT * H * DV).rearrange("p (q h d) -> p q h d", q=QT, h=H)
        sq = mine.take(QT * H * DV).rearrange("p (q h d) -> p q h d", q=QT, h=H)
        rot = sq.rearrange("p q h d -> p (q h d)").rearrange("p (a h t) -> p a h t", a=2, h=2)
        gated_out = sq[:, 0:2].rearrange("p q h d -> p (q h d)").rearrange("p (n d) -> p n d", n=QT)
        shared_silu = sq[:, 2].rearrange("p h d -> p (h d)")
        tail_silus = sq[:, 2:4].rearrange("p q h d -> p q (h d)")
        shared_hidT = dev.rearrange("p q h d -> p (q h d)").rearrange("p (c t) -> p c t", c=F // P)
        vo = mine.take(QT * KV * 2 * DV).rearrange("p (t g d) -> p t g d", t=QT, g=KV)
        xin = mine.take(QT * D).rearrange("p (n d) -> p n d", n=QT)
        xT = mine.take(DC * T).rearrange("p (c t) -> p c t", c=DC)
        ol = mine.take(2 * T).rearrange("p (u t) -> p u t", u=2)
        xres = mine.take(QT * D).rearrange("p (n d) -> p n d", n=QT)

        tables = sb("tables", [P, 3584])
        mine = Place(tables)
        cos = mine.take(T)
        sin = mine.take(T)
        wqk_sb = mine.take(DC * 3 * 2 * P).rearrange("p (c a h m) -> p c a h m", c=DC, a=3, h=2)
        wo_sb = mine.take(4 * D).rearrange("p (c n) -> p c n", c=4)

        theirs = Place(tables)
        xe = theirs.take(2 * D).rearrange("p (u d) -> p u d", u=2)
        xeT = theirs.take(2 * D).rearrange("p (u c t) -> p u c t", u=2, c=DC)
        yo = theirs.take(2 * D).rearrange("p (u d) -> p u d", u=2)
        is_top = theirs.take(NTOK * E).rearrange("p (n e) -> p n e", e=E)
        choice = theirs.take(NTOK * E).rearrange("p (n e) -> p n e", e=E)
        chosen = theirs.take(NTOK * E).rearrange("p (n e) -> p n e", e=E)
        scan = theirs.take(2 * NTOK * E).rearrange("p (u n e) -> p u n e", u=2, e=E)
        tiles_cmp = theirs.take(E * NTOK).rearrange("p (e n) -> p e n", e=E)
        place_f = theirs.take(NTOK * E).rearrange("p (n e) -> p n e", e=E)
        owner_cmp = theirs.take(NROUTE * E).rearrange("p (n e) -> p n e", e=E)

        gated = [xin, vo.rearrange("p t g d -> p (t g d)").rearrange("p (n d) -> p n d", n=QT),
                 att[:, 0:2].rearrange("p q h d -> p (q h d)").rearrange("p (n d) -> p n d", n=QT), gated_out]
        theirs = Place(work)
        theirs.at = 8192
        silu = theirs.take(2 * F).rearrange("p (u f) -> p u f", u=2)
        hid = theirs.take(2 * F).rearrange("p (u f) -> p u f", u=2)
        hidT = theirs.take(2 * F).rearrange("p (u c t) -> p u c t", u=2, c=F // P)

        wv_sb = sb("wv_sb", [P, DC, P])
        w_sh = sb("w_sh", [P, WEXP])
        router_sb = sb("router_sb", [P, DC, E])
        gw = sb("gw", [P, 2 * H * DH])
        gb = sb("gb", [P, 2 * H * DH])
        ident = sb("ident", [P, P])
        identb = sb("identb", [P, P], BF16)
        mask_f = sb("mask_f", [P, P])
        mask = sb("mask", [P, P], BF16)
        before = sb("before", [P, P], BF16)
        onesb = sb("onesb", [P, P], BF16)
        lamv = sb("lamv", [P, 4, DH])
        lamp = sb("lamp", [P, 2, DH])
        lams2 = sb("lams2", [P, 2])
        lame = sb("lame", [P, 2])
        neglam = sb("neglam", [P, 1])
        mneg = sb("mneg", [P, QT, HS])
        msplit = sb("msplit", [P, 2, P], BF16)
        mT = sb("mT", [2 * HS, 2, P], BF16)
        rl = sb("rl", [P, 4, 2])
        o12 = sb("o12", [P, 4, 2, DV])
        head_tot = sb("head_tot", [P, H])
        head_sq = sb("head_sq", [P, H])
        head_var = sb("head_var", [P, H])
        head_rstd = sb("head_rstd", [P, H])
        scale_row = sb("scale_row", [P, H, DV])
        averager = sb("averager", [P, P])
        st6 = sb("st6", [P, 6])
        mv = sb("mv", [P, 2, 2])
        rstd = sb("rstd", [P, 2])
        halfneg = sb("halfneg", [P, 1])
        zT = sb("zT", [P, 4, P])
        y = sb("y", [P, 2, D])
        zero_row = y[:, 0]
        x2T = sb("x2T", [P, DC, T])
        x2 = sb("x2", [P, NTOK, D])
        logits = sb("logits", [P, NTOK, E])
        counts = sb("counts", [P, E + NTOK + NROUTE])
        top = sb("top", [P, NTOK])
        logits_now = sb("logits_now", [P, QT, E])
        top_now = sb("top_now", [P, QT])
        gate = sb("gate", [P, 2, QT])
        first = sb("first", [P, NTOK])
        chosenb = sb("chosenb", [P, NTOK, E], BF16)
        tiles_n = sb("tiles_n", [P, E])
        tiles_cum = sb("tiles_cum", [P, 2, E])
        first_slot = sb("first_slot", [P, E])
        slot_f = sb("slot_f", [P, NTOK])
        slot = sb("slot", [P, NTOK], I32)
        owner_f = sb("owner_f", [P, NROUTE])
        owner = sb("owner", [P, NROUTE], I32)
        st6f = sb("st6f", [P, NTOK, 6])
        mvf = sb("mvf", [P, NTOK, 2])
        rstdf = sb("rstdf", [P, NTOK])

        s_ps = ctx.enter_context(nc.psum_tensor("s_ps", [P, 2, T], F32))
        st_ps = ctx.enter_context(nc.psum_tensor("st_ps", [P, 2, 2, T], F32))
        pv_ps = ctx.enter_context(nc.psum_tensor("pv_ps", [P, T], F32))
        misc = ctx.enter_context(nc.psum_tensor("misc", [P, T], F32))

        consts_loaded = sem("consts_loaded")
        ident_loaded = sem("ident_loaded")
        wqk_loaded = sem("wqk_loaded")
        consts_ready = sem("consts_ready")
        start_pool = sem("start_pool")
        start_dve = sem("start_dve")
        start_high = sem("start_high")
        start_mid = sem("start_mid")
        x_loaded = sem("x_loaded")
        xres_loaded = sem("xres_loaded")
        parts_written = sem("parts_written")
        q_loaded = [sem(f"q_loaded{i}") for i in range(QT)]
        k_loaded = sem("k_loaded")
        max_stored = sem("max_stored")
        max_loaded = [sem(f"max_loaded{i}") for i in range(QT)]
        st_full = sem("st_full")
        st_done = sem("st_done")
        bank_full = sem("bank_full")
        bank_done = sem("bank_done")
        misc_full = sem("misc_full")
        misc_done = sem("misc_done")
        pv_done = sem("pv_done")
        pv_step = sem("pv_step")
        diag_done = sem("diag_done")
        prep_done = sem("prep_done")
        high_done = sem("high_done")
        mid_done = sem("mid_done")
        split_done = sem("split_done")
        dve_chain = sem("dve_chain")
        pool_chain = sem("pool_chain")
        lam_summed = sem("lam_summed")
        lam_exp = sem("lam_exp")
        lam_ready = sem("lam_ready")
        summed = sem("summed")
        centred = sem("centred")
        squared = sem("squared")
        stats_taken = sem("stats_taken")
        exps_taken = sem("exps_taken")
        squares_summed = sem("squares_summed")
        att_var = sem("att_var")
        scaled = sem("scaled")
        scale_ready = sem("scale_ready")
        y_var = sem("y_var")
        y_rstd = sem("y_rstd")
        x2_done = sem("x2_done")
        gated_stored = sem("gated_stored")
        gated_loaded = sem("gated_loaded")
        near_loaded = sem("near_loaded")
        x2_kept = sem("x2_kept")
        stored = sem("stored")
        zeroed = sem("zeroed")
        zero_ready = sem("zero_ready")
        shared_loaded = sem("shared_loaded")
        experts_loaded = sem("experts_loaded")
        gate_exp = sem("gate_exp")
        top_found = sem("top_found")
        gated_done = sem("gated_done")
        chosen_done = sem("chosen_done")
        ranked = sem("ranked")
        tail_full = sem("tail_full")
        tail_silu = sem("tail_silu")
        tail_hid = sem("tail_hid")
        tail_added = sem("tail_added")
        slots_done = sem("slots_done")
        owners_done = sem("owners_done")
        scattered = sem("scattered")
        tile_loaded = [sem(f"tile_loaded{i}") for i in range(2)]
        turned = sem("turned")
        turned_done = sem("turned_done")
        up_full = sem("up_full")
        hid_turned = sem("hid_turned")
        hidT_done = sem("hidT_done")
        silu_done = sem("silu_done")
        hid_done = sem("hid_done")
        down_full = sem("down_full")
        down_done = sem("down_done")
        routed_stored = [sem(f"routed_stored{i}") for i in range(2)]
        gathered = [sem(f"gathered{i}") for i in range(4)]
        final_var = sem("final_var")
        final_rstd = sem("final_rstd")
        final_done = sem("final_done")

        block = ctx.enter_context(nc.Block())

        NCONST = 13

        def by_half(part):
            return part.rearrange("p q h t -> p h q t")

        k_warm = identb[:].unsqueeze(1).to_broadcast([P, 4, P])
        WARM = {"norm": 14, "mean": 24, "var": 16, "project": 2, "turn": 2, "retake": 2, "logits": 2}

        def raw_q(pair):
            return raw[:, pair].rearrange("p h (q t) -> p h q t", q=QT)

        def prepare(eng, what, pair, rotated):
            X = raw[:, pair]
            both = [P, 2, T]
            if what == "cos":
                return eng.tensor_tensor(rotated[:, 0], X, cos[:].unsqueeze(1).to_broadcast(both), ALU.mult)
            if what == "sin":
                return eng.tensor_tensor(rotated[:, 1], X, sin[:].unsqueeze(1).to_broadcast(both), ALU.mult)
            if what == "even":
                return eng.tensor_tensor(X[:, 0], rotated[:, 0, 0], rotated[:, 1, 1], ALU.subtract)
            if what == "odd":
                return eng.tensor_tensor(X[:, 1], rotated[:, 1, 0], rotated[:, 0, 1], ALU.add)
            if what == "rest":
                return eng.tensor_tensor(raw_q(pair), raw_q(pair), by_half(parts[:, pair, 0]), ALU.subtract)
            return eng.tensor_tensor(by_half(parts[:, pair, 2]), raw_q(pair), by_half(parts[:, pair, 1]), ALU.subtract)

        START_POOL = [(what, 0) for what in ("cos", "sin", "even", "odd", "rest", "low")]
        START_DVE = ([(what, pair) for pair in (1, 2) for what in ("cos", "sin", "even", "odd")]
                     + [(what, pair) for what in ("rest", "low") for pair in (1, 2)])
        START_CASTS = (1, 0, 2)

        def started(op):
            of, steps = (start_pool, START_POOL) if op[1] == 0 else (start_dve, START_DVE)
            return of, steps.index(op) + 1

        def start_prepare(engine, eng, steps, sem, rotated):
            for what, pair in steps:
                if what == "cos":
                    engine.wait_ge(st_done, prep_slot(None, pair + 1))
                    if pair == 2:
                        engine.wait_ge(*started(("odd", 1)))
                elif what == "even":
                    engine.wait_ge(*started(("sin", pair)))
                elif what == "rest":
                    engine.wait_ge(start_high, START_CASTS.index(pair) + 1)
                elif what == "low":
                    engine.wait_ge(start_mid, START_CASTS.index(pair) + 1)
                prepare(eng, what, pair, rotated).then_inc(sem, 1)

        def st_at(b, k, prep):
            return ST_HEAD + b * ST_TURN + (ST_PREP if prep else 0) + k + 1

        def prep_slot(b, k):
            return k + 1 if b is None else ST_HEAD + b * ST_TURN + k + 1

        class Misc:

            def __init__(self):
                self.n, self.turns = 0, 0

            def next(self):
                self.n += 1
                return self.turns + self.n

            def turn(self, head, per, done):
                assert self.n in (head, head + per), (self.n, head, per)
                self.n, self.turns = head, done * per

        @block.sync
        def _(sp):
            def load_x(b):
                sp.dma_start(xin[:], x[b].rearrange("(n p) d -> p n d", p=P)).then_inc(x_loaded, 16)

            sp.dma_start(ident[:], ident_d).then_inc(ident_loaded, 16)
            load_x(0)
            sp.dma_start(wqk_sb[:], wqk.rearrange("(c p) a h m -> p c a h m", p=P)).then_inc(wqk_loaded, 16)
            sp.dma_start(cos[:], cos_d).then_inc(consts_loaded, 16)
            sp.dma_start(sin[:], sin_d).then_inc(consts_loaded, 16)
            sp.dma_start(mask_f[:], mask_d).then_inc(consts_loaded, 16)
            sp.dma_start(wv_sb[:], wv.rearrange("(c p) m -> p c m", p=P)).then_inc(consts_loaded, 16)
            sp.dma_start(wo_sb[:], wo.rearrange("(c p) m -> p c m", p=P)).then_inc(consts_loaded, 16)
            for i, v in enumerate(lams):
                sp.dma_start(lamv[:, i, :], v.unsqueeze(0).to_broadcast([P, DH])).then_inc(consts_loaded, 16)
            sp.dma_start(gw[:], gnw.unsqueeze(0).to_broadcast([P, T])).then_inc(consts_loaded, 16)
            sp.dma_start(gb[:], gnb.unsqueeze(0).to_broadcast([P, T])).then_inc(consts_loaded, 16)

            sp.dma_start(router_sb[:], router.rearrange("(c p) e -> p c e", p=P)).then_inc(consts_loaded, 16)
            sp.dma_start(counts[:], counts_d.unsqueeze(0).to_broadcast([P, E + NTOK + NROUTE])).then_inc(consts_loaded, 16)
            sp.dma_start(w_sh[:, 0:WUP].rearrange("p (c n) -> p c n", c=DC), s_up.rearrange("(c p) n -> p c n", p=P)).then_inc(shared_loaded, 16)
            sp.dma_start(w_sh[:, WUP:WEXP].rearrange("p (c n) -> p c n", c=F // P), s_down.rearrange("(c p) n -> p c n", p=P)).then_inc(shared_loaded, 16)
            sp.wait_ge(zero_ready, 1)
            sp.dma_start(sorted_rows.rearrange("(n p) d -> p n d", p=P), zero_row.unsqueeze(1).to_broadcast([P, NROUTE, D])).then_inc(zeroed, 16)

            def load_q(b, qt, used):
                if used is not None:
                    sp.wait_ge(st_full, used)
                sp.wait_ge(parts_written, (b + 1) * 3 * 16)
                for s in range(SLOTS):
                    sp.dma_start(q_stack[s * DH:(s + 1) * DH, qt].rearrange("p (a r) t -> p a r t", a=2),
                                 scratch[b, 0:2, QPART[s], qt].rearrange("a h (j r) t -> (h j) a r t", j=8)
                                 ).then_inc(q_loaded[qt], 16)

            def load_k(b):
                sp.wait_ge(parts_written, (b + 1) * 3 * 16)
                for s in range(SLOTS):
                    sp.dma_start(k_stack[s * DH:(s + 1) * DH],
                                 scratch[b, 2, KPART[s]].rearrange("q h (j r) t -> (h j) q r t", j=8)[:, :, 0:2 * KV, :]
                                 ).then_inc(k_loaded, 16)

            def load_near(b):
                sp.wait_ge(parts_written, (b + 1) * 3 * 16)
                for s in range(SLOTS):
                    sp.dma_start(k_near[s * DH:(s + 1) * DH],
                                 scratch[b, 2, KPART[s], 0:2].rearrange("q h (j r) t -> (h j) q r t", j=8)[:, :, 0:2 * KV, :]
                                 ).then_inc(near_loaded, 16)

            def max_rows(b, qt, fills):
                sp.wait_ge(misc_done, fills)
                sp.dma_start(mrows[b, qt], mT[:, qt % 2, :]).then_inc(max_stored, 16)
                sp.wait_ge(max_stored, (b * QT + qt + 1) * 16)
                sp.dma_start(q_stack[KROWS:MROWS, qt, :, :],
                             mrows[b, qt].rearrange("(m r) t -> m r t", m=2)).then_inc(max_loaded[qt], 16)

            def load_residual(b):
                sp.wait_ge(x2_done, BEGUN + b * QT)
                sp.dma_start(xres[:], x[b].rearrange("(n p) d -> p n d", p=P)).then_inc(xres_loaded, 16)

            def load_experts(first, end):
                for e in range(first, end):
                    w = w_exp[:, e * WEXP:(e + 1) * WEXP]
                    sp.dma_start(w[:, 0:WUP].rearrange("p (c n) -> p c n", c=DC), w_up[e].rearrange("(c p) n -> p c n", p=P)).then_inc(experts_loaded, 16)
                    sp.dma_start(w[:, WUP:WEXP].rearrange("p (c n) -> p c n", c=F // P), w_down[e].rearrange("(c p) n -> p c n", p=P)).then_inc(experts_loaded, 16)

            def store_gated(b):
                sp.wait_ge(gated_done, b + 1)
                sp.dma_start(gated_rows[b].rearrange("(n p) d -> p n d", p=P), gated_out[:]).then_inc(gated_stored, 16)

            def body(b, prep, post):
                if prep and post:
                    sp.wait_ge(st_full, prep_slot(b - 1, 0))
                    load_x(b + 1)
                if post:
                    sp.wait_ge(st_full, st_at(b - 1, NSTEP - 1, True))
                    load_k(b)
                    load_q(b, 3, None)
                if post:
                    load_residual(b - 1)
                max_rows(b, 2, turned_maxima(b, 2, 0))
                max_rows(b, 3, turned_maxima(b, 3, 0))
                if prep:
                    load_q(b + 1, 0, st_at(b, LAST_ST[0], prep))
                    sp.wait_ge(st_full, st_at(b, LAST_ST[1], prep))
                    load_near(b + 1)
                    load_q(b + 1, 1, None)
                    load_q(b + 1, 2, st_at(b, LAST_ST[2], prep))
                if not prep:
                    load_experts(0, 2)
                    sp.wait_ge(st_full, st_at(b, LAST_ST[1], prep))
                    load_experts(2, 4)
                if post:
                    store_gated(b - 1)
                if prep:
                    max_rows(b + 1, 0, turned_maxima(b, 0, -1))
                    max_rows(b + 1, 1, turned_maxima(b, 1, -1))

            load_near(0)
            load_q(0, 0, None)
            load_q(0, 1, None)
            load_k(0)
            load_q(0, 2, None)
            load_q(0, 3, None)
            sp.wait_ge(st_full, prep_slot(None, 0))
            load_x(1)
            max_rows(0, 0, misc_count(HEAD[:HEAD.index(("mt", 0, 0)) + 1]))
            max_rows(0, 1, misc_count(HEAD))
            body(0, True, False)
            with sp.Fori(1, B - 1) as b:
                body(b, True, True)
            body(B - 1, False, True)
            load_residual(B - 1)
            sp.wait_ge(pv_step, B * NSTEP)
            load_experts(4, E)
            sp.wait_ge(gated_stored, (BEGUN + B - 1) * 16)
            sp.wait_ge(centred, B)
            for b in range(B - 1):
                sp.dma_start(gated[b], gated_rows[b].rearrange("(n p) d -> p n d", p=P)).then_inc(gated_loaded, 16)

            def load_tile(i, pair, r):
                if not (isinstance(pair, int) and pair == 0):
                    sp.wait_ge(turned, i - 1)
                sp.dma_start(xe[:, r], sorted_rows[bass.ds(i * P, P), :]).then_inc(tile_loaded[r], 16)

            def store_routed(i, pair, r):
                sp.wait_ge(down_done, BEGUN + i + 1)
                sp.dma_start(routed_rows[bass.ds(i * P, P), :], yo[:, r]).then_inc(routed_stored[r], 16)

            def routed_turn(k, r):
                i = 2 * k + r
                if not (isinstance(i, int) and i + 2 >= NROUTE):
                    load_tile(i + 2, k + 1, r)
                store_routed(i, k, r)

            sp.wait_ge(scattered, NTOK * 16)
            for r in range(2):
                load_tile(r, 0, r)
            with sp.Fori(0, LOOPED) as k:
                for r in range(2):
                    routed_turn(k, r)
            for i in range(2 * LOOPED, NROUTE):
                routed_turn(i // 2, i % 2)

            for g in range(4):
                sp.wait_ge(final_done, g + 1)
                sp.dma_start(out[g].rearrange("(n p) d -> p n d", p=P), x2[:, g * 4:(g + 1) * 4]).then_inc(stored, 16)
            sp.wait_ge(stored, 4 * 16)

        @block.tensor
        def _(pe):
            m = Misc()
            bank = Misc()

            def prep(b):
                nb = 0 if b is None else b + 1
                pe.wait_ge(x_loaded, (nb + 1) * 16)
                for k in range(4):
                    v = prep_slot(b, k)
                    if not (b is None and k < 2):
                        pe.wait_ge(st_done, v - 2)
                    slot = st_ps[:, k % 2]
                    if k == 0:
                        for c in range(DC):
                            for t in range(QT):
                                last = nc.tensor.transpose(slot[:, c, t * P:(t + 1) * P], xin[:, t, c * P:(c + 1) * P], ident[:])
                    else:
                        if k == 1:
                            pe.wait_ge(st_done, prep_slot(b, 0))
                            if b is None:
                                pe.wait_ge(wqk_loaded, 16)
                        for half in range(2):
                            for c in range(DC):
                                last = nc.tensor.matmul(slot[:, half, :], wqk_sb[:, c, k - 1, half, :], xT[:, c, :],
                                                        start=(c == 0), stop=(c == DC - 1))
                    last.then_inc(st_full, 1)

            def score_bank(b, qt, i):
                v = bank.next()
                if not (isinstance(v, int) and v <= 2):
                    pe.wait_ge(bank_done, v - 2)
                rows = banks(qt)[i]
                w = (qt + 1) * P
                keys = k_near if qt < 2 else k_stack
                for n, hs in enumerate(rows):
                    gs = hs // 4
                    o = s_ps[:, (i % 2), n * w:(n + 1) * w]
                    nc.tensor.matmul(o, q_stack[0:KROWS, qt, hs, :], keys[0:KROWS, 0:qt + 1, gs, :], start=True, stop=False)
                    last = nc.tensor.matmul(o[:, w - P:w], identb[:], mask[:], start=False, stop=True)
                last.then_inc(bank_full, 1)

            def await_stacks(b, qt):
                pe.wait_ge(q_loaded[qt], (b + 1) * SLOTS * 16)
                if qt == 0:
                    pe.wait_ge(near_loaded, (b + 1) * SLOTS * 16)
                if qt == 2:
                    pe.wait_ge(k_loaded, (b + 1) * SLOTS * 16)

            def task(name, arg, b):
                if name == "banks":
                    qt, lo, hi = arg
                    await_stacks(b, qt)
                    for i in range(lo, hi):
                        score_bank(b, qt, i)
                if name not in MISC_TASKS:
                    return
                v = m.next()
                if not (isinstance(v, int) and v == 1):
                    pe.wait_ge(misc_done, v - 1)
                if name == "v":
                    for t in range(QT):
                        for c in range(DC):
                            last = nc.tensor.matmul(misc[:, t * P:(t + 1) * P], xT[:, c, t * P:(t + 1) * P], wv_sb[:, c, :],
                                                    start=(c == 0), stop=(c == DC - 1))
                elif name == "mt":
                    pe.wait_ge(split_done, b * QT + arg + 1)
                    last = nc.tensor.transpose(misc[:, 0:P // 2].bitcast(BF16), msplit[:, arg % 2, :], identb[:])
                elif name == "norm":
                    pe.wait_ge(pv_done, b * NUNIT + arg + 1)
                    for r in range(4):
                        last = nc.tensor.transpose(misc[:, r * P:(r + 1) * P], ol[:, arg % 2, r * P:(r + 1) * P], ident[:])
                elif name == "mean":
                    pe.wait_ge(summed, b + 1)
                    last = nc.tensor.matmul(misc[:, 0:H], averager[:], head_tot[:], start=True, stop=True)
                elif name == "var":
                    pe.wait_ge(squares_summed, b + 1)
                    last = nc.tensor.matmul(misc[:, 0:H], averager[:], head_sq[:], start=True, stop=True)
                elif name == "turn":
                    pe.wait_ge(scaled, b * QT + arg + 1)
                    for r in range(4):
                        last = nc.tensor.transpose(misc[:, r * P:(r + 1) * P], dev[:, arg].rearrange("p h d -> p (h d)")[:, r * P:(r + 1) * P], ident[:])
                elif name == "project":
                    for r in range(4):
                        last = nc.tensor.matmul(misc[:, 0:D], zT[:, r, :], wo_sb[:, r, :], start=(r == 0), stop=(r == 3))
                elif name == "retake":
                    pe.wait_ge(x2_done, BEGUN + b * QT + arg + 1)
                    for ch in range(DC):
                        last = nc.tensor.transpose(misc[:, ch * P:(ch + 1) * P], y[:, arg % 2, ch * P:(ch + 1) * P], ident[:])
                elif name == "logits":
                    for ch in range(DC):
                        last = nc.tensor.matmul(misc[:, 0:E], x2T[:, ch, arg * P:(arg + 1) * P], router_sb[:, ch, :],
                                                start=(ch == 0), stop=(ch == DC - 1))
                elif name in ("shared_gate", "shared_up"):
                    at = (F if name == "shared_up" else 0) + arg * P
                    for ch in range(DC):
                        last = nc.tensor.matmul(misc[:], w_sh[:, ch * 2 * F + at:ch * 2 * F + at + P], x2T[:, ch, :],
                                                start=(ch == 0), stop=(ch == DC - 1))
                elif name == "shared_down":
                    for fc in range(F // P):
                        last = nc.tensor.matmul(misc[:, 0:D], shared_hidT[:, fc, arg * P:(arg + 1) * P], w_sh[:, WUP + fc * D:WUP + (fc + 1) * D],
                                                start=(fc == 0), stop=(fc == F // P - 1))
                last.then_inc(misc_full, 1)

            def scores(b, n, prep):
                qt, g, kt = STEPS[n]
                v = st_at(b, n, prep)
                if n == FIRST_ST[qt]:
                    pe.wait_ge(max_loaded[qt], (b + 1) * 16)
                pe.wait_ge(st_done, v - 2)
                for s in range(2):
                    gs = 2 * g + s
                    last = nc.tensor.matmul(st_ps[:, n % 2, s, :], (k_near if qt < 2 else k_stack)[0:MROWS, kt, gs, :],
                                            q_stack[0:MROWS, qt, gs * 4:gs * 4 + 4, :], start=True, stop=True)
                last.then_inc(st_full, 1)

            def weigh(b, n, prep):
                qt, g, kt = STEPS[n]
                u = qt * KV + g
                if kt == qt:
                    pe.wait_ge(diag_done, b * NUNIT + DIAG.index(n) + 1)
                else:
                    pe.wait_ge(st_done, st_at(b, n, prep))
                if kt == 0:
                    if u > 0:
                        pe.wait_ge(pv_done, b * NUNIT + u)
                for s in range(2):
                    last = nc.tensor.matmul(pv_ps[s * 64:(s + 1) * 64, :], (vo, vo_lam)[s][:, kt, g, :], probs[:, n % NP, s, :],
                                            start=(kt == 0), stop=(kt == qt))
                last.then_inc(pv_step, 1)

            def keep_warm(count):
                for _ in range(count):
                    nc.tensor.matmul(s_ps[:, 0, :], identb[:], k_warm, start=True, stop=True)

            def body(b, prep_next, post):
                if prep_next:
                    prep(b)
                scores(b, 0, prep_next)
                scores(b, 1, prep_next)
                for n in range(NSTEP):
                    if n + 2 < NSTEP:
                        scores(b, n + 2, prep_next)
                    now = [x for x in BANKS_AT.get(n, []) if x[2] == 0 or prep_next]
                    for part in (0, 1):
                        if part == 1 and n > 0:
                            weigh(b, n - 1, prep_next)
                        for qt, i, back in (now[:len(now) // 2], now[len(now) // 2:])[part]:
                            if i == 0:
                                await_stacks(b - back, qt)
                            score_bank(b - back, qt, i)
                    for name, arg, back in tasks_at(n, prep_next, post):
                        task(name, arg, b - back)
                weigh(b, NSTEP - 1, prep_next)

            def boundary(b):
                for name, arg, back in BOUNDARY:
                    task(name, arg, b - back)

            pe.wait_ge(ident_loaded, 16)
            prep(None)
            pe.wait_ge(consts_loaded, NCONST * 16)
            pe.wait_ge(consts_ready, 2)
            for name, arg, _ in HEAD:
                task(name, arg, 0)
            body(0, True, False)
            with pe.Fori(1, B - 1) as b:
                m.turn(MISC_HEAD, MISC_TURN, b - 1)
                bank.turn(BANK_HEAD, BANK_TURN, b - 1)
                boundary(b)
                body(b, True, True)
            m.turn(MISC_HEAD, MISC_TURN, B - 2)
            bank.turn(BANK_HEAD, BANK_TURN, B - 2)
            boundary(B - 1)
            body(B - 1, False, True)
            for name, arg, _ in TAIL:
                task(name, arg, B - 1)
                keep_warm(WARM.get(name, 0))

            pe.wait_ge(misc_done, m.turns + m.n)
            pe.wait_ge(chosen_done, 1)
            nc.tensor.matmul(misc[:, 0:NTOK * E], before[:], chosenb[:], start=True, stop=True)
            nc.tensor.matmul(misc[:, NTOK * E:2 * NTOK * E], onesb[:], chosenb[:], start=True, stop=True).then_inc(ranked, 1)
            for fc in range(F // P):
                for half, done in ((0, tail_silu), (1, tail_hid)):
                    if fc > 0:
                        pe.wait_ge(done, fc)
                    for ch in range(DC):
                        at = ch * 2 * F + half * F + fc * P
                        last = nc.tensor.matmul(s_ps[:, half], w_sh[:, at:at + P], x2T[:, ch, :], start=(ch == 0), stop=(ch == DC - 1))
                    last.then_inc(tail_full, 1)
            pe.wait_ge(tail_silu, F // P)
            pe.wait_ge(tail_hid, F // P)
            for t in range(QT):
                if t >= 2:
                    pe.wait_ge(tail_added, t - 1)
                for fc in range(F // P):
                    last = nc.tensor.matmul(s_ps[:, t % 2, 0:D], shared_hidT[:, fc, t * P:(t + 1) * P],
                                            w_sh[:, WUP + fc * D:WUP + (fc + 1) * D], start=(fc == 0), stop=(fc == F // P - 1))
                last.then_inc(tail_full, 1)
            pe.wait_ge(tail_added, QT)

            def turn_tile(pair, r):
                i = 2 * pair + r
                pe.wait_ge(tile_loaded[r], (pair + 1) * 16)
                if not (isinstance(i, int) and i == 0):
                    pe.wait_ge(turned_done, i)
                for ch in range(DC):
                    last = nc.tensor.transpose(s_ps[:, 0, ch * P:(ch + 1) * P], xe[:, r, ch * P:(ch + 1) * P], ident[:])
                last.then_inc(turned, 1)

            def up(pair, r, e):
                i = 2 * pair + r
                pe.wait_ge(turned_done, i + 1)
                if not (isinstance(i, int) and i < 2):
                    pe.wait_ge(hid_done, BEGUN + i - 1)
                for half in range(2):
                    for ch in range(DC):
                        w = w_exp[:, bass.ds(e * WEXP + ch * 2 * F + half * F, F)]
                        last = nc.tensor.matmul(st_ps[:, r, half, :], xeT[:, r, ch, :], w, start=(ch == 0), stop=(ch == DC - 1))
                last.then_inc(up_full, 1)

            def turn_hidden(pair, r):
                i = 2 * pair + r
                pe.wait_ge(hid_done, BEGUN + i + 1)
                if not (isinstance(i, int) and i == 0):
                    pe.wait_ge(hidT_done, BEGUN + i)
                for ch in range(F // P):
                    last = nc.tensor.transpose(s_ps[:, 1, ch * P:(ch + 1) * P], hid[:, r, ch * P:(ch + 1) * P], ident[:])
                last.then_inc(hid_turned, 1)

            def down(pair, r, e):
                i = 2 * pair + r
                pe.wait_ge(hidT_done, BEGUN + i + 1)
                if not (isinstance(i, int) and i < 1):
                    pe.wait_ge(down_done, BEGUN + i)
                for fc in range(F // P):
                    w = w_exp[:, bass.ds(e * WEXP + WUP + fc * D, D)]
                    last = nc.tensor.matmul(pv_ps[:, 0:D], hidT[:, r, fc, :], w, start=(fc == 0), stop=(fc == F // P - 1))
                last.then_inc(down_full, 1)

            def owner_of(i):
                return pe.value_load(owner[0:1, bass.ds(i, 1)], min_val=0, max_val=E - 1)

            pe.wait_ge(owners_done, 1)
            pe.wait_ge(experts_loaded, 2 * E * 16)
            turn_tile(0, 0)
            up(0, 0, owner_of(0))
            turn_tile(0, 1)

            def routed_turn(k, r):
                i = 2 * k + r
                static = isinstance(i, int)
                turn_hidden(k, r)
                if not (static and i + 1 >= NROUTE):
                    up(k + r, 1 - r, owner_of(i + 1))
                if not (static and i + 2 >= NROUTE):
                    turn_tile(k + 1, r)
                down(k, r, owner_of(i))

            with pe.Fori(0, LOOPED) as k:
                for r in range(2):
                    routed_turn(k, r)
            for i in range(2 * LOOPED, NROUTE):
                routed_turn(i // 2, i % 2)

        @block.scalar
        def _(act):
            m = Misc()

            def evacuate(b, k):
                act.wait_ge(st_full, prep_slot(b, k))
                if k == 0:
                    nc.scalar.copy(xT[:], st_ps[:, 0]).then_inc(st_done, 1)
                else:
                    nc.scalar.copy(raw[:, k - 1], st_ps[:, k % 2]).then_inc(st_done, 1)

            def cast(nb, part, pair):
                if part == 0:
                    act.wait_ge(parts_written, nb * 3 * 16)
                    act.wait_ge(prep_done, (nb - 1) * NPREP + PREP_DONE[("odd", pair)])
                    nc.scalar.copy(by_half(parts[:, pair, 0]), raw_q(pair)).then_inc(high_done, 1)
                else:
                    act.wait_ge(prep_done, (nb - 1) * NPREP + PREP_DONE[("rest", pair)])
                    nc.scalar.copy(by_half(parts[:, pair, 1]), raw_q(pair)).then_inc(mid_done, 1)

            def write_parts(nb, pair):
                act.wait_ge(prep_done, (nb - 1) * NPREP + PREP_DONE[("low", pair)])
                store_parts(nb, pair)

            def store_parts(nb, pair):
                act.dma_start(scratch[nb, pair].rearrange("s q h r t -> r (s q h) t"),
                              parts[:, pair].rearrange("p s q h t -> p (s q h) t")).then_inc(parts_written, 16)

            casts_at = {}
            for pair in range(3):
                for what, part, step in (("cast", 0, PREP_AT[("odd", pair)] + 2), ("cast", 1, PREP_AT[("rest", pair)] + 2),
                                         ("write", 0, PREP_AT[("low", pair)] + 3)):
                    casts_at.setdefault(PREP_FROM + step, []).append((what, part, pair))

            def task(name, arg, b):
                if name == "square":
                    act.wait_ge(centred, b + 1)
                    if not (isinstance(b, int) and b == 0):
                        act.wait_ge(gated_stored, (BEGUN + b) * 16)
                    nc.scalar.activation(sq[:], dev[:], ACT.Square).then_inc(squared, 1)
                if name == "top":
                    act.wait_ge(top_found, b + 1)
                    nc.scalar.activation(gate[:, 0], top_now[:], ACT.Exp, scale=-1.0).then_inc(gate_exp, 1)
                if name not in MISC_TASKS:
                    return
                v = m.next()
                if name == "shared_gate":
                    if arg == 0:
                        act.wait_ge(gated_done, b + 1)
                    act.wait_ge(misc_full, v)
                    nc.scalar.activation(shared_silu, misc[:], ACT.Silu).then_inc(misc_done, 1)
                if name == "v":
                    act.wait_ge(misc_full, v)
                    if isinstance(b, int) and b == 0:
                        act.wait_ge(lam_ready, 1)
                    values = misc[:].rearrange("p (t g d) -> p t g d", t=QT, g=KV)
                    nc.scalar.copy(vo[:, :, :, 0:DV], values)
                    nc.scalar.activation(vo_lam[:, :, :, 0:DV], values, ACT.Copy, scale=neglam[:]).then_inc(misc_done, 1)
                elif name == "turn":
                    act.wait_ge(misc_full, v)
                    nc.scalar.copy(zT[:], misc[:].rearrange("p (r t) -> p r t", r=4)).then_inc(misc_done, 1)
                elif name == "retake":
                    act.wait_ge(misc_full, v)
                    nc.scalar.copy(x2T[:, :, arg * P:(arg + 1) * P], misc[:, 0:D].rearrange("p (c t) -> p c t", c=DC)).then_inc(misc_done, 1)

            def body(b, prep, post):
                if prep:
                    for k in range(4):
                        evacuate(b, k)
                for n in range(NSTEP):
                    qt, g, kt = STEPS[n]
                    v = st_at(b, n, prep)
                    act.wait_ge(st_full, v)
                    if n >= NP or (isinstance(b, int) and b > 0):
                        act.wait_ge(pv_step, b * NSTEP + n + 1 - NP)
                    nc.scalar.activation(probs[:, n % NP], st_ps[:, n % 2], ACT.Exp, scale=float(DH) ** -0.5).then_inc(st_done, 1)
                    if n >= 2:
                        finish_unit(b, n - 2)
                    for name, arg, back in tasks_at(n - 1, prep, post) if n else []:
                        task(name, arg, b - back)
                    for what, part, pair in casts_at.get(n, []) if prep else []:
                        if what == "cast":
                            cast(b + 1, part, pair)
                        else:
                            write_parts(b + 1, pair)
                for name, arg, back in tasks_at(NSTEP - 1, prep, post):
                    task(name, arg, b - back)
                finish_unit(b, NSTEP - 1)

            def finish_unit(b, n):
                qt, g, kt = STEPS[n]
                if kt != qt:
                    return
                u = qt * KV + g
                act.wait_ge(pv_step, b * NSTEP + n + 1)
                nc.scalar.copy(ol[:, u % 2], pv_ps[:]).then_inc(pv_done, 1)

            act.wait_ge(lam_summed, 1)
            nc.scalar.activation(lame[:], lams2[:], ACT.Exp).then_inc(lam_exp, 1)
            for k in range(4):
                evacuate(None, k)
            for part, before_it, done in ((0, "odd", start_high), (1, "rest", start_mid)):
                for pair in START_CASTS:
                    act.wait_ge(*started((before_it, pair)))
                    nc.scalar.copy(by_half(parts[:, pair, part]), raw_q(pair)).then_inc(done, 1)
            for pair in START_CASTS:
                act.wait_ge(*started(("low", pair)))
                store_parts(0, pair)
            for name, arg, _ in HEAD:
                task(name, arg, 0)

            def boundary(b):
                for name, arg, back in BOUNDARY:
                    task(name, arg, b - back)

            body(0, True, False)
            with act.Fori(1, B - 1) as b:
                m.turn(MISC_HEAD, MISC_TURN, b - 1)
                boundary(b)
                body(b, True, True)
            m.turn(MISC_HEAD, MISC_TURN, B - 2)
            boundary(B - 1)
            body(B - 1, False, True)
            for name, arg, _ in TAIL:
                task(name, arg, B - 1)

            for fc in range(F // P):
                act.wait_ge(tail_full, 2 * fc + 1)
                if fc >= 2:
                    act.wait_ge(tail_hid, fc - 1)
                nc.scalar.activation(tail_silus[:, fc % 2], s_ps[:, 0], ACT.Silu).then_inc(tail_silu, 1)

            def take_tile(pair, r):
                act.wait_ge(turned, 2 * pair + r + 1)
                nc.scalar.copy(xeT[:, r], s_ps[:, 0, 0:D].rearrange("p (c t) -> p c t", c=DC)).then_inc(turned_done, 1)

            def make_silu(pair, r):
                act.wait_ge(up_full, 2 * pair + r + 1)
                nc.scalar.activation(silu[:, r], st_ps[:, r, 0, :], ACT.Silu).then_inc(silu_done, 1)

            def take_hidden(pair, r):
                act.wait_ge(hid_turned, 2 * pair + r + 1)
                nc.scalar.copy(hidT[:, r], s_ps[:, 1].rearrange("p (c t) -> p c t", c=F // P)).then_inc(hidT_done, 1)

            take_tile(0, 0)
            make_silu(0, 0)
            take_tile(0, 1)

            def routed_turn(k, r):
                i = 2 * k + r
                static = isinstance(i, int)
                take_hidden(k, r)
                if not (static and i + 1 >= NROUTE):
                    make_silu(k + r, 1 - r)
                if not (static and i + 2 >= NROUTE):
                    take_tile(k + 1, r)

            with act.Fori(0, LOOPED) as k:
                for r in range(2):
                    routed_turn(k, r)
            for i in range(2 * LOOPED, NROUTE):
                routed_turn(i // 2, i % 2)

        @block.gpsimd
        def _(pool):
            c = Chain(pool, pool_chain)

            def prep(b, op):
                what, pair = op
                base = (b - 1) * NPREP
                if what == "cos":
                    pool.wait_ge(st_done, prep_slot(b - 1, pair + 1))
                    if pair > 0:
                        pool.wait_ge(prep_done, base + PREP_DONE[("odd", pair - 1)])
                    elif not isinstance(b, int):
                        pool.wait_ge(prep_done, base)
                elif what == "even":
                    pool.wait_ge(prep_done, base + PREP_DONE[("sin", pair)])
                elif what == "rest":
                    pool.wait_ge(high_done, (b - 1) * 3 + pair + 1)
                elif what == "low":
                    pool.wait_ge(mid_done, (b - 1) * 3 + pair + 1)
                ins = prepare(nc.gpsimd, what, pair, rot)
                ins.then_inc(prep_done, 1)

            def task(name, arg, b):
                if name == "var":
                    pool.wait_ge(att_var, b + 1)
                    c.link(nc.gpsimd.tensor_tensor(head_rstd[:], head_var[:], halfneg[:].to_broadcast([P, H]), ALU.pow))
                    c.link(nc.gpsimd.tensor_tensor(scale_row[:], gw[:].rearrange("p (h d) -> p h d", h=H),
                                                   head_rstd[:].unsqueeze(2).to_broadcast([P, H, DV]), ALU.mult))
                    pool.sem_inc(scale_ready, 1)
                elif name == "affine":
                    z = dev[:, arg].rearrange("p h d -> p (h d)")
                    c.link(nc.gpsimd.tensor_tensor(z, z, scale_row[:].rearrange("p h d -> p (h d)"), ALU.mult))
                    nc.gpsimd.tensor_tensor(z, z, gb[:], ALU.add).then_inc(scaled, 1)
                elif name == "project":
                    pool.wait_ge(y_var, b * QT + arg + 1)
                    nc.gpsimd.tensor_tensor(rstd[:, arg % 2:arg % 2 + 1], mv[:, arg % 2, 1:2], halfneg[:], ALU.pow).then_inc(y_rstd, 1)

            def body(b, prep_next, post):
                for n in range(NSTEP):
                    qt, g, kt = STEPS[n]
                    if kt == qt:
                        pool.wait_ge(st_done, st_at(b, n, prep_next))
                        pool.sem_inc(exps_taken, 1)
                        e = probs[:, n % NP].rearrange("p s (r q) -> p (s r) q", r=4)
                        nc.gpsimd.affine_select(out=e, in_=e, compare_op=ALU.is_ge, fill=0.0, base=0,
                                                pattern=[[0, 8], [1, P]], channel_multiplier=-1).then_inc(diag_done, 1)
                    if n >= 1:
                        for name, arg, back in tasks_at(n - 1, prep_next, post):
                            task(name, arg, b - back)
                    if prep_next and 0 <= n - PREP_FROM < NPREP:
                        prep(b + 1, PREP[n - PREP_FROM])
                for name, arg, back in tasks_at(NSTEP - 1, prep_next, post):
                    task(name, arg, b - back)

            c.link(nc.gpsimd.memset(halfneg[:], -0.5))
            pool.wait_ge(consts_loaded, NCONST * 16)
            c.link(nc.gpsimd.tensor_scalar(gw[:], gw[:], 1.0 - LAMBDA_INIT, None, ALU.mult))
            c.link(nc.gpsimd.tensor_scalar(gb[:], gb[:], 1.0 - LAMBDA_INIT, None, ALU.mult))
            start_prepare(pool, nc.gpsimd, START_POOL, start_pool, rot)
            body(0, True, False)
            head = c.n
            with pool.Fori(1, B - 1) as b:
                c.turn(head, POOL_TURN, b - 1)
                body(b, True, True)
            c.turn(head, POOL_TURN, B - 2)
            body(B - 1, False, True)
            for name, arg, _ in TAIL:
                if name != "affine":
                    task(name, arg, B - 1)

            pool.wait_ge(zeroed, 16)
            pool.wait_ge(slots_done, 1)
            pool.wait_ge(gated_loaded, (B - 1) * 16)
            pool.wait_ge(gated_done, B)
            for t in range(NTOK):
                nc.gpsimd.indirect_dma_start(out=sorted_rows, out_offset=bass.IndirectOffsetOnAxis(ap=slot[:, t:t + 1], axis=0),
                                             in_=gated[t // QT][:, t % QT], in_offset=None).then_inc(scattered, 16)
            for r in range(2):
                pool.wait_ge(routed_stored[r], (BEGUN + (NROUTE + 1 - r) // 2) * 16)
            for t in range(NTOK):
                nc.gpsimd.indirect_dma_start(out=gated[t // QT][:, t % QT], out_offset=None, in_=routed_rows,
                                             in_offset=bass.IndirectOffsetOnAxis(ap=slot[:, t:t + 1], axis=0)).then_inc(gathered[t // 4], 16)
            for g in range(4):
                pool.wait_ge(final_var, g + 1)
                nc.gpsimd.tensor_tensor(rstdf[:, g * 4:(g + 1) * 4], mvf[:, g * 4:(g + 1) * 4, 1], halfneg[:].to_broadcast([P, 4]),
                                        ALU.pow).then_inc(final_rstd, 1)

        @block.vector
        def _(dve):
            c = Chain(dve, dve_chain)
            m = Misc()
            bank = Misc()

            def maximum(qt, i):
                v = bank.next()
                rows = banks(qt)[i]
                dve.wait_ge(bank_full, v)
                w = (qt + 1) * P
                nc.vector.tensor_reduce(out=mneg[:, qt, rows[0]:rows[-1] + 1],
                                        in_=s_ps[:, i % 2, 0:len(rows) * w].rearrange("p (r k) -> p r k", r=len(rows)),
                                        axis=AX.X, op=ALU.max, negate=True).then_inc(bank_done, 1)
                if i == NBANK[qt] - 1:
                    dve.wait_ge(bank_done, v)
                    c.link(nc.vector.tensor_copy(msplit[:, qt % 2, 0:HS], mneg[:, qt]))
                    nc.vector.tensor_tensor(msplit[:, qt % 2, HS:2 * HS], mneg[:, qt], msplit[:, qt % 2, 0:HS],
                                            ALU.subtract).then_inc(split_done, 1)

            def task(name, arg, b, ahead=False, last_batch=False):
                if name == "banks":
                    for i in range(arg[1], arg[2]):
                        maximum(arg[0], i)
                if name in MISC_TASKS:
                    v = m.next()
                if name == "mt":
                    dve.wait_ge(misc_full, v)
                    if not (isinstance(b, int) and b == 0 and arg < 2):
                        dve.wait_ge(max_stored, (b * QT + arg - 1) * 16)
                    nc.vector.tensor_copy(mT[:, arg % 2, :], misc[0:2 * HS, 0:P // 2].bitcast(BF16)).then_inc(misc_done, 1)
                elif name == "norm":
                    qt, g = divmod(arg, KV)
                    dve.wait_ge(misc_full, v)
                    t = misc[:].rearrange("p (r s d) -> p r s d", r=4, s=2)
                    c.link(nc.vector.reciprocal(rl[:], t[:, :, :, DV]))
                    nc.vector.tensor_tensor(o12[:], t[:, :, :, 0:DV], rl[:].unsqueeze(3).to_broadcast([P, 4, 2, DV]), ALU.mult).then_inc(misc_done, 1)
                    dve.wait_ge(misc_done, v)
                    c.link(nc.vector.tensor_tensor(att[:, qt, g * 4:g * 4 + 4, :], o12[:, :, 0], o12[:, :, 1], ALU.add))
                elif name == "mean":
                    nc.vector.tensor_reduce(out=head_tot[:], in_=att[:].rearrange("p q h d -> p h q d"), axis=AX.XY,
                                            op=ALU.add).then_inc(summed, 1)
                    dve.wait_ge(misc_full, v)
                    mean = misc[:, 0:H].unsqueeze(2).to_broadcast([P, H, DV])
                    for qt in range(QT):
                        ins = nc.vector.tensor_tensor(dev[:, qt], att[:, qt], mean, ALU.subtract)
                        if qt == QT - 2:
                            c.link(ins)
                        if qt == QT - 1:
                            ins.then_inc(misc_done, 1)
                    dve.wait_ge(misc_done, v)
                    dve.sem_inc(centred, 1)
                elif name == "var":
                    dve.wait_ge(squared, b + 1)
                    nc.vector.tensor_reduce(out=head_sq[:], in_=sq[:].rearrange("p q h d -> p h q d"), axis=AX.XY,
                                            op=ALU.add).then_inc(squares_summed, 1)
                    dve.wait_ge(misc_full, v)
                    nc.vector.tensor_scalar(head_var[:], misc[:, 0:H], EPS, None, ALU.add).then_inc(misc_done, 1)
                    dve.wait_ge(misc_done, v)
                    dve.sem_inc(att_var, 1)
                elif name == "project":
                    dve.wait_ge(misc_full, v)
                    if arg == 0:
                        dve.wait_ge(xres_loaded, (b + 1) * 16)
                    nc.vector.tensor_tensor(y[:, arg % 2], misc[:, 0:D], xres[:, arg], ALU.add).then_inc(misc_done, 1)
                    dve.wait_ge(misc_done, v)
                    c.link(nc.vector.bn_stats(st6[:], y[:, arg % 2]))
                    dve.sem_inc(stats_taken, 1)
                    c.link(nc.vector.bn_aggr(mv[:, arg % 2], st6[:]))
                    nc.vector.tensor_scalar(mv[:, arg % 2, 1:2], mv[:, arg % 2, 1:2], EPS, None, ALU.add).then_inc(y_var, 1)
                elif name == "x2":
                    dve.wait_ge(y_rstd, b * QT + arg + 1)
                    nc.vector.tensor_scalar(x2[:, bass.ds(b * QT + arg, 1), :], y[:, arg % 2:arg % 2 + 1], mv[:, arg % 2, 0:1],
                                            rstd[:, arg % 2:arg % 2 + 1], ALU.subtract, ALU.mult).then_inc(x2_kept, 1)
                    dve.wait_ge(x2_kept, b * QT + arg + 1)
                    nc.vector.tensor_scalar(y[:, arg % 2], y[:, arg % 2], mv[:, arg % 2, 0:1],
                                            rstd[:, arg % 2:arg % 2 + 1], ALU.subtract, ALU.mult).then_inc(x2_done, 1)
                elif name == "logits":
                    dve.wait_ge(misc_full, v)
                    nc.vector.tensor_copy(logits_now[:, arg], misc[:, 0:E])
                    nc.vector.tensor_copy(logits[:, bass.ds(b * QT + arg, 1), :], misc[:, 0:E].unsqueeze(1)).then_inc(misc_done, 1)
                elif name == "affine" and last_batch:
                    if arg == 0:
                        dve.wait_ge(scale_ready, B)
                    z = dev[:, arg].rearrange("p h d -> p (h d)")
                    c.link(nc.vector.tensor_tensor(z, z, scale_row[:].rearrange("p h d -> p (h d)"), ALU.mult))
                    nc.vector.tensor_tensor(z, z, gb[:], ALU.add).then_inc(scaled, 1)
                elif name == "shared_up":
                    dve.wait_ge(misc_full, v)
                    nc.vector.tensor_tensor(shared_hidT[:, arg], shared_silu, misc[:], ALU.mult).then_inc(misc_done, 1)
                elif name == "shared_down":
                    dve.wait_ge(misc_full, v)
                    rows = x2[:, bass.ds(b * QT + arg, 1), :]
                    nc.vector.tensor_tensor(rows, rows, misc[:, 0:D].unsqueeze(1), ALU.add).then_inc(misc_done, 1)
                elif name == "top":
                    dve.wait_ge(misc_done, m.turns + m.n)
                    nc.vector.tensor_reduce(out=top_now[:], in_=logits_now[:], axis=AX.X, op=ALU.max).then_inc(top_found, 1)
                elif name == "gate":
                    dve.wait_ge(gate_exp, b + 1)
                    c.link(nc.vector.tensor_scalar(gate[:, 0], gate[:, 0], 1.0, None, ALU.add))
                    c.link(nc.vector.reciprocal(gate[:, 1], gate[:, 0]))
                    if ahead:
                        dve.wait_ge(prep_done, (b + 2) * NPREP)
                    nc.vector.tensor_tensor(gated_out[:], x2[:, bass.ds(b * QT, QT), :], gate[:, 1].unsqueeze(2).to_broadcast([P, QT, D]),
                                            ALU.mult).then_inc(gated_done, 1)

            def body(b, ahead, post):
                for n in range(NSTEP):
                    for qt, i, back in BANKS_AT.get(n, []):
                        if back == 0 or ahead:
                            maximum(qt, i)
                    for name, arg, back in tasks_at(n, ahead, post):
                        task(name, arg, b - back, ahead)

            def boundary(b):
                for name, arg, back in BOUNDARY:
                    task(name, arg, b - back)

            for begun in (x2_done, hid_done, hidT_done, down_done):
                dve.sem_inc(begun, BEGUN)
            for begun in [gated_stored] + routed_stored:
                dve.sem_inc(begun, BEGUN * 16)
            nc.vector.memset(zero_row, 0.0).then_inc(zero_ready, 1)
            c.link(nc.vector.memset(onesb[:], 1.0))
            c.link(nc.vector.memset(msplit[:, :, 2 * HS:P], 0.0))
            c.link(nc.vector.memset(averager[:], 1.0 / (T * DV)))
            c.link(nc.vector.memset(vo[:, :, :, DV:2 * DV], 1.0))
            c.link(nc.vector.memset(vo_lam[:, :, :, DV:2 * DV], 1.0))
            c.link(nc.vector.memset(k_stack[KROWS:P], 1.0))
            c.link(nc.vector.memset(k_near[KROWS:P], 1.0))
            dve.wait_ge(consts_loaded, NCONST * 16)
            nc.vector.tensor_copy(identb[:], ident[:]).then_inc(consts_ready, 1)
            nc.vector.tensor_copy(mask[:], mask_f[:]).then_inc(consts_ready, 1)
            c.link(nc.vector.tensor_scalar(before[:], mask_f[:], 0.0, None, ALU.is_lt))
            c.link(nc.vector.tensor_tensor(lamp[:], lamv[:, 0:4:2, :], lamv[:, 1:4:2, :], ALU.mult))
            nc.vector.tensor_reduce(out=lams2[:], in_=lamp[:], axis=AX.X, op=ALU.add).then_inc(lam_summed, 1)
            dve.wait_ge(lam_exp, 1)
            c.link(nc.vector.tensor_tensor(neglam[:], lame[:, 1:2], lame[:, 0:1], ALU.subtract))
            nc.vector.tensor_scalar(neglam[:], neglam[:], -LAMBDA_INIT, None, ALU.add).then_inc(lam_ready, 1)
            start_prepare(dve, nc.vector, START_DVE, start_dve, att[:].rearrange("p q h d -> p (q h d)").rearrange("p (a h t) -> p a h t", a=2, h=2))
            for name, arg, _ in HEAD:
                task(name, arg, 0)
            body(0, True, False)
            head = c.n
            dve.wait_ge(zeroed, 16)
            with dve.Fori(1, B - 1) as b:
                m.turn(MISC_HEAD, MISC_TURN, b - 1)
                bank.turn(BANK_HEAD, BANK_TURN, b - 1)
                c.turn(head, DVE_TURN, b - 1)
                boundary(b)
                body(b, True, True)
            m.turn(MISC_HEAD, MISC_TURN, B - 2)
            bank.turn(BANK_HEAD, BANK_TURN, B - 2)
            c.turn(head, DVE_TURN, B - 2)
            boundary(B - 1)
            body(B - 1, False, True)
            for name, arg, _ in TAIL:
                task(name, arg, B - 1, last_batch=True)

            dve.wait_ge(misc_done, m.turns + m.n)
            dve.wait_ge(x2_kept, NTOK)
            tok = [P, NTOK, E]
            expert = counts[:, 0:E].unsqueeze(1).to_broadcast(tok)
            c.link(nc.vector.tensor_reduce(out=top[:], in_=logits[:], axis=AX.X, op=ALU.max))
            c.link(nc.vector.tensor_tensor(is_top[:], logits[:], top[:].unsqueeze(2).to_broadcast(tok), ALU.is_equal))
            c.link(nc.vector.tensor_scalar(is_top[:], is_top[:], -float(E), float(E), ALU.mult, ALU.add))
            c.link(nc.vector.tensor_tensor(choice[:], is_top[:], expert, ALU.add))
            c.link(nc.vector.tensor_reduce(out=first[:], in_=choice[:], axis=AX.X, op=ALU.min))
            picked = first[:].unsqueeze(2).to_broadcast(tok)
            nc.vector.tensor_tensor(chosenb[:], expert, picked, ALU.is_equal).then_inc(chosen_done, 1)
            c.link(nc.vector.tensor_tensor(chosen[:], expert, picked, ALU.is_equal))
            dve.wait_ge(ranked, 1)
            rank = misc[:, 0:NTOK * E].rearrange("p (n e) -> p n e", e=E)
            c.link(nc.vector.tensor_copy(scan[:, 0], misc[:, NTOK * E:2 * NTOK * E].rearrange("p (n e) -> p n e", e=E)))
            a = 0
            for d in (1, 2, 4, 8):
                nc.vector.tensor_copy(scan[:, 1 - a, 0:d], scan[:, a, 0:d])
                c.link(nc.vector.tensor_tensor(scan[:, 1 - a, d:], scan[:, a, d:], scan[:, a, 0:NTOK - d], ALU.add))
                a = 1 - a
            cmp = [P, E, NTOK]
            c.link(nc.vector.tensor_tensor(tiles_cmp[:], scan[:, a, NTOK - 1].unsqueeze(2).to_broadcast(cmp),
                                           counts[:, E:E + NTOK].unsqueeze(1).to_broadcast(cmp), ALU.is_gt))
            c.link(nc.vector.tensor_reduce(out=tiles_n[:], in_=tiles_cmp[:], axis=AX.X, op=ALU.add))
            c.link(nc.vector.tensor_copy(tiles_cum[:, 0], tiles_n[:]))
            t = 0
            for d in (1, 2, 4):
                nc.vector.tensor_copy(tiles_cum[:, 1 - t, 0:d], tiles_cum[:, t, 0:d])
                c.link(nc.vector.tensor_tensor(tiles_cum[:, 1 - t, d:], tiles_cum[:, t, d:], tiles_cum[:, t, 0:E - d], ALU.add))
                t = 1 - t
            c.link(nc.vector.tensor_tensor(first_slot[:], tiles_cum[:, t], tiles_n[:], ALU.subtract))
            c.link(nc.vector.tensor_scalar(first_slot[:], first_slot[:], float(P), None, ALU.mult))
            c.link(nc.vector.tensor_tensor(place_f[:], rank, scan[:, a], ALU.add))
            c.link(nc.vector.tensor_tensor(scan[:, 1 - a], misc[:, NTOK * E:2 * NTOK * E].rearrange("p (n e) -> p n e", e=E),
                                           first_slot[:].unsqueeze(1).to_broadcast(tok), ALU.subtract))
            c.link(nc.vector.tensor_tensor(place_f[:], place_f[:], scan[:, 1 - a], ALU.subtract))
            c.link(nc.vector.tensor_tensor(place_f[:], place_f[:], chosen[:], ALU.mult))
            c.link(nc.vector.tensor_reduce(out=slot_f[:], in_=place_f[:], axis=AX.X, op=ALU.add))
            nc.vector.tensor_copy(slot[:], slot_f[:]).then_inc(slots_done, 1)
            own = [P, NROUTE, E]
            c.link(nc.vector.tensor_tensor(owner_cmp[:], tiles_cum[:, t].unsqueeze(1).to_broadcast(own),
                                           counts[:, E + NTOK:].unsqueeze(2).to_broadcast(own), ALU.is_le))
            c.link(nc.vector.tensor_reduce(out=owner_f[:], in_=owner_cmp[:], axis=AX.X, op=ALU.add))
            nc.vector.tensor_scalar(owner[:], owner_f[:], float(E - 1), None, ALU.min).then_inc(owners_done, 1)

            for fc in range(F // P):
                dve.wait_ge(tail_full, 2 * fc + 2)
                dve.wait_ge(tail_silu, fc + 1)
                nc.vector.tensor_tensor(shared_hidT[:, fc], tail_silus[:, fc % 2], s_ps[:, 1], ALU.mult).then_inc(tail_hid, 1)
            for t in range(QT):
                dve.wait_ge(tail_full, 2 * (F // P) + t + 1)
                rows = x2[:, (B - 1) * QT + t]
                nc.vector.tensor_tensor(rows, rows, s_ps[:, t % 2, 0:D], ALU.add).then_inc(tail_added, 1)

            def make_hidden(pair, r):
                i = 2 * pair + r
                dve.wait_ge(silu_done, i + 1)
                nc.vector.tensor_tensor(hid[:, r], silu[:, r], st_ps[:, r, 1, :], ALU.mult).then_inc(hid_done, 1)

            def take_routed(pair, r):
                i = 2 * pair + r
                dve.wait_ge(down_full, i + 1)
                if not (isinstance(pair, int) and pair == 0):
                    dve.wait_ge(routed_stored[r], (BEGUN + pair) * 16)
                nc.vector.tensor_copy(yo[:, r], pv_ps[:, 0:D]).then_inc(down_done, 1)

            def routed_turn(k, r):
                i = 2 * k + r
                if not (isinstance(i, int) and i + 1 >= NROUTE):
                    make_hidden(k + r, 1 - r)
                take_routed(k, r)

            make_hidden(0, 0)
            with dve.Fori(0, LOOPED) as k:
                for r in range(2):
                    routed_turn(k, r)
            for i in range(2 * LOOPED, NROUTE):
                routed_turn(i // 2, i % 2)

            for g in range(4):
                dve.wait_ge(gathered[g], 4 * 16)
                if g == 0:
                    dve.wait_ge(tail_added, QT)
                rows = slice(g * 4, (g + 1) * 4)
                c.link(nc.vector.tensor_tensor(x2[:, rows], x2[:, rows], gated[g], ALU.add))
                for t in range(g * 4, g * 4 + 4):
                    ins = nc.vector.bn_stats(st6f[:, t], x2[:, t])
                c.link(ins)
                for t in range(g * 4, g * 4 + 4):
                    ins = nc.vector.bn_aggr(mvf[:, t], st6f[:, t])
                c.link(ins)
                nc.vector.tensor_scalar(mvf[:, rows, 1], mvf[:, rows, 1], EPS, None, ALU.add).then_inc(final_var, 1)
            for g in range(4):
                dve.wait_ge(final_rstd, g + 1)
                for t in range(g * 4, g * 4 + 4):
                    ins = nc.vector.tensor_scalar(x2[:, t], x2[:, t], mvf[:, t, 0:1], rstdf[:, t:t + 1], ALU.subtract, ALU.mult)
                ins.then_inc(final_done, 1)


def kernel(**inputs):
    import concourse.bacc as bacc
    from concourse.bass_utils import run_bass_kernel_spmd as run

    a = {k.replace("L0_", ""): np.ascontiguousarray(v) for k, v in inputs.items()}
    wq = a["attn_Wq"].reshape(D, 2, 2, 4, 2, 8, 2).transpose(0, 1, 6, 5, 2, 4, 3).reshape(D, 2, 2, P)
    wk = a["attn_Wk"].reshape(D, KV, 2, 8, 2).transpose(0, 4, 3, 1, 2).reshape(D, 2, 8, 2 * KV)
    wk = np.concatenate([wk, wk], axis=3).reshape(D, 1, 2, P)
    inv = (1.0 / np.float32(10000.0) ** (np.arange(0, DH, 2, dtype=np.float32) / np.float32(DH))).astype(np.float32)
    angle = (np.arange(T, dtype=np.float32)[:, None] * inv[None, :]).astype(np.float32)
    cos = np.repeat(np.cos(angle.astype(np.float64)).T.astype(np.float32), 16, axis=0)
    sin = np.repeat(np.sin(angle.astype(np.float64)).T.astype(np.float32), 16, axis=0)
    i = np.arange(P)
    arrays = {
        "x": a["attn_x"], "wqk": np.ascontiguousarray(np.concatenate([wq, wk], axis=1)), "wv": a["attn_Wv"], "wo": a["attn_Wo"],
        "lq1": a["attn_lambda_q1"], "lk1": a["attn_lambda_k1"], "lq2": a["attn_lambda_q2"], "lk2": a["attn_lambda_k2"],
        "gnw": a["attn_gn_w"], "gnb": a["attn_gn_b"], "cos_d": np.ascontiguousarray(cos), "sin_d": np.ascontiguousarray(sin),
        "ident_d": np.eye(P, dtype=np.float32), "mask_d": np.where(i[None, :] > i[:, None], NEG, 0.0).astype(np.float32),
        "router": np.ascontiguousarray(a["ffn_router_w"].T), "w_up": a["ffn_w_gate_up"], "w_down": a["ffn_w_down"],
        "s_up": a["ffn_shared_gate_up"], "s_down": a["ffn_shared_down"],
        "counts_d": np.concatenate([np.arange(E), np.arange(NTOK) * P, np.arange(NROUTE)]).astype(np.float32),
    }
    nc = bacc.Bacc("TRN2", target_bir_lowering=False, num_devices=1)
    t = {n: nc.dram_tensor(n + "_in", v.shape, mybir.dt.from_np(v.dtype), kind="ExternalInput").ap() for n, v in arrays.items()}
    out = nc.dram_tensor("out", (B, T, D), F32, kind="ExternalOutput").ap()
    build(nc, t["x"], t["wqk"], t["wv"], t["wo"], [t["lq1"], t["lk1"], t["lq2"], t["lk2"]], t["gnw"], t["gnb"],
          t["cos_d"], t["sin_d"], t["ident_d"], t["mask_d"],
          t["router"], t["w_up"], t["w_down"], t["s_up"], t["s_down"], t["counts_d"], out)
    r = run(nc, [{n + "_in": v for n, v in arrays.items()}], core_ids=[0])
    return r.results[0]["out"]
```

```python
from contextlib import ExitStack

import numpy as np

import concourse.bass as bass
from concourse import mybir

F32 = mybir.dt.float32
BF16 = mybir.dt.bfloat16
I32 = mybir.dt.int32
ALU = mybir.AluOpType
ACT = mybir.ActivationFunctionType
AX = mybir.AxisListType

P = 128
B, T, D = 4, 512, 256
H, KV, DH = 16, 4, 16
HS = 2 * H
DV = 2 * DH
QT = T // P
DC = D // P
SLOTS = 6
QPART = (0, 0, 0, 1, 1, 2)
KPART = (0, 1, 2, 0, 1, 0)
KROWS = SLOTS * DH
MROWS = KROWS + 2
LAMBDA_INIT = 0.2
EPS = 1e-5
NEG = -1e30
BEGUN = 1
NP = 4
E, F = 8, 512
NTOK = B * QT
NROUTE = NTOK + E - 1
LOOPED = (NROUTE - 2) // 2
WUP = DC * 2 * F
WEXP = WUP + F // P * D


class Chain:

    def __init__(self, eng, sem):
        self.eng, self.sem, self.n, self.turns = eng, sem, 0, 0

    def link(self, ins):
        self.n += 1
        ins.then_inc(self.sem, 1)
        self.eng.wait_ge(self.sem, self.turns + self.n)

    def turn(self, head, per, done):
        assert self.n in (head, head + per), (self.n, head, per)
        self.n, self.turns = head, done * per


STEPS = [(qt, g, kt) for qt in range(QT) for g in range(KV) for kt in range(qt + 1)]
NSTEP = len(STEPS)
NUNIT = QT * KV
DIAG = [n for n, (qt, g, kt) in enumerate(STEPS) if kt == qt]


def banks(qt):
    per = max(1, QT // (qt + 1))
    return [list(range(i, i + per)) for i in range(0, HS, per)]


NBANK = [len(banks(qt)) for qt in range(QT)]
FIRST_ST = [min(n for n, s in enumerate(STEPS) if s[0] == qt) for qt in range(QT)]
LAST_ST = [max(n for n, s in enumerate(STEPS) if s[0] == qt) for qt in range(QT)]


def spread(count, lo, hi):
    at = {}
    for i in range(count):
        at.setdefault(lo + i * (hi - lo) // count, []).append(i)
    return at


BANKS_AT = {}
for _qt, _lo, _hi, _back in ((2, 0, 7, 0), (3, 7, 19, 0), (0, 33, 35, -1), (1, 35, 39, -1)):
    for _n, _idx in spread(NBANK[_qt], _lo, _hi).items():
        BANKS_AT.setdefault(_n, []).extend((_qt, i, _back) for i in _idx)

TASKS = {n: [] for n in range(NSTEP)}
for _u in range(NUNIT - 1):
    _qt, _g = divmod(_u, KV)
    TASKS[FIRST_ST[_qt] + (_g + 1) * (_qt + 1) + 1].append(("norm", _u, 0))
TASKS[7].append(("mt", 2, 0))
TASKS[19].append(("mt", 3, 0))
TASKS[35].append(("mt", 0, -1))
TASKS[39].append(("mt", 1, -1))
PER_TILE = ("affine", "turn", "project", "x2", "retake", "logits")
SHARED = [(name, fc) for fc in range(F // P) for name in ("shared_gate", "shared_up")] + [("shared_down", t) for t in range(QT)]
for _n, _name in ((0, "sum"), (1, "mean"), (2, "square"), (3, "sum_squares"), (4, "var")):
    TASKS[_n].append((_name, 0, 1))
for _qt in range(QT):
    for _i, _name in enumerate(PER_TILE):
        TASKS[6 + 5 * _qt + _i].append((_name, _qt, 1))
TASKS[27].append(("top", 0, 1))
TASKS[27].append(("gate", 0, 1))
for _i, (_name, _arg) in enumerate(SHARED):
    TASKS[28 + _i].append((_name, _arg, 1))

HEAD = [("v", 0, 0), ("banks", (0, 0, 8), 0), ("mt", 0, 0), ("banks", (1, 0, 16), 0), ("mt", 1, 0)]
BOUNDARY = [("v", 0, 0), ("norm", NUNIT - 1, 1)]
TAIL = [(_name, _arg, 1 if _name.startswith("late") else 0) for _name, _arg in (
    ("norm", NUNIT - 1), ("sum", 0), ("late_gate", 0), ("late_up", 0), ("mean", 0), ("late_gate", 1), ("square", 0), ("late_up", 1),
    ("late_gate", 2), ("sum_squares", 0), ("late_up", 2), ("var", 0), ("late_gate", 3), ("late_up", 3),
    ("affine", 0), ("tail_turn", 0), ("affine", 1), ("tail_turn", 1), ("tail_project", 0), ("affine", 2), ("tail_turn", 2), ("x2", 0),
    ("tail_project", 1), ("retake", 0), ("affine", 3), ("tail_turn", 3), ("late_down", 0), ("logits", 0), ("x2", 1), ("tail_project", 2),
    ("retake", 1), ("late_down", 1), ("logits", 1), ("x2", 2), ("tail_project", 3), ("retake", 2), ("late_down", 2), ("logits", 2),
    ("x2", 3), ("late_down", 3), ("retake", 3), ("logits", 3), ("top", 0), ("gate", 0))]
MISC_TASKS = ("v", "mt", "norm", "mean", "var", "turn", "project", "tail_project", "retake", "logits",
              "shared_gate", "shared_up", "shared_down")


def tasks_at(n, ahead, post):
    return [t for t in TASKS[n] if t[2] == 0 or (t[2] < 0 and ahead) or (t[2] > 0 and post and (ahead or t[:2] not in SHARED))]


def body_tasks(ahead, post):
    return [t for n in range(NSTEP) for t in tasks_at(n, ahead, post)]


def misc_count(tasks):
    return sum(t[0] in MISC_TASKS for t in tasks)


FIRST, TURN = HEAD + body_tasks(True, False), BOUNDARY + body_tasks(True, True)
MISC_HEAD, MISC_TURN = misc_count(FIRST), misc_count(TURN)
BANK_HEAD, BANK_TURN = sum(NBANK) + NBANK[0] + NBANK[1], sum(NBANK)
ST_HEAD, ST_PREP = 4, 4
ST_TURN = ST_PREP + NSTEP
LINKS = {"norm": 2, "mean": 1, "project": 2, "gate": 2}
POOL_TURN = 2 + QT
DVE_TURN = sum(LINKS.get(t[0], 0) for t in TURN) + QT


def turned_maxima(b, qt, back):
    tasks, before = (FIRST, 0) if isinstance(b, int) and b == 0 else (TURN, MISC_HEAD + (b - 1) * MISC_TURN)
    return before + misc_count(tasks[:tasks.index(("mt", qt, back)) + 1])


PREP = [("cos", 0), ("sin", 0), ("even", 0), ("odd", 0), ("cos", 1), ("sin", 1), ("rest", 0), ("even", 1), ("odd", 1),
        ("cos", 2), ("low", 0), ("sin", 2), ("rest", 1), ("even", 2), ("odd", 2), ("low", 1), ("rest", 2), ("low", 2)]
PREP_AT = {k: i for i, k in enumerate(PREP)}
PREP_DONE = {k: i + 1 for i, k in enumerate(PREP)}
NPREP = len(PREP)
WRITES = 5
PREP_FROM = 6


def build(nc, x, wqk, wv, wo, lams, gnw, gnb, cos_d, sin_d, ident_d, mask_d,
          router, w_up, w_down, s_up, s_down, counts_d, tokens_d, spare_d, out):
    q_parts = nc.dram_tensor("q_parts", (B, 2, DH // 2, 2, 16, 3, QT, P), BF16, kind="Internal").ap()
    k_parts = nc.dram_tensor("k_parts", (B, 2, P, 3, QT, P), BF16, kind="Internal").ap()
    mrows = nc.dram_tensor("max_rows", (B, QT, 2 * HS, P), BF16, kind="Internal").ap()

    gated_rows = nc.dram_tensor("gated_rows", (B, T, D), F32, kind="Internal").ap()
    sorted_rows = nc.dram_tensor("sorted_rows", (NROUTE * P, D), F32, kind="Internal").ap()
    token_rows = nc.dram_tensor("token_rows", ((NTOK + NROUTE) * P, D), F32, kind="Internal").ap()
    slot_tokens = nc.dram_tensor("slot_tokens", (NROUTE * P, 1), I32, kind="Internal").ap()

    ctx = ExitStack()
    with ctx:
        def sb(name, shape, dt=F32):
            return ctx.enter_context(nc.sbuf_tensor(name, shape, dt))

        def sem(name):
            return ctx.enter_context(nc.semaphore(name))

        w_exp = sb("w_exp", [P, E * WEXP])
        work = sb("work", [P, 11264])

        class Place:

            def __init__(self, tensor):
                self.tensor, self.at = tensor, 0

            def take(self, columns, dt=F32):
                a = self.tensor[:, self.at:self.at + columns]
                self.at += columns
                return a if dt == F32 else a.bitcast(dt)

        early = Place(w_exp)
        raw = early.take(3 * 2 * T).rearrange("p (a h t) -> p a h t", a=3, h=2)
        parts = early.take(3 * 3 * T, BF16).rearrange("p (a h s q t) -> p a h s q t", a=3, h=2, s=3, q=QT)
        k_near = early.take(2 * KV * P, BF16).rearrange("p (r q t) -> p r q t", q=2, r=2 * KV)
        q_stack = early.take(QT * HS * P // 2, BF16).rearrange("p (q r t) -> p q r t", q=QT, r=HS)
        k_stack = early.take(QT * KV * P, BF16).rearrange("p (r q t) -> p r q t", q=QT, r=2 * KV)
        vo_lam = early.take(QT * KV * 2 * DV).rearrange("p (t g d) -> p t g d", t=QT, g=KV)
        probs = early.take(NP * 2 * T).rearrange("p (n s t) -> p n s t", n=NP, s=2)
        assert early.at <= E * WEXP and 2 * WEXP <= 3 * 2 * T + 3 * 3 * T
        assert 4 * WEXP <= 3 * 2 * T + 3 * 3 * T + 2 * KV * P + 2 * HS * P // 2

        mine = Place(work)
        att = mine.take(QT * H * DV).rearrange("p (q h d) -> p q h d", q=QT, h=H)
        dev = mine.take(QT * H * DV).rearrange("p (q h d) -> p q h d", q=QT, h=H)
        sq = mine.take(QT * H * DV).rearrange("p (q h d) -> p q h d", q=QT, h=H)
        rot = sq.rearrange("p q h d -> p (q h d)").rearrange("p (a h t) -> p a h t", a=2, h=2)
        gated_out = sq[:, 0:2].rearrange("p q h d -> p (q h d)").rearrange("p (n d) -> p n d", n=QT)
        shared_silu = sq[:, 2].rearrange("p h d -> p (h d)")
        tail_silus = sq[:, 2:4].rearrange("p q h d -> p q (h d)")
        shared_hidT = dev.rearrange("p q h d -> p (q h d)").rearrange("p (c t) -> p c t", c=F // P)
        vo = mine.take(QT * KV * 2 * DV).rearrange("p (t g d) -> p t g d", t=QT, g=KV)
        xin = mine.take(QT * D).rearrange("p (n d) -> p n d", n=QT)
        xT = mine.take(DC * T).rearrange("p (c t) -> p c t", c=DC)
        ol = mine.take(2 * T).rearrange("p (u t) -> p u t", u=2)
        xres = mine.take(QT * D).rearrange("p (n d) -> p n d", n=QT)

        tables = sb("tables", [P, 3584])
        mine = Place(tables)
        cos = mine.take(T)
        sin = mine.take(T)
        wqk_sb = mine.take(DC * 3 * 2 * P).rearrange("p (c a h m) -> p c a h m", c=DC, a=3, h=2)
        wo_sb = mine.take(4 * D).rearrange("p (c n) -> p c n", c=4)

        theirs = Place(tables)
        xe = theirs.take(2 * D).rearrange("p (u d) -> p u d", u=2)
        xeT = theirs.take(2 * D).rearrange("p (u c t) -> p u c t", u=2, c=DC)
        yo = theirs.take(2 * D).rearrange("p (u d) -> p u d", u=2)
        is_top = theirs.take(NTOK * E).rearrange("p (n e) -> p n e", e=E)
        choice = theirs.take(NTOK * E).rearrange("p (n e) -> p n e", e=E)
        chosen = theirs.take(NTOK * E).rearrange("p (n e) -> p n e", e=E)
        scan = theirs.take(2 * NTOK * E).rearrange("p (u n e) -> p u n e", u=2, e=E)
        tiles_cmp = theirs.take(E * NTOK).rearrange("p (e n) -> p e n", e=E)
        place_f = theirs.take(NTOK * E).rearrange("p (n e) -> p n e", e=E)
        owner_cmp = theirs.take(NROUTE * E).rearrange("p (n e) -> p n e", e=E)

        gated = [xin, vo.rearrange("p t g d -> p (t g d)").rearrange("p (n d) -> p n d", n=QT),
                 att[:, 0:2].rearrange("p q h d -> p (q h d)").rearrange("p (n d) -> p n d", n=QT), gated_out]
        theirs = Place(work)
        theirs.at = 8192
        silu = theirs.take(2 * F).rearrange("p (u f) -> p u f", u=2)
        hid = theirs.take(2 * F).rearrange("p (u f) -> p u f", u=2)
        hidT = theirs.take(2 * F).rearrange("p (u c t) -> p u c t", u=2, c=F // P)

        tail_zT = att.rearrange("p q h d -> p (q h d)").rearrange("p (q r t) -> p q r t", q=QT, r=4)
        late_hidT = tables[:, 0:QT * T].rearrange("p (c t) -> p c t", c=F // P)
        late_silus = ol

        wv_sb = sb("wv_sb", [P, DC, P])
        w_sh = sb("w_sh", [P, WEXP])
        router_sb = sb("router_sb", [P, DC, E])
        gw = sb("gw", [P, 2 * H * DH])
        gb = sb("gb", [P, 2 * H * DH])
        ident = sb("ident", [P, P])
        identb = sb("identb", [P, P], BF16)
        mask_f = sb("mask_f", [P, P])
        mask = sb("mask", [P, P], BF16)
        before = sb("before", [P, P], BF16)
        onesb = sb("onesb", [P, P], BF16)
        lamv = sb("lamv", [P, 4, DH])
        lamp = sb("lamp", [P, 2, DH])
        lams2 = sb("lams2", [P, 2])
        lame = sb("lame", [P, 2])
        neglam = sb("neglam", [P, 1])
        mneg = sb("mneg", [P, QT, HS])
        msplit = sb("msplit", [P, 2, P], BF16)
        mT = sb("mT", [2 * HS, 2, P], BF16)
        rl = sb("rl", [P, 4, 2])
        o12 = sb("o12", [P, 4, 2, DV])
        head_tot = sb("head_tot", [P, H])
        head_sq = sb("head_sq", [P, H])
        head_var = sb("head_var", [P, H])
        head_rstd = sb("head_rstd", [P, H])
        scale_row = sb("scale_row", [P, H, DV])
        averager = sb("averager", [P, P])
        st6 = sb("st6", [P, 6])
        mv = sb("mv", [P, 2, 2])
        rstd = sb("rstd", [P, 2])
        halfneg = sb("halfneg", [P, 1])
        zT = sb("zT", [P, 4, P])
        y = sb("y", [P, 2, D])
        zero_row = y[:, 0]
        x2T = sb("x2T", [P, DC, T])
        x2 = sb("x2", [P, NTOK, D])
        logits = sb("logits", [P, NTOK, E])
        counts = sb("counts", [P, E + NTOK + NROUTE])
        top = sb("top", [P, NTOK])
        logits_now = sb("logits_now", [P, QT, E])
        top_now = sb("top_now", [P, QT])
        gate = sb("gate", [P, 2, QT])
        first = sb("first", [P, NTOK])
        chosenb = sb("chosenb", [P, NTOK, E], BF16)
        tiles_n = sb("tiles_n", [P, E])
        tiles_cum = sb("tiles_cum", [P, 2, E])
        first_slot = sb("first_slot", [P, E])
        slot_f = sb("slot_f", [P, NTOK])
        slot = sb("slot", [P, NTOK], I32)
        owner_f = sb("owner_f", [P, NROUTE])
        owner = sb("owner", [P, NROUTE], I32)
        tokens = sb("tokens", [P, NTOK], I32)
        rows_of = sb("rows_of", [P, NROUTE], I32)
        shift = sb("shift", [P, NTOK])
        st6f = sb("st6f", [P, NTOK, 6])
        mvf = sb("mvf", [P, NTOK, 2])
        rstdf = sb("rstdf", [P, NTOK])

        s_ps = ctx.enter_context(nc.psum_tensor("s_ps", [P, 2, T], F32))
        st_ps = ctx.enter_context(nc.psum_tensor("st_ps", [P, 2, 2, T], F32))
        pv_ps = ctx.enter_context(nc.psum_tensor("pv_ps", [P, T], F32))
        misc = ctx.enter_context(nc.psum_tensor("misc", [P, T], F32))

        consts_loaded = sem("consts_loaded")
        ident_loaded = sem("ident_loaded")
        wqk_loaded = sem("wqk_loaded")
        consts_ready = sem("consts_ready")
        start_pool = sem("start_pool")
        start_dve = sem("start_dve")
        start_high = sem("start_high")
        start_mid = sem("start_mid")
        x_loaded = sem("x_loaded")
        xres_loaded = sem("xres_loaded")
        parts_written = sem("parts_written")
        start_written = sem("start_written")
        q_loaded = [sem(f"q_loaded{i}") for i in range(QT)]
        k_loaded = sem("k_loaded")
        max_stored = sem("max_stored")
        max_loaded = [sem(f"max_loaded{i}") for i in range(QT)]
        st_full = sem("st_full")
        st_done = sem("st_done")
        bank_full = sem("bank_full")
        bank_done = sem("bank_done")
        misc_full = sem("misc_full")
        misc_done = sem("misc_done")
        pv_done = sem("pv_done")
        pv_step = sem("pv_step")
        diag_done = sem("diag_done")
        prep_done = sem("prep_done")
        high_done = sem("high_done")
        mid_done = sem("mid_done")
        split_done = sem("split_done")
        dve_chain = sem("dve_chain")
        pool_chain = sem("pool_chain")
        lam_summed = sem("lam_summed")
        lam_exp = sem("lam_exp")
        lam_ready = sem("lam_ready")
        summed = sem("summed")
        centred = sem("centred")
        squared = sem("squared")
        stats_taken = sem("stats_taken")
        exps_taken = sem("exps_taken")
        squares_summed = sem("squares_summed")
        att_var = sem("att_var")
        scaled = sem("scaled")
        scale_ready = sem("scale_ready")
        y_var = sem("y_var")
        y_rstd = sem("y_rstd")
        x2_done = sem("x2_done")
        gated_stored = sem("gated_stored")
        gated_loaded = sem("gated_loaded")
        near_loaded = sem("near_loaded")
        x2_kept = sem("x2_kept")
        stored = sem("stored")
        zeroed = sem("zeroed")
        zero_ready = sem("zero_ready")
        shared_loaded = sem("shared_loaded")
        experts_loaded = sem("experts_loaded")
        gate_exp = sem("gate_exp")
        top_found = sem("top_found")
        gated_done = sem("gated_done")
        chosen_done = sem("chosen_done")
        ranked = sem("ranked")
        tail_full = sem("tail_full")
        late_full = sem("late_full")
        late_silu = sem("late_silu")
        late_hid = sem("late_hid")
        late_added = sem("late_added")
        tail_turned = sem("tail_turned")
        tail_taken = sem("tail_taken")
        tail_silu = sem("tail_silu")
        tail_hid = sem("tail_hid")
        tail_added = sem("tail_added")
        slots_done = sem("slots_done")
        owners_done = sem("owners_done")
        scattered = sem("scattered")
        tokens_ready = sem("tokens_ready")
        tokens_scattered = sem("tokens_scattered")
        rows_of_loaded = sem("rows_of_loaded")
        tile_loaded = [sem(f"tile_loaded{i}") for i in range(2)]
        turned = sem("turned")
        turned_done = sem("turned_done")
        up_full = sem("up_full")
        hid_turned = sem("hid_turned")
        hidT_done = sem("hidT_done")
        silu_done = sem("silu_done")
        hid_done = sem("hid_done")
        down_full = sem("down_full")
        down_done = sem("down_done")
        routed_stored = [sem(f"routed_stored{i}") for i in range(2)]
        gathered = [sem(f"gathered{i}") for i in range(4)]
        pool_added = sem("pool_added")
        final_var = sem("final_var")
        final_rstd = sem("final_rstd")
        final_shifted = sem("final_shifted")
        final_done = sem("final_done")

        block = ctx.enter_context(nc.Block())

        NCONST = 13

        def raw_q(pair):
            return raw[:, pair].rearrange("p h (q t) -> p h q t", q=QT)

        def prepare(eng, what, pair, rotated):
            X = raw[:, pair]
            both = [P, 2, T]
            if what == "cos":
                return eng.tensor_tensor(rotated[:, 0], X, cos[:].unsqueeze(1).to_broadcast(both), ALU.mult)
            if what == "sin":
                return eng.tensor_tensor(rotated[:, 1], X, sin[:].unsqueeze(1).to_broadcast(both), ALU.mult)
            if what == "even":
                return eng.tensor_tensor(X[:, 0], rotated[:, 0, 0], rotated[:, 1, 1], ALU.subtract)
            if what == "odd":
                return eng.tensor_tensor(X[:, 1], rotated[:, 1, 0], rotated[:, 0, 1], ALU.add)
            if what == "rest":
                return eng.tensor_tensor(raw_q(pair), raw_q(pair), parts[:, pair, :, 0], ALU.subtract)
            return eng.tensor_tensor(parts[:, pair, :, 2], raw_q(pair), parts[:, pair, :, 1], ALU.subtract)

        START_POOL = [(what, 0) for what in ("cos", "sin", "even", "odd", "rest", "low")]
        START_DVE = ([(what, pair) for pair in (1, 2) for what in ("cos", "sin", "even", "odd")]
                     + [(what, pair) for what in ("rest", "low") for pair in (1, 2)])
        START_CASTS = (1, 0, 2)

        def started(op):
            of, steps = (start_pool, START_POOL) if op[1] == 0 else (start_dve, START_DVE)
            return of, steps.index(op) + 1

        def start_prepare(engine, eng, steps, sem, rotated):
            for what, pair in steps:
                if what == "cos":
                    engine.wait_ge(st_done, prep_slot(None, pair + 1))
                    if pair == 2:
                        engine.wait_ge(*started(("odd", 1)))
                elif what == "even":
                    engine.wait_ge(*started(("sin", pair)))
                elif what == "rest":
                    engine.wait_ge(start_high, START_CASTS.index(pair) + 1)
                elif what == "low":
                    engine.wait_ge(start_mid, START_CASTS.index(pair) + 1)
                prepare(eng, what, pair, rotated).then_inc(sem, 1)

        def st_at(b, k, prep):
            return ST_HEAD + b * ST_TURN + (ST_PREP if prep else 0) + k + 1

        def prep_slot(b, k):
            return k + 1 if b is None else ST_HEAD + b * ST_TURN + k + 1

        class Misc:

            def __init__(self):
                self.n, self.turns = 0, 0

            def next(self):
                self.n += 1
                return self.turns + self.n

            def turn(self, head, per, done):
                assert self.n in (head, head + per), (self.n, head, per)
                self.n, self.turns = head, done * per

        def store_parts(engine, nb, pair, first=0, end=3, written=parts_written):
            if pair == 2:
                engine.dma_start(k_parts[nb, :, :, first:end].rearrange("h r s q t -> r h (s q t)"),
                                 parts[:, pair, :, first:end].rearrange("p h s q t -> p h (s q t)")).then_inc(written, 16)
            else:
                for h in range(2):
                    engine.dma_start(q_parts[nb, h, :, pair, :, first:end].rearrange("j r s q t -> j r (s q t)"),
                                     parts[:, pair, h, first:end].rearrange("p s q t -> p (s q t)")).then_inc(written, 16)

        @block.sync
        def _(sp):
            def load_x(b):
                sp.dma_start(xin[:], x[b].rearrange("(n p) d -> p n d", p=P)).then_inc(x_loaded, 16)

            sp.dma_start(ident[:], ident_d).then_inc(ident_loaded, 16)
            load_x(0)
            sp.dma_start(wqk_sb[:], wqk.rearrange("(c p) a h m -> p c a h m", p=P)).then_inc(wqk_loaded, 16)
            sp.dma_start(cos[:], cos_d).then_inc(consts_loaded, 16)
            sp.dma_start(sin[:], sin_d).then_inc(consts_loaded, 16)
            sp.dma_start(mask_f[:], mask_d).then_inc(consts_loaded, 16)
            sp.dma_start(wv_sb[:], wv.rearrange("(c p) m -> p c m", p=P)).then_inc(consts_loaded, 16)
            sp.dma_start(wo_sb[:], wo.rearrange("(c p) m -> p c m", p=P)).then_inc(consts_loaded, 16)
            for i, v in enumerate(lams):
                sp.dma_start(lamv[:, i, :], v.unsqueeze(0).to_broadcast([P, DH])).then_inc(consts_loaded, 16)
            sp.dma_start(gw[:], gnw.unsqueeze(0).to_broadcast([P, T])).then_inc(consts_loaded, 16)
            sp.dma_start(gb[:], gnb.unsqueeze(0).to_broadcast([P, T])).then_inc(consts_loaded, 16)

            sp.dma_start(router_sb[:], router.rearrange("(c p) e -> p c e", p=P)).then_inc(consts_loaded, 16)
            sp.dma_start(counts[:], counts_d.unsqueeze(0).to_broadcast([P, E + NTOK + NROUTE])).then_inc(consts_loaded, 16)
            sp.dma_start(w_sh[:, 0:WUP].rearrange("p (c n) -> p c n", c=DC), s_up.rearrange("(c p) n -> p c n", p=P)).then_inc(shared_loaded, 16)
            sp.dma_start(w_sh[:, WUP:WEXP].rearrange("p (c n) -> p c n", c=F // P), s_down.rearrange("(c p) n -> p c n", p=P)).then_inc(shared_loaded, 16)
            sp.dma_start(tokens[:], tokens_d).then_inc(tokens_ready, 16)
            sp.dma_start(slot_tokens, spare_d).then_inc(tokens_ready, 16)
            sp.wait_ge(zero_ready, 1)
            sp.dma_start(sorted_rows.rearrange("(n p) d -> p n d", p=P), zero_row.unsqueeze(1).to_broadcast([P, NROUTE, D])).then_inc(zeroed, 16)

            def await_parts(b, slots, part):
                if isinstance(b, int) and b == 0:
                    sp.wait_ge(start_written, WRITES * 16)
                    if all(part[s] == 0 for s in slots):
                        return
                sp.wait_ge(parts_written, (b + 1) * WRITES * 16)

            def load_q(b, qt, used, slots=range(SLOTS)):
                if used is not None:
                    sp.wait_ge(st_full, used)
                await_parts(b, slots, QPART)
                for s in slots:
                    sp.dma_start(q_stack[s * DH:(s + 1) * DH, qt],
                                 q_parts[b, :, :, :, :, QPART[s], qt].rearrange("h j a r t -> (h j) (a r) t")
                                 ).then_inc(q_loaded[qt], 16)

            def load_k(b):
                await_parts(b, range(SLOTS), KPART)
                for s in range(SLOTS):
                    sp.dma_start(k_stack[s * DH:(s + 1) * DH],
                                 k_parts[b, :, :, KPART[s]].rearrange("h (j r) q t -> (h j) r q t", j=8)[:, 0:2 * KV]
                                 ).then_inc(k_loaded, 16)

            def load_near(b, slots=range(SLOTS)):
                await_parts(b, slots, KPART)
                for s in slots:
                    sp.dma_start(k_near[s * DH:(s + 1) * DH],
                                 k_parts[b, :, :, KPART[s], 0:2].rearrange("h (j r) q t -> (h j) r q t", j=8)[:, 0:2 * KV]
                                 ).then_inc(near_loaded, 16)

            def max_rows(b, qt, fills):
                sp.wait_ge(misc_done, fills)
                sp.dma_start(mrows[b, qt], mT[:, qt % 2, :]).then_inc(max_stored, 16)
                sp.wait_ge(max_stored, (b * QT + qt + 1) * 16)
                sp.dma_start(q_stack[KROWS:MROWS, qt, :, :],
                             mrows[b, qt].rearrange("(m r) t -> m r t", m=2)).then_inc(max_loaded[qt], 16)

            def load_residual(b):
                sp.wait_ge(x2_done, BEGUN + b * QT)
                sp.dma_start(xres[:], x[b].rearrange("(n p) d -> p n d", p=P)).then_inc(xres_loaded, 16)

            def load_experts(first, end):
                for e in range(first, end):
                    w = w_exp[:, e * WEXP:(e + 1) * WEXP]
                    sp.dma_start(w[:, 0:WUP].rearrange("p (c n) -> p c n", c=DC), w_up[e].rearrange("(c p) n -> p c n", p=P)).then_inc(experts_loaded, 16)
                    sp.dma_start(w[:, WUP:WEXP].rearrange("p (c n) -> p c n", c=F // P), w_down[e].rearrange("(c p) n -> p c n", p=P)).then_inc(experts_loaded, 16)

            def store_gated(b):
                sp.wait_ge(gated_done, b + 1)
                sp.dma_start(gated_rows[b].rearrange("(n p) d -> p n d", p=P), gated_out[:]).then_inc(gated_stored, 16)

            def body(b, prep, post):
                if prep and post:
                    sp.wait_ge(st_full, prep_slot(b - 1, 0))
                    load_x(b + 1)
                if post:
                    sp.wait_ge(st_full, st_at(b - 1, NSTEP - 1, True))
                    load_k(b)
                    load_q(b, 3, None)
                if post:
                    load_residual(b - 1)
                max_rows(b, 2, turned_maxima(b, 2, 0))
                max_rows(b, 3, turned_maxima(b, 3, 0))
                if prep:
                    load_q(b + 1, 0, st_at(b, LAST_ST[0], prep))
                    sp.wait_ge(st_full, st_at(b, LAST_ST[1], prep))
                    load_near(b + 1)
                    load_q(b + 1, 1, None)
                    load_q(b + 1, 2, st_at(b, LAST_ST[2], prep))
                if not prep:
                    load_experts(0, 2)
                    sp.wait_ge(st_full, st_at(b, LAST_ST[1], prep))
                    load_experts(2, 4)
                if post:
                    store_gated(b - 1)
                if prep:
                    max_rows(b + 1, 0, turned_maxima(b, 0, -1))
                    max_rows(b + 1, 1, turned_maxima(b, 1, -1))

            for k, pair in enumerate(START_CASTS):
                sp.wait_ge(start_high, k + 1)
                store_parts(sp, 0, pair, 0, 1, start_written)
            for high in (True, False):
                load_near(0, [s for s in range(SLOTS) if (KPART[s] == 0) == high])
                load_q(0, 0, None, [s for s in range(SLOTS) if (QPART[s] == 0) == high])
            load_q(0, 1, None)
            load_k(0)
            load_q(0, 2, None)
            load_q(0, 3, None)
            sp.wait_ge(st_full, prep_slot(None, 0))
            load_x(1)
            max_rows(0, 0, misc_count(HEAD[:HEAD.index(("mt", 0, 0)) + 1]))
            max_rows(0, 1, misc_count(HEAD))
            body(0, True, False)
            with sp.Fori(1, B - 1) as b:
                body(b, True, True)
            body(B - 1, False, True)
            load_residual(B - 1)
            sp.wait_ge(pv_step, B * NSTEP)
            load_experts(4, E)
            sp.wait_ge(gated_stored, (BEGUN + B - 1) * 16)
            sp.wait_ge(centred, B)
            for b in range(B - 1):
                if b == B - 2:
                    sp.wait_ge(y_var, B * QT)
                sp.dma_start(gated[b], gated_rows[b].rearrange("(n p) d -> p n d", p=P)).then_inc(gated_loaded, 16)

            def load_tile(i, pair, r):
                if not (isinstance(pair, int) and pair == 0):
                    sp.wait_ge(turned, i - 1)
                sp.dma_start(xe[:, r], sorted_rows[bass.ds(i * P, P), :]).then_inc(tile_loaded[r], 16)

            def routed_turn(k, r):
                load_tile(2 * k + r, k, r)

            sp.wait_ge(scattered, NTOK * 16)
            for r in range(2):
                load_tile(r, 0, r)
            for r in range(2):
                routed_turn(1, r)
            sp.wait_ge(tokens_scattered, NTOK * 16)
            sp.dma_start(rows_of[:], slot_tokens.rearrange("(n p) o -> p (n o)", p=P), allow_slow_non_contiguous=True).then_inc(rows_of_loaded, 16)
            with sp.Fori(2, LOOPED) as k:
                for r in range(2):
                    routed_turn(k, r)
            for i in range(2 * LOOPED, NROUTE):
                routed_turn(i // 2, i % 2)
            for r in range(2):
                sp.wait_ge(routed_stored[r], (NROUTE + 1 - r) // 2 * 16)
            for g in range(4):
                sp.dma_start(gated[g], token_rows[g * T:(g + 1) * T, :].rearrange("(n p) d -> p n d", p=P)).then_inc(gathered[g], 16)

            for g in range(4):
                sp.wait_ge(final_done, g + 1)
                sp.dma_start(out[g].rearrange("(n p) d -> p n d", p=P), x2[:, g * 4:(g + 1) * 4]).then_inc(stored, 16)
            sp.wait_ge(stored, 4 * 16)

        @block.tensor
        def _(pe):
            m = Misc()
            bank = Misc()

            def prep(b):
                nb = 0 if b is None else b + 1
                pe.wait_ge(x_loaded, (nb + 1) * 16)
                for k in range(4):
                    v = prep_slot(b, k)
                    if not (b is None and k < 2):
                        pe.wait_ge(st_done, v - 2)
                    slot = st_ps[:, k % 2]
                    if k == 0:
                        for c in range(DC):
                            for t in range(QT):
                                last = nc.tensor.transpose(slot[:, c, t * P:(t + 1) * P], xin[:, t, c * P:(c + 1) * P], ident[:])
                    else:
                        if k == 1:
                            pe.wait_ge(st_done, prep_slot(b, 0))
                            if b is None:
                                pe.wait_ge(wqk_loaded, 16)
                        for half in range(2):
                            for c in range(DC):
                                last = nc.tensor.matmul(slot[:, half, :], wqk_sb[:, c, k - 1, half, :], xT[:, c, :],
                                                        start=(c == 0), stop=(c == DC - 1))
                    last.then_inc(st_full, 1)

            def score_bank(b, qt, i):
                v = bank.next()
                if not (isinstance(v, int) and v <= 2):
                    pe.wait_ge(bank_done, v - 2)
                rows = banks(qt)[i]
                w = (qt + 1) * P
                keys = k_near if qt < 2 else k_stack
                for n, hs in enumerate(rows):
                    gs = hs // 4
                    o = s_ps[:, (i % 2), n * w:(n + 1) * w]
                    nc.tensor.matmul(o, q_stack[0:KROWS, qt, hs, :], keys[0:KROWS, gs, 0:qt + 1, :], start=True, stop=False)
                    last = nc.tensor.matmul(o[:, w - P:w], identb[:], mask[:], start=False, stop=True)
                last.then_inc(bank_full, 1)

            def await_stacks(b, qt):
                pe.wait_ge(q_loaded[qt], (b + 1) * SLOTS * 16)
                if qt == 0:
                    pe.wait_ge(near_loaded, (b + 1) * SLOTS * 16)
                if qt == 2:
                    pe.wait_ge(k_loaded, (b + 1) * SLOTS * 16)

            def task(name, arg, b):
                if name == "banks":
                    qt, lo, hi = arg
                    await_stacks(b, qt)
                    for i in range(lo, hi):
                        score_bank(b, qt, i)
                if name in ("late_gate", "late_up"):
                    half = int(name == "late_up")
                    if arg > 0:
                        pe.wait_ge((late_silu, late_hid)[half], arg)
                    for ch in range(DC):
                        at = ch * 2 * F + half * F + arg * P
                        last = nc.tensor.matmul(s_ps[:, half], w_sh[:, at:at + P], x2T[:, ch, :], start=(ch == 0), stop=(ch == DC - 1))
                    last.then_inc(late_full, 1)
                if name == "late_down":
                    if arg == 0:
                        pe.wait_ge(late_silu, F // P)
                        pe.wait_ge(late_hid, F // P)
                    if arg >= 2:
                        pe.wait_ge(late_added, arg - 1)
                    for fc in range(F // P):
                        last = nc.tensor.matmul(s_ps[:, arg % 2, 0:D], late_hidT[:, fc, arg * P:(arg + 1) * P],
                                                w_sh[:, WUP + fc * D:WUP + (fc + 1) * D], start=(fc == 0), stop=(fc == F // P - 1))
                    last.then_inc(late_full, 1)
                if name == "tail_turn":
                    pe.wait_ge(scaled, b * QT + arg + 1)
                    for r in range(4):
                        last = nc.tensor.transpose(st_ps[:, arg // 2, arg % 2, r * P:(r + 1) * P],
                                                   dev[:, arg].rearrange("p h d -> p (h d)")[:, r * P:(r + 1) * P], ident[:])
                    last.then_inc(tail_turned, 1)
                if name not in MISC_TASKS:
                    return
                v = m.next()
                if not (isinstance(v, int) and v == 1):
                    pe.wait_ge(misc_done, v - 1)
                if name == "v":
                    for t in range(QT):
                        for c in range(DC):
                            last = nc.tensor.matmul(misc[:, t * P:(t + 1) * P], xT[:, c, t * P:(t + 1) * P], wv_sb[:, c, :],
                                                    start=(c == 0), stop=(c == DC - 1))
                elif name == "mt":
                    pe.wait_ge(split_done, b * QT + arg + 1)
                    last = nc.tensor.transpose(misc[:, 0:P // 2].bitcast(BF16), msplit[:, arg % 2, :], identb[:])
                elif name == "norm":
                    pe.wait_ge(pv_done, b * NUNIT + arg + 1)
                    for r in range(4):
                        last = nc.tensor.transpose(misc[:, r * P:(r + 1) * P], ol[:, arg % 2, r * P:(r + 1) * P], ident[:])
                elif name == "mean":
                    pe.wait_ge(summed, b + 1)
                    last = nc.tensor.matmul(misc[:, 0:H], averager[:], head_tot[:], start=True, stop=True)
                elif name == "var":
                    pe.wait_ge(squares_summed, b + 1)
                    last = nc.tensor.matmul(misc[:, 0:H], averager[:], head_sq[:], start=True, stop=True)
                elif name == "turn":
                    pe.wait_ge(scaled, b * QT + arg + 1)
                    for r in range(4):
                        last = nc.tensor.transpose(misc[:, r * P:(r + 1) * P], dev[:, arg].rearrange("p h d -> p (h d)")[:, r * P:(r + 1) * P], ident[:])
                elif name == "project":
                    for r in range(4):
                        last = nc.tensor.matmul(misc[:, 0:D], zT[:, r, :], wo_sb[:, r, :], start=(r == 0), stop=(r == 3))
                elif name == "tail_project":
                    pe.wait_ge(tail_taken, arg + 1)
                    for r in range(4):
                        last = nc.tensor.matmul(misc[:, 0:D], tail_zT[:, arg, r, :], wo_sb[:, r, :], start=(r == 0), stop=(r == 3))
                elif name == "retake":
                    pe.wait_ge(x2_done, BEGUN + b * QT + arg + 1)
                    for ch in range(DC):
                        last = nc.tensor.transpose(misc[:, ch * P:(ch + 1) * P], y[:, arg % 2, ch * P:(ch + 1) * P], ident[:])
                elif name == "logits":
                    for ch in range(DC):
                        last = nc.tensor.matmul(misc[:, 0:E], x2T[:, ch, arg * P:(arg + 1) * P], router_sb[:, ch, :],
                                                start=(ch == 0), stop=(ch == DC - 1))
                elif name in ("shared_gate", "shared_up"):
                    at = (F if name == "shared_up" else 0) + arg * P
                    for ch in range(DC):
                        last = nc.tensor.matmul(misc[:], w_sh[:, ch * 2 * F + at:ch * 2 * F + at + P], x2T[:, ch, :],
                                                start=(ch == 0), stop=(ch == DC - 1))
                elif name == "shared_down":
                    for fc in range(F // P):
                        last = nc.tensor.matmul(misc[:, 0:D], shared_hidT[:, fc, arg * P:(arg + 1) * P], w_sh[:, WUP + fc * D:WUP + (fc + 1) * D],
                                                start=(fc == 0), stop=(fc == F // P - 1))
                last.then_inc(misc_full, 1)

            def scores(b, n, prep):
                qt, g, kt = STEPS[n]
                v = st_at(b, n, prep)
                if n == FIRST_ST[qt]:
                    pe.wait_ge(max_loaded[qt], (b + 1) * 16)
                pe.wait_ge(st_done, v - 2)
                for s in range(2):
                    gs = 2 * g + s
                    last = nc.tensor.matmul(st_ps[:, n % 2, s, :], (k_near if qt < 2 else k_stack)[0:MROWS, gs, kt, :],
                                            q_stack[0:MROWS, qt, gs * 4:gs * 4 + 4, :], start=True, stop=True)
                last.then_inc(st_full, 1)

            def weigh(b, n, prep):
                qt, g, kt = STEPS[n]
                u = qt * KV + g
                if kt == qt:
                    pe.wait_ge(diag_done, b * NUNIT + DIAG.index(n) + 1)
                else:
                    pe.wait_ge(st_done, st_at(b, n, prep))
                if kt == 0:
                    if u > 0:
                        pe.wait_ge(pv_done, b * NUNIT + u)
                for s in range(2):
                    last = nc.tensor.matmul(pv_ps[s * 64:(s + 1) * 64, :], (vo, vo_lam)[s][:, kt, g, :], probs[:, n % NP, s, :],
                                            start=(kt == 0), stop=(kt == qt))
                last.then_inc(pv_step, 1)

            def body(b, prep_next, post):
                if prep_next:
                    prep(b)
                scores(b, 0, prep_next)
                scores(b, 1, prep_next)
                for n in range(NSTEP):
                    if n + 2 < NSTEP:
                        scores(b, n + 2, prep_next)
                    now = [x for x in BANKS_AT.get(n, []) if x[2] == 0 or prep_next]
                    for part in (0, 1):
                        if part == 1 and n > 0:
                            weigh(b, n - 1, prep_next)
                        for qt, i, back in (now[:(len(now) + 1) // 2], now[(len(now) + 1) // 2:])[part]:
                            if i == 0:
                                await_stacks(b - back, qt)
                            score_bank(b - back, qt, i)
                    for name, arg, back in tasks_at(n, prep_next, post):
                        task(name, arg, b - back)
                weigh(b, NSTEP - 1, prep_next)

            def boundary(b):
                for name, arg, back in BOUNDARY:
                    task(name, arg, b - back)

            pe.wait_ge(ident_loaded, 16)
            prep(None)
            pe.wait_ge(consts_loaded, NCONST * 16)
            pe.wait_ge(consts_ready, 2)
            for name, arg, _ in HEAD:
                task(name, arg, 0)
            body(0, True, False)
            with pe.Fori(1, B - 1) as b:
                m.turn(MISC_HEAD, MISC_TURN, b - 1)
                bank.turn(BANK_HEAD, BANK_TURN, b - 1)
                boundary(b)
                body(b, True, True)
            m.turn(MISC_HEAD, MISC_TURN, B - 2)
            bank.turn(BANK_HEAD, BANK_TURN, B - 2)
            boundary(B - 1)
            body(B - 1, False, True)
            for name, arg, back in TAIL:
                task(name, arg, B - 1 - back)

            pe.wait_ge(misc_done, m.turns + m.n)
            pe.wait_ge(chosen_done, 1)
            nc.tensor.matmul(misc[:, 0:NTOK * E], before[:], chosenb[:], start=True, stop=True)
            nc.tensor.matmul(misc[:, NTOK * E:2 * NTOK * E], onesb[:], chosenb[:], start=True, stop=True).then_inc(ranked, 1)
            for fc in range(F // P):
                for half, done in ((0, tail_silu), (1, tail_hid)):
                    if fc > 0:
                        pe.wait_ge(done, fc)
                    for ch in range(DC):
                        at = ch * 2 * F + half * F + fc * P
                        last = nc.tensor.matmul(s_ps[:, half], w_sh[:, at:at + P], x2T[:, ch, :], start=(ch == 0), stop=(ch == DC - 1))
                    last.then_inc(tail_full, 1)
            pe.wait_ge(tail_silu, F // P)
            pe.wait_ge(tail_hid, F // P)
            for t in range(QT):
                if t >= 2:
                    pe.wait_ge(tail_added, t - 1)
                for fc in range(F // P):
                    last = nc.tensor.matmul(s_ps[:, t % 2, 0:D], shared_hidT[:, fc, t * P:(t + 1) * P],
                                            w_sh[:, WUP + fc * D:WUP + (fc + 1) * D], start=(fc == 0), stop=(fc == F // P - 1))
                last.then_inc(tail_full, 1)
            pe.wait_ge(tail_added, QT)

            def turn_tile(pair, r):
                i = 2 * pair + r
                pe.wait_ge(tile_loaded[r], (pair + 1) * 16)
                if not (isinstance(i, int) and i == 0):
                    pe.wait_ge(turned_done, i)
                for ch in range(DC):
                    last = nc.tensor.transpose(s_ps[:, 0, ch * P:(ch + 1) * P], xe[:, r, ch * P:(ch + 1) * P], ident[:])
                last.then_inc(turned, 1)

            def up(pair, r, e):
                i = 2 * pair + r
                pe.wait_ge(turned_done, i + 1)
                if not (isinstance(i, int) and i < 2):
                    pe.wait_ge(hid_done, BEGUN + i - 1)
                for half in range(2):
                    for ch in range(DC):
                        w = w_exp[:, bass.ds(e * WEXP + ch * 2 * F + half * F, F)]
                        last = nc.tensor.matmul(st_ps[:, r, half, :], xeT[:, r, ch, :], w, start=(ch == 0), stop=(ch == DC - 1))
                last.then_inc(up_full, 1)

            def turn_hidden(pair, r):
                i = 2 * pair + r
                pe.wait_ge(hid_done, BEGUN + i + 1)
                if not (isinstance(i, int) and i == 0):
                    pe.wait_ge(hidT_done, BEGUN + i)
                for ch in range(F // P):
                    last = nc.tensor.transpose(s_ps[:, 1, ch * P:(ch + 1) * P], hid[:, r, ch * P:(ch + 1) * P], ident[:])
                last.then_inc(hid_turned, 1)

            def down(pair, r, e):
                i = 2 * pair + r
                pe.wait_ge(hidT_done, BEGUN + i + 1)
                if not (isinstance(i, int) and i < 1):
                    pe.wait_ge(down_done, BEGUN + i)
                for fc in range(F // P):
                    w = w_exp[:, bass.ds(e * WEXP + WUP + fc * D, D)]
                    last = nc.tensor.matmul(pv_ps[:, 0:D], hidT[:, r, fc, :], w, start=(fc == 0), stop=(fc == F // P - 1))
                last.then_inc(down_full, 1)

            def owner_of(i):
                return pe.value_load(owner[0:1, bass.ds(i, 1)], min_val=0, max_val=E - 1)

            pe.wait_ge(owners_done, 1)
            pe.wait_ge(experts_loaded, 2 * E * 16)
            turn_tile(0, 0)
            up(0, 0, owner_of(0))
            turn_tile(0, 1)

            def routed_turn(k, r):
                i = 2 * k + r
                static = isinstance(i, int)
                turn_hidden(k, r)
                if not (static and i + 1 >= NROUTE):
                    up(k + r, 1 - r, owner_of(i + 1))
                if not (static and i + 2 >= NROUTE):
                    turn_tile(k + 1, r)
                down(k, r, owner_of(i))

            with pe.Fori(0, LOOPED) as k:
                for r in range(2):
                    routed_turn(k, r)
            for i in range(2 * LOOPED, NROUTE):
                routed_turn(i // 2, i % 2)

        @block.scalar
        def _(act):
            m = Misc()

            def evacuate(b, k):
                act.wait_ge(st_full, prep_slot(b, k))
                if k == 0:
                    nc.scalar.copy(xT[:], st_ps[:, 0]).then_inc(st_done, 1)
                else:
                    nc.scalar.copy(raw[:, k - 1], st_ps[:, k % 2]).then_inc(st_done, 1)

            def cast(nb, part, pair):
                if part == 0:
                    act.wait_ge(parts_written, nb * WRITES * 16)
                    act.wait_ge(prep_done, (nb - 1) * NPREP + PREP_DONE[("odd", pair)])
                    nc.scalar.copy(parts[:, pair, :, 0], raw_q(pair)).then_inc(high_done, 1)
                else:
                    act.wait_ge(prep_done, (nb - 1) * NPREP + PREP_DONE[("rest", pair)])
                    nc.scalar.copy(parts[:, pair, :, 1], raw_q(pair)).then_inc(mid_done, 1)

            def write_parts(nb, pair):
                act.wait_ge(prep_done, (nb - 1) * NPREP + PREP_DONE[("low", pair)])
                store_parts(act, nb, pair)

            casts_at = {}
            for pair in range(3):
                for what, part, step in (("cast", 0, PREP_AT[("odd", pair)] + 2), ("cast", 1, PREP_AT[("rest", pair)] + 2),
                                         ("write", 0, PREP_AT[("low", pair)] + 3)):
                    casts_at.setdefault(PREP_FROM + step, []).append((what, part, pair))

            def task(name, arg, b):
                if name == "square":
                    act.wait_ge(centred, b + 1)
                    if not (isinstance(b, int) and b == 0):
                        act.wait_ge(gated_stored, (BEGUN + b) * 16)
                    nc.scalar.activation(sq[:], dev[:], ACT.Square).then_inc(squared, 1)
                if name == "late_gate":
                    act.wait_ge(late_full, 2 * arg + 1)
                    if arg >= 2:
                        act.wait_ge(late_hid, arg - 1)
                    nc.scalar.activation(late_silus[:, arg % 2], s_ps[:, 0], ACT.Silu).then_inc(late_silu, 1)
                if name == "tail_turn":
                    act.wait_ge(tail_turned, arg + 1)
                    nc.scalar.copy(tail_zT[:, arg], st_ps[:, arg // 2, arg % 2].rearrange("p (r t) -> p r t", r=4)).then_inc(tail_taken, 1)
                if name == "top":
                    act.wait_ge(top_found, b + 1)
                    nc.scalar.activation(gate[:, 0], top_now[:], ACT.Exp, scale=-1.0).then_inc(gate_exp, 1)
                if name not in MISC_TASKS:
                    return
                v = m.next()
                if name == "shared_gate":
                    if arg == 0:
                        act.wait_ge(gated_done, b + 1)
                    act.wait_ge(misc_full, v)
                    nc.scalar.activation(shared_silu, misc[:], ACT.Silu).then_inc(misc_done, 1)
                if name == "v":
                    act.wait_ge(misc_full, v)
                    if isinstance(b, int) and b == 0:
                        act.wait_ge(lam_ready, 1)
                    values = misc[:].rearrange("p (t g d) -> p t g d", t=QT, g=KV)
                    nc.scalar.copy(vo[:, :, :, 0:DV], values)
                    nc.scalar.activation(vo_lam[:, :, :, 0:DV], values, ACT.Copy, scale=neglam[:]).then_inc(misc_done, 1)
                elif name == "turn":
                    act.wait_ge(misc_full, v)
                    nc.scalar.copy(zT[:], misc[:].rearrange("p (r t) -> p r t", r=4)).then_inc(misc_done, 1)
                elif name == "retake":
                    act.wait_ge(misc_full, v)
                    nc.scalar.copy(x2T[:, :, arg * P:(arg + 1) * P], misc[:, 0:D].rearrange("p (c t) -> p c t", c=DC)).then_inc(misc_done, 1)

            def body(b, prep, post):
                if prep:
                    for k in range(4):
                        evacuate(b, k)
                for n in range(NSTEP):
                    qt, g, kt = STEPS[n]
                    v = st_at(b, n, prep)
                    act.wait_ge(st_full, v)
                    if n >= NP or (isinstance(b, int) and b > 0):
                        act.wait_ge(pv_step, b * NSTEP + n + 1 - NP)
                    nc.scalar.activation(probs[:, n % NP], st_ps[:, n % 2], ACT.Exp, scale=float(DH) ** -0.5).then_inc(st_done, 1)
                    if n >= 2:
                        finish_unit(b, n - 2)
                    for name, arg, back in tasks_at(n - 1, prep, post) if n else []:
                        task(name, arg, b - back)
                    for what, part, pair in casts_at.get(n, []) if prep else []:
                        if what == "cast":
                            cast(b + 1, part, pair)
                        else:
                            write_parts(b + 1, pair)
                for name, arg, back in tasks_at(NSTEP - 1, prep, post):
                    task(name, arg, b - back)
                finish_unit(b, NSTEP - 1)

            def finish_unit(b, n):
                qt, g, kt = STEPS[n]
                if kt != qt:
                    return
                u = qt * KV + g
                act.wait_ge(pv_step, b * NSTEP + n + 1)
                nc.scalar.copy(ol[:, u % 2], pv_ps[:]).then_inc(pv_done, 1)

            evacuate(None, 0)
            act.wait_ge(lam_summed, 1)
            nc.scalar.activation(lame[:], lams2[:], ACT.Exp).then_inc(lam_exp, 1)
            for k in range(1, 4):
                evacuate(None, k)
            for part, before_it, done in ((0, "odd", start_high), (1, "rest", start_mid)):
                for pair in START_CASTS:
                    act.wait_ge(*started((before_it, pair)))
                    nc.scalar.copy(parts[:, pair, :, part], raw_q(pair)).then_inc(done, 1)
            for pair in START_CASTS:
                act.wait_ge(*started(("low", pair)))
                store_parts(act, 0, pair, 1, 3)
            for name, arg, _ in HEAD:
                task(name, arg, 0)

            def boundary(b):
                for name, arg, back in BOUNDARY:
                    task(name, arg, b - back)

            body(0, True, False)
            with act.Fori(1, B - 1) as b:
                m.turn(MISC_HEAD, MISC_TURN, b - 1)
                boundary(b)
                body(b, True, True)
            m.turn(MISC_HEAD, MISC_TURN, B - 2)
            boundary(B - 1)
            body(B - 1, False, True)
            for name, arg, back in TAIL:
                task(name, arg, B - 1 - back)

            for fc in range(F // P):
                act.wait_ge(tail_full, 2 * fc + 1)
                if fc >= 2:
                    act.wait_ge(tail_hid, fc - 1)
                nc.scalar.activation(tail_silus[:, fc % 2], s_ps[:, 0], ACT.Silu).then_inc(tail_silu, 1)

            def take_tile(pair, r):
                act.wait_ge(turned, 2 * pair + r + 1)
                nc.scalar.copy(xeT[:, r], s_ps[:, 0, 0:D].rearrange("p (c t) -> p c t", c=DC)).then_inc(turned_done, 1)

            def make_silu(pair, r):
                act.wait_ge(up_full, 2 * pair + r + 1)
                nc.scalar.activation(silu[:, r], st_ps[:, r, 0, :], ACT.Silu).then_inc(silu_done, 1)

            def take_hidden(pair, r):
                act.wait_ge(hid_turned, 2 * pair + r + 1)
                nc.scalar.copy(hidT[:, r], s_ps[:, 1].rearrange("p (c t) -> p c t", c=F // P)).then_inc(hidT_done, 1)

            take_tile(0, 0)
            make_silu(0, 0)
            take_tile(0, 1)

            def routed_turn(k, r):
                i = 2 * k + r
                static = isinstance(i, int)
                take_hidden(k, r)
                if not (static and i + 1 >= NROUTE):
                    make_silu(k + r, 1 - r)
                if not (static and i + 2 >= NROUTE):
                    take_tile(k + 1, r)

            with act.Fori(0, LOOPED) as k:
                for r in range(2):
                    routed_turn(k, r)
            for i in range(2 * LOOPED, NROUTE):
                routed_turn(i // 2, i % 2)

            for g in range(4):
                act.wait_ge(final_shifted, g + 1)
                for t in range(g * 4, g * 4 + 4):
                    ins = nc.scalar.activation(x2[:, t], x2[:, t], ACT.Identity, scale=rstdf[:, t:t + 1], bias=shift[:, t:t + 1])
                ins.then_inc(final_done, 1)

        @block.gpsimd
        def _(pool):
            c = Chain(pool, pool_chain)

            def prep(b, op):
                what, pair = op
                base = (b - 1) * NPREP
                if what == "cos":
                    pool.wait_ge(st_done, prep_slot(b - 1, pair + 1))
                    if pair > 0:
                        pool.wait_ge(prep_done, base + PREP_DONE[("odd", pair - 1)])
                    elif not isinstance(b, int):
                        pool.wait_ge(prep_done, base)
                elif what == "even":
                    pool.wait_ge(prep_done, base + PREP_DONE[("sin", pair)])
                elif what == "rest":
                    pool.wait_ge(high_done, (b - 1) * 3 + pair + 1)
                elif what == "low":
                    pool.wait_ge(mid_done, (b - 1) * 3 + pair + 1)
                ins = prepare(nc.gpsimd, what, pair, rot)
                ins.then_inc(prep_done, 1)

            def task(name, arg, b):
                if name == "var":
                    pool.wait_ge(att_var, b + 1)
                    c.link(nc.gpsimd.tensor_tensor(head_rstd[:], head_var[:], halfneg[:].to_broadcast([P, H]), ALU.pow))
                    c.link(nc.gpsimd.tensor_tensor(scale_row[:], gw[:].rearrange("p (h d) -> p h d", h=H),
                                                   head_rstd[:].unsqueeze(2).to_broadcast([P, H, DV]), ALU.mult))
                    pool.sem_inc(scale_ready, 1)
                elif name == "affine":
                    z = dev[:, arg].rearrange("p h d -> p (h d)")
                    c.link(nc.gpsimd.tensor_tensor(z, z, scale_row[:].rearrange("p h d -> p (h d)"), ALU.mult))
                    nc.gpsimd.tensor_tensor(z, z, gb[:], ALU.add).then_inc(scaled, 1)
                elif name in ("project", "tail_project"):
                    pool.wait_ge(y_var, b * QT + arg + 1)
                    nc.gpsimd.tensor_tensor(rstd[:, arg % 2:arg % 2 + 1], mv[:, arg % 2, 1:2], halfneg[:], ALU.pow).then_inc(y_rstd, 1)

            def body(b, prep_next, post):
                for n in range(NSTEP):
                    qt, g, kt = STEPS[n]
                    if kt == qt:
                        pool.wait_ge(st_done, st_at(b, n, prep_next))
                        pool.sem_inc(exps_taken, 1)
                        e = probs[:, n % NP].rearrange("p s (r q) -> p (s r) q", r=4)
                        nc.gpsimd.affine_select(out=e, in_=e, compare_op=ALU.is_ge, fill=0.0, base=0,
                                                pattern=[[0, 8], [1, P]], channel_multiplier=-1).then_inc(diag_done, 1)
                    if n >= 1:
                        for name, arg, back in tasks_at(n - 1, prep_next, post):
                            task(name, arg, b - back)
                    if prep_next and 0 <= n - PREP_FROM < NPREP:
                        prep(b + 1, PREP[n - PREP_FROM])
                for name, arg, back in tasks_at(NSTEP - 1, prep_next, post):
                    task(name, arg, b - back)

            c.link(nc.gpsimd.memset(halfneg[:], -0.5))
            pool.wait_ge(consts_loaded, NCONST * 16)
            c.link(nc.gpsimd.tensor_scalar(gw[:], gw[:], 1.0 - LAMBDA_INIT, None, ALU.mult))
            c.link(nc.gpsimd.tensor_scalar(gb[:], gb[:], 1.0 - LAMBDA_INIT, None, ALU.mult))
            start_prepare(pool, nc.gpsimd, START_POOL, start_pool, rot)
            body(0, True, False)
            head = c.n
            with pool.Fori(1, B - 1) as b:
                c.turn(head, POOL_TURN, b - 1)
                body(b, True, True)
            c.turn(head, POOL_TURN, B - 2)
            body(B - 1, False, True)
            for name, arg, back in TAIL:
                if name != "affine":
                    task(name, arg, B - 1 - back)

            pool.wait_ge(zeroed, 16)
            pool.wait_ge(slots_done, 1)
            pool.wait_ge(gated_loaded, (B - 1) * 16)
            pool.wait_ge(gated_done, B)
            for t in range(NTOK):
                nc.gpsimd.indirect_dma_start(out=sorted_rows, out_offset=bass.IndirectOffsetOnAxis(ap=slot[:, t:t + 1], axis=0),
                                             in_=gated[t // QT][:, t % QT], in_offset=None).then_inc(scattered, 16)
            pool.wait_ge(tokens_ready, 32)
            for t in range(NTOK):
                nc.gpsimd.indirect_dma_start(out=slot_tokens, out_offset=bass.IndirectOffsetOnAxis(ap=slot[:, t:t + 1], axis=0),
                                             in_=tokens[:, t:t + 1], in_offset=None).then_inc(tokens_scattered, 16)
            pool.wait_ge(rows_of_loaded, 16)
            for i in range(NROUTE):
                pool.wait_ge(down_done, BEGUN + i + 1)
                nc.gpsimd.indirect_dma_start(out=token_rows, out_offset=bass.IndirectOffsetOnAxis(ap=rows_of[:, i:i + 1], axis=0),
                                             in_=yo[:, i % 2], in_offset=None).then_inc(routed_stored[i % 2], 16)
            def final_rstd_of(g):
                pool.wait_ge(final_var, g + 1)
                nc.gpsimd.tensor_tensor(rstdf[:, g * 4:(g + 1) * 4], mvf[:, g * 4:(g + 1) * 4, 1], halfneg[:].to_broadcast([P, 4]),
                                        ALU.pow).then_inc(final_rstd, 1)

            for g in (2, 3):
                pool.wait_ge(gathered[g], 16)
                pool.wait_ge(late_added, QT)
                pool.wait_ge(tail_added, QT)
                rows = slice(g * 4, (g + 1) * 4)
                nc.gpsimd.tensor_tensor(x2[:, rows], x2[:, rows], gated[g], ALU.add).then_inc(pool_added, 1)
                if g == 2:
                    final_rstd_of(0)
            for g in range(1, 4):
                final_rstd_of(g)

        @block.vector
        def _(dve):
            c = Chain(dve, dve_chain)
            m = Misc()
            bank = Misc()

            def maximum(qt, i):
                v = bank.next()
                rows = banks(qt)[i]
                dve.wait_ge(bank_full, v)
                w = (qt + 1) * P
                nc.vector.tensor_reduce(out=mneg[:, qt, rows[0]:rows[-1] + 1],
                                        in_=s_ps[:, i % 2, 0:len(rows) * w].rearrange("p (r k) -> p r k", r=len(rows)),
                                        axis=AX.X, op=ALU.max, negate=True).then_inc(bank_done, 1)
                if i == NBANK[qt] - 1:
                    dve.wait_ge(bank_done, v)
                    c.link(nc.vector.tensor_copy(msplit[:, qt % 2, 0:HS], mneg[:, qt]))
                    nc.vector.tensor_tensor(msplit[:, qt % 2, HS:2 * HS], mneg[:, qt], msplit[:, qt % 2, 0:HS],
                                            ALU.subtract).then_inc(split_done, 1)

            def task(name, arg, b, ahead=False, last_batch=False):
                if name == "banks":
                    for i in range(arg[1], arg[2]):
                        maximum(arg[0], i)
                if name in MISC_TASKS:
                    v = m.next()
                if name == "mt":
                    dve.wait_ge(misc_full, v)
                    if not (isinstance(b, int) and b == 0 and arg < 2):
                        dve.wait_ge(max_stored, (b * QT + arg - 1) * 16)
                    nc.vector.tensor_copy(mT[:, arg % 2, :], misc[0:2 * HS, 0:P // 2].bitcast(BF16)).then_inc(misc_done, 1)
                elif name == "norm":
                    qt, g = divmod(arg, KV)
                    dve.wait_ge(misc_full, v)
                    t = misc[:].rearrange("p (r s d) -> p r s d", r=4, s=2)
                    c.link(nc.vector.reciprocal(rl[:], t[:, :, :, DV]))
                    nc.vector.tensor_tensor(o12[:], t[:, :, :, 0:DV], rl[:].unsqueeze(3).to_broadcast([P, 4, 2, DV]), ALU.mult).then_inc(misc_done, 1)
                    dve.wait_ge(misc_done, v)
                    c.link(nc.vector.tensor_tensor(att[:, qt, g * 4:g * 4 + 4, :], o12[:, :, 0], o12[:, :, 1], ALU.add))
                elif name == "sum":
                    nc.vector.tensor_reduce(out=head_tot[:], in_=att[:].rearrange("p q h d -> p h q d"), axis=AX.XY,
                                            op=ALU.add).then_inc(summed, 1)
                elif name == "mean":
                    dve.wait_ge(misc_full, v)
                    mean = misc[:, 0:H].unsqueeze(2).to_broadcast([P, H, DV])
                    for qt in range(QT):
                        ins = nc.vector.tensor_tensor(dev[:, qt], att[:, qt], mean, ALU.subtract)
                        if qt == QT - 2:
                            c.link(ins)
                        if qt == QT - 1:
                            ins.then_inc(misc_done, 1)
                    dve.wait_ge(misc_done, v)
                    dve.sem_inc(centred, 1)
                elif name == "sum_squares":
                    dve.wait_ge(squared, b + 1)
                    nc.vector.tensor_reduce(out=head_sq[:], in_=sq[:].rearrange("p q h d -> p h q d"), axis=AX.XY,
                                            op=ALU.add).then_inc(squares_summed, 1)
                elif name == "var":
                    dve.wait_ge(misc_full, v)
                    nc.vector.tensor_scalar(head_var[:], misc[:, 0:H], EPS, None, ALU.add).then_inc(misc_done, 1)
                    dve.wait_ge(misc_done, v)
                    dve.sem_inc(att_var, 1)
                elif name in ("project", "tail_project"):
                    dve.wait_ge(misc_full, v)
                    if arg == 0:
                        dve.wait_ge(xres_loaded, (b + 1) * 16)
                    nc.vector.tensor_tensor(y[:, arg % 2], misc[:, 0:D], xres[:, arg], ALU.add).then_inc(misc_done, 1)
                    dve.wait_ge(misc_done, v)
                    c.link(nc.vector.bn_stats(st6[:], y[:, arg % 2]))
                    dve.sem_inc(stats_taken, 1)
                    c.link(nc.vector.bn_aggr(mv[:, arg % 2], st6[:]))
                    nc.vector.tensor_scalar(mv[:, arg % 2, 1:2], mv[:, arg % 2, 1:2], EPS, None, ALU.add).then_inc(y_var, 1)
                elif name == "x2":
                    dve.wait_ge(y_rstd, b * QT + arg + 1)
                    nc.vector.tensor_scalar(x2[:, bass.ds(b * QT + arg, 1), :], y[:, arg % 2:arg % 2 + 1], mv[:, arg % 2, 0:1],
                                            rstd[:, arg % 2:arg % 2 + 1], ALU.subtract, ALU.mult).then_inc(x2_kept, 1)
                    dve.wait_ge(x2_kept, b * QT + arg + 1)
                    nc.vector.tensor_scalar(y[:, arg % 2], y[:, arg % 2], mv[:, arg % 2, 0:1],
                                            rstd[:, arg % 2:arg % 2 + 1], ALU.subtract, ALU.mult).then_inc(x2_done, 1)
                elif name == "logits":
                    dve.wait_ge(misc_full, v)
                    nc.vector.tensor_copy(logits_now[:, arg], misc[:, 0:E])
                    nc.vector.tensor_copy(logits[:, bass.ds(b * QT + arg, 1), :], misc[:, 0:E].unsqueeze(1)).then_inc(misc_done, 1)
                elif name == "late_up":
                    dve.wait_ge(late_full, 2 * arg + 2)
                    dve.wait_ge(late_silu, arg + 1)
                    nc.vector.tensor_tensor(late_hidT[:, arg], late_silus[:, arg % 2], s_ps[:, 1], ALU.mult).then_inc(late_hid, 1)
                elif name == "late_down":
                    dve.wait_ge(late_full, 2 * (F // P) + arg + 1)
                    rows = x2[:, b * QT + arg]
                    nc.vector.tensor_tensor(rows, rows, s_ps[:, arg % 2, 0:D], ALU.add).then_inc(late_added, 1)
                elif name == "affine" and last_batch:
                    if arg == 0:
                        dve.wait_ge(scale_ready, B)
                    z = dev[:, arg].rearrange("p h d -> p (h d)")
                    c.link(nc.vector.tensor_tensor(z, z, scale_row[:].rearrange("p h d -> p (h d)"), ALU.mult))
                    nc.vector.tensor_tensor(z, z, gb[:], ALU.add).then_inc(scaled, 1)
                elif name == "shared_up":
                    dve.wait_ge(misc_full, v)
                    nc.vector.tensor_tensor(shared_hidT[:, arg], shared_silu, misc[:], ALU.mult).then_inc(misc_done, 1)
                elif name == "shared_down":
                    dve.wait_ge(misc_full, v)
                    rows = x2[:, bass.ds(b * QT + arg, 1), :]
                    nc.vector.tensor_tensor(rows, rows, misc[:, 0:D].unsqueeze(1), ALU.add).then_inc(misc_done, 1)
                elif name == "top":
                    dve.wait_ge(misc_done, m.turns + m.n)
                    nc.vector.tensor_reduce(out=top_now[:], in_=logits_now[:], axis=AX.X, op=ALU.max).then_inc(top_found, 1)
                elif name == "gate":
                    dve.wait_ge(gate_exp, b + 1)
                    c.link(nc.vector.tensor_scalar(gate[:, 0], gate[:, 0], 1.0, None, ALU.add))
                    c.link(nc.vector.reciprocal(gate[:, 1], gate[:, 0]))
                    if ahead:
                        dve.wait_ge(prep_done, (b + 2) * NPREP)
                    nc.vector.tensor_tensor(gated_out[:], x2[:, bass.ds(b * QT, QT), :], gate[:, 1].unsqueeze(2).to_broadcast([P, QT, D]),
                                            ALU.mult).then_inc(gated_done, 1)

            def body(b, ahead, post):
                for n in range(NSTEP):
                    for qt, i, back in BANKS_AT.get(n, []):
                        if back == 0 or ahead:
                            maximum(qt, i)
                    for name, arg, back in tasks_at(n, ahead, post):
                        task(name, arg, b - back, ahead)

            def boundary(b):
                for name, arg, back in BOUNDARY:
                    task(name, arg, b - back)

            for begun in (x2_done, hid_done, hidT_done, down_done):
                dve.sem_inc(begun, BEGUN)
            dve.sem_inc(gated_stored, BEGUN * 16)
            nc.vector.memset(zero_row, 0.0).then_inc(zero_ready, 1)
            c.link(nc.vector.memset(onesb[:], 1.0))
            c.link(nc.vector.memset(msplit[:, :, 2 * HS:P], 0.0))
            c.link(nc.vector.memset(averager[:], 1.0 / (T * DV)))
            c.link(nc.vector.memset(vo[:, :, :, DV:2 * DV], 1.0))
            c.link(nc.vector.memset(vo_lam[:, :, :, DV:2 * DV], 1.0))
            c.link(nc.vector.memset(k_stack[KROWS:P], 1.0))
            c.link(nc.vector.memset(k_near[KROWS:P], 1.0))
            dve.wait_ge(consts_loaded, NCONST * 16)
            nc.vector.tensor_copy(identb[:], ident[:]).then_inc(consts_ready, 1)
            nc.vector.tensor_copy(mask[:], mask_f[:]).then_inc(consts_ready, 1)
            c.link(nc.vector.tensor_scalar(before[:], mask_f[:], 0.0, None, ALU.is_lt))
            c.link(nc.vector.tensor_tensor(lamp[:], lamv[:, 0:4:2, :], lamv[:, 1:4:2, :], ALU.mult))
            nc.vector.tensor_reduce(out=lams2[:], in_=lamp[:], axis=AX.X, op=ALU.add).then_inc(lam_summed, 1)
            dve.wait_ge(lam_exp, 1)
            c.link(nc.vector.tensor_tensor(neglam[:], lame[:, 1:2], lame[:, 0:1], ALU.subtract))
            nc.vector.tensor_scalar(neglam[:], neglam[:], -LAMBDA_INIT, None, ALU.add).then_inc(lam_ready, 1)
            start_prepare(dve, nc.vector, START_DVE, start_dve, att[:].rearrange("p q h d -> p (q h d)").rearrange("p (a h t) -> p a h t", a=2, h=2))
            for name, arg, _ in HEAD:
                task(name, arg, 0)
            body(0, True, False)
            head = c.n
            dve.wait_ge(zeroed, 16)
            with dve.Fori(1, B - 1) as b:
                m.turn(MISC_HEAD, MISC_TURN, b - 1)
                bank.turn(BANK_HEAD, BANK_TURN, b - 1)
                c.turn(head, DVE_TURN, b - 1)
                boundary(b)
                body(b, True, True)
            m.turn(MISC_HEAD, MISC_TURN, B - 2)
            bank.turn(BANK_HEAD, BANK_TURN, B - 2)
            c.turn(head, DVE_TURN, B - 2)
            boundary(B - 1)
            body(B - 1, False, True)
            for name, arg, back in TAIL:
                task(name, arg, B - 1 - back, last_batch=True)

            dve.wait_ge(misc_done, m.turns + m.n)
            dve.wait_ge(x2_kept, NTOK)
            tok = [P, NTOK, E]
            expert = counts[:, 0:E].unsqueeze(1).to_broadcast(tok)
            c.link(nc.vector.tensor_reduce(out=top[:], in_=logits[:], axis=AX.X, op=ALU.max))
            c.link(nc.vector.tensor_tensor(is_top[:], logits[:], top[:].unsqueeze(2).to_broadcast(tok), ALU.is_equal))
            c.link(nc.vector.tensor_scalar(is_top[:], is_top[:], -float(E), float(E), ALU.mult, ALU.add))
            c.link(nc.vector.tensor_tensor(choice[:], is_top[:], expert, ALU.add))
            c.link(nc.vector.tensor_reduce(out=first[:], in_=choice[:], axis=AX.X, op=ALU.min))
            picked = first[:].unsqueeze(2).to_broadcast(tok)
            nc.vector.tensor_tensor(chosenb[:], expert, picked, ALU.is_equal).then_inc(chosen_done, 1)
            c.link(nc.vector.tensor_tensor(chosen[:], expert, picked, ALU.is_equal))
            dve.wait_ge(ranked, 1)
            rank = misc[:, 0:NTOK * E].rearrange("p (n e) -> p n e", e=E)
            c.link(nc.vector.tensor_copy(scan[:, 0], misc[:, NTOK * E:2 * NTOK * E].rearrange("p (n e) -> p n e", e=E)))
            a = 0
            for d in (1, 2, 4, 8):
                nc.vector.tensor_copy(scan[:, 1 - a, 0:d], scan[:, a, 0:d])
                c.link(nc.vector.tensor_tensor(scan[:, 1 - a, d:], scan[:, a, d:], scan[:, a, 0:NTOK - d], ALU.add))
                a = 1 - a
            cmp = [P, E, NTOK]
            c.link(nc.vector.tensor_tensor(tiles_cmp[:], scan[:, a, NTOK - 1].unsqueeze(2).to_broadcast(cmp),
                                           counts[:, E:E + NTOK].unsqueeze(1).to_broadcast(cmp), ALU.is_gt))
            c.link(nc.vector.tensor_reduce(out=tiles_n[:], in_=tiles_cmp[:], axis=AX.X, op=ALU.add))
            c.link(nc.vector.tensor_copy(tiles_cum[:, 0], tiles_n[:]))
            t = 0
            for d in (1, 2, 4):
                nc.vector.tensor_copy(tiles_cum[:, 1 - t, 0:d], tiles_cum[:, t, 0:d])
                c.link(nc.vector.tensor_tensor(tiles_cum[:, 1 - t, d:], tiles_cum[:, t, d:], tiles_cum[:, t, 0:E - d], ALU.add))
                t = 1 - t
            c.link(nc.vector.tensor_tensor(first_slot[:], tiles_cum[:, t], tiles_n[:], ALU.subtract))
            c.link(nc.vector.tensor_scalar(first_slot[:], first_slot[:], float(P), None, ALU.mult))
            c.link(nc.vector.tensor_tensor(place_f[:], rank, scan[:, a], ALU.add))
            c.link(nc.vector.tensor_tensor(scan[:, 1 - a], misc[:, NTOK * E:2 * NTOK * E].rearrange("p (n e) -> p n e", e=E),
                                           first_slot[:].unsqueeze(1).to_broadcast(tok), ALU.subtract))
            c.link(nc.vector.tensor_tensor(place_f[:], place_f[:], scan[:, 1 - a], ALU.subtract))
            c.link(nc.vector.tensor_tensor(place_f[:], place_f[:], chosen[:], ALU.mult))
            c.link(nc.vector.tensor_reduce(out=slot_f[:], in_=place_f[:], axis=AX.X, op=ALU.add))
            nc.vector.tensor_copy(slot[:], slot_f[:]).then_inc(slots_done, 1)
            own = [P, NROUTE, E]
            c.link(nc.vector.tensor_tensor(owner_cmp[:], tiles_cum[:, t].unsqueeze(1).to_broadcast(own),
                                           counts[:, E + NTOK:].unsqueeze(2).to_broadcast(own), ALU.is_le))
            c.link(nc.vector.tensor_reduce(out=owner_f[:], in_=owner_cmp[:], axis=AX.X, op=ALU.add))
            nc.vector.tensor_scalar(owner[:], owner_f[:], float(E - 1), None, ALU.min).then_inc(owners_done, 1)

            for fc in range(F // P):
                dve.wait_ge(tail_full, 2 * fc + 2)
                dve.wait_ge(tail_silu, fc + 1)
                nc.vector.tensor_tensor(shared_hidT[:, fc], tail_silus[:, fc % 2], s_ps[:, 1], ALU.mult).then_inc(tail_hid, 1)
            for t in range(QT):
                dve.wait_ge(tail_full, 2 * (F // P) + t + 1)
                rows = x2[:, (B - 1) * QT + t]
                nc.vector.tensor_tensor(rows, rows, s_ps[:, t % 2, 0:D], ALU.add).then_inc(tail_added, 1)

            def make_hidden(pair, r):
                i = 2 * pair + r
                dve.wait_ge(silu_done, i + 1)
                nc.vector.tensor_tensor(hid[:, r], silu[:, r], st_ps[:, r, 1, :], ALU.mult).then_inc(hid_done, 1)

            def take_routed(pair, r):
                i = 2 * pair + r
                dve.wait_ge(down_full, i + 1)
                if not (isinstance(pair, int) and pair == 0):
                    dve.wait_ge(routed_stored[r], pair * 16)
                nc.vector.tensor_copy(yo[:, r], pv_ps[:, 0:D]).then_inc(down_done, 1)

            def routed_turn(k, r):
                i = 2 * k + r
                if not (isinstance(i, int) and i + 1 >= NROUTE):
                    make_hidden(k + r, 1 - r)
                take_routed(k, r)

            make_hidden(0, 0)
            for r in range(2):
                routed_turn(0, r)
            with dve.Fori(1, LOOPED) as k:
                for r in range(2):
                    routed_turn(k, r)
            for i in range(2 * LOOPED, NROUTE):
                routed_turn(i // 2, i % 2)

            def final_shift(g):
                dve.wait_ge(final_rstd, g + 1)
                rows = slice(g * 4, (g + 1) * 4)
                c.link(nc.vector.tensor_scalar(shift[:, rows], mvf[:, rows, 0], -1.0, None, ALU.mult))
                nc.vector.tensor_tensor(shift[:, rows], shift[:, rows], rstdf[:, rows], ALU.mult).then_inc(final_shifted, 1)

            for g in range(4):
                dve.wait_ge(gathered[g], 16)
                if g == 0:
                    dve.wait_ge(tail_added, QT)
                rows = slice(g * 4, (g + 1) * 4)
                if g < 2:
                    c.link(nc.vector.tensor_tensor(x2[:, rows], x2[:, rows], gated[g], ALU.add))
                else:
                    dve.wait_ge(pool_added, g - 1)
                for t in range(g * 4, g * 4 + 4):
                    ins = nc.vector.bn_stats(st6f[:, t], x2[:, t])
                c.link(ins)
                for t in range(g * 4, g * 4 + 4):
                    ins = nc.vector.bn_aggr(mvf[:, t], st6f[:, t])
                c.link(ins)
                nc.vector.tensor_scalar(mvf[:, rows, 1], mvf[:, rows, 1], EPS, None, ALU.add).then_inc(final_var, 1)
                if g >= 1:
                    final_shift(g - 1)
            final_shift(3)


def kernel(**inputs):
    import concourse.bacc as bacc
    from concourse.bass_utils import run_bass_kernel_spmd as run

    a = {k.replace("L0_", ""): np.ascontiguousarray(v) for k, v in inputs.items()}
    wq = a["attn_Wq"].reshape(D, 2, 2, 4, 2, 8, 2).transpose(0, 1, 6, 5, 2, 4, 3).reshape(D, 2, 2, P)
    wk = a["attn_Wk"].reshape(D, KV, 2, 8, 2).transpose(0, 4, 3, 1, 2).reshape(D, 2, 8, 2 * KV)
    wk = np.concatenate([wk, wk], axis=3).reshape(D, 1, 2, P)
    inv = (1.0 / np.float32(10000.0) ** (np.arange(0, DH, 2, dtype=np.float32) / np.float32(DH))).astype(np.float32)
    angle = (np.arange(T, dtype=np.float32)[:, None] * inv[None, :]).astype(np.float32)
    cos = np.repeat(np.cos(angle.astype(np.float64)).T.astype(np.float32), 16, axis=0)
    sin = np.repeat(np.sin(angle.astype(np.float64)).T.astype(np.float32), 16, axis=0)
    i = np.arange(P)
    arrays = {
        "x": a["attn_x"], "wqk": np.ascontiguousarray(np.concatenate([wq, wk], axis=1)), "wv": a["attn_Wv"], "wo": a["attn_Wo"],
        "lq1": a["attn_lambda_q1"], "lk1": a["attn_lambda_k1"], "lq2": a["attn_lambda_q2"], "lk2": a["attn_lambda_k2"],
        "gnw": a["attn_gn_w"], "gnb": a["attn_gn_b"], "cos_d": np.ascontiguousarray(cos), "sin_d": np.ascontiguousarray(sin),
        "ident_d": np.eye(P, dtype=np.float32), "mask_d": np.where(i[None, :] > i[:, None], NEG, 0.0).astype(np.float32),
        "router": np.ascontiguousarray(a["ffn_router_w"].T), "w_up": a["ffn_w_gate_up"], "w_down": a["ffn_w_down"],
        "s_up": a["ffn_shared_gate_up"], "s_down": a["ffn_shared_down"],
        "tokens_d": (np.arange(NTOK)[None, :] * P + i[:, None]).astype(np.int32),
        "spare_d": (NTOK * P + np.arange(NROUTE * P))[:, None].astype(np.int32),
        "counts_d": np.concatenate([np.arange(E), np.arange(NTOK) * P, np.arange(NROUTE)]).astype(np.float32),
    }
    nc = bacc.Bacc("TRN2", target_bir_lowering=False, num_devices=1)
    t = {n: nc.dram_tensor(n + "_in", v.shape, mybir.dt.from_np(v.dtype), kind="ExternalInput").ap() for n, v in arrays.items()}
    out = nc.dram_tensor("out", (B, T, D), F32, kind="ExternalOutput").ap()
    build(nc, t["x"], t["wqk"], t["wv"], t["wo"], [t["lq1"], t["lk1"], t["lq2"], t["lk2"]], t["gnw"], t["gnb"],
          t["cos_d"], t["sin_d"], t["ident_d"], t["mask_d"],
          t["router"], t["w_up"], t["w_down"], t["s_up"], t["s_down"], t["counts_d"], t["tokens_d"], t["spare_d"], out)
    r = run(nc, [{n + "_in": v for n, v in arrays.items()}], core_ids=[0])
    return r.results[0]["out"]
```
